# Optimizing a Trainium2 kernel written in Bass

```python
import numpy as np
import jax
import jax.numpy as jnp

def _softmax(x, axis=-1):
    return jax.nn.softmax(x, axis=axis)

def _gelu(x):
    return jax.nn.gelu(x, approximate=True)

def _silu(x):
    return jax.nn.silu(x)

def _sigmoid(x):
    return jax.nn.sigmoid(x)

def _layernorm(x, axis=-1, eps=1e-05):
    m = jnp.mean(x, axis=axis, keepdims=True)
    v = jnp.var(x, axis=axis, keepdims=True)
    return (x - m) / jnp.sqrt(v + eps)

def _scatter_add(tgt, idx, src, axis=0):
    return tgt.at[idx].add(src)

def _segment_sum(src, seg, n):
    return jax.ops.segment_sum(src, seg, n)
kernel_name = 'mk_gnn_preln_d4_gnn_r32_98f1df'

def setup_inputs(seed: int=0):
    np.random.seed(seed)
    _w = jnp.asarray

    def _rec_inputs():
        import jax
        import jax.numpy as jnp
        _gk = jax.random.key(seed)
        x = -0.0005121 + 1.001 * jax.random.normal(jax.random.fold_in(_gk, 1), (50000, 64), jnp.float32)
        src = jax.random.randint(jax.random.fold_in(_gk, 2), (50000,), 0, 50000, jnp.int32)
        dst = jax.random.randint(jax.random.fold_in(_gk, 3), (50000,), 0, 50000, jnp.int32)
        _o = jnp.argsort(dst, stable=True)
        src = src[_o]
        dst = dst[_o]
        edge_attr_64 = -5.3897e-05 + 0.999841 * jax.random.normal(jax.random.fold_in(_gk, 13), (50000, 64), jnp.float32)
        edge_weight = jax.random.uniform(jax.random.fold_in(_gk, 15), (50000,), jnp.float32, 0.0, 4.99999)
        edge_weight1 = -0.000414295 + 0.999828 * jax.random.normal(jax.random.fold_in(_gk, 16), (50000, 1), jnp.float32)
        return (x, src, dst, edge_attr_64, edge_weight, edge_weight1)
    x, src, dst, edge_attr_64, edge_weight, edge_weight1 = _rec_inputs()

    def _L0_gnn_setup():
        import jax, jax.numpy as jnp
        import numpy as np
        N_NODES = 50000
        N_EDGES = 12500
        C = 64
        EDGE_DIM = 64
        Z_DIM = 2 * C + EDGE_DIM
        SIGMA = 3.0
        key = jax.random.key(seed)
        ks = jax.random.split(key, 6)
        x = jax.random.normal(ks[0], (N_NODES, C), dtype=jnp.float32)
        edge_attr = jax.random.normal(ks[1], (N_EDGES, EDGE_DIM), dtype=jnp.float32)
        distance = jax.random.uniform(ks[2], (N_EDGES,), dtype=jnp.float32) * 5.0
        W_f = jax.random.normal(ks[3], (Z_DIM, C), dtype=jnp.float32) * (1.0 / np.sqrt(Z_DIM))
        b_f = jnp.zeros((C,), dtype=jnp.float32)
        W_s = jax.random.normal(ks[4], (Z_DIM, C), dtype=jnp.float32) * (1.0 / np.sqrt(Z_DIM))
        b_s = jnp.zeros((C,), dtype=jnp.float32)
        edge_index = jax.random.randint(ks[5], (2, N_EDGES), 0, N_NODES, dtype=jnp.int64)
        batch = jnp.zeros((N_NODES,), dtype=jnp.int64)
        return {'x': x, 'edge_attr': edge_attr, 'distance': distance, 'W_f': W_f, 'b_f': b_f, 'W_s': W_s, 'b_s': b_s, 'edge_index': edge_index, 'batch': batch}
    _L0_gnn_all = _L0_gnn_setup()
    _L0_gnn_in = {k: v for k, v in _L0_gnn_all.items() if k in ('W_f', 'b_f', 'W_s', 'b_s')}
    del _L0_gnn_all

    def _L1_gnn_setup():
        import jax, jax.numpy as jnp
        import numpy as np
        N_NODES = 3125
        N_EDGES = 50000
        IN_FEATS = 64
        OUT_FEATS = 64
        EDGE_FEATS = 1
        key = jax.random.key(seed)
        ks = jax.random.split(key, 6)
        h = jax.random.normal(ks[0], (N_NODES, IN_FEATS), dtype=jnp.float32)
        e = jax.random.normal(ks[1], (N_EDGES, EDGE_FEATS), dtype=jnp.float32)
        src = jax.random.randint(ks[2], (N_EDGES,), 0, N_NODES, dtype=jnp.int32)
        dst = jax.random.randint(ks[3], (N_EDGES,), 0, N_NODES, dtype=jnp.int32)
        cat_dim = 2 * IN_FEATS + EDGE_FEATS
        W1 = jax.random.normal(ks[4], (cat_dim, OUT_FEATS), dtype=jnp.float32) / np.sqrt(cat_dim)
        b1 = jnp.zeros((OUT_FEATS,), dtype=jnp.float32)
        W2 = jax.random.normal(ks[5], (OUT_FEATS, OUT_FEATS), dtype=jnp.float32) / np.sqrt(OUT_FEATS)
        b2 = jnp.zeros((OUT_FEATS,), dtype=jnp.float32)
        return {'h': h, 'e': e, 'src': src, 'dst': dst, 'W1': W1, 'b1': b1, 'W2': W2, 'b2': b2}
    _L1_gnn_all = _L1_gnn_setup()
    _L1_gnn_in = {k: v for k, v in _L1_gnn_all.items() if k in ('W1', 'b1', 'W2', 'b2')}
    del _L1_gnn_all

    def _L2_gnn_setup():
        import jax, jax.numpy as jnp
        import numpy as np
        H = 5
        NEG_SLOPE = 0.2
        N_NODES = 50000
        N_EDGES = 12500
        IN_CH = 64
        OUT_CH = 64

        def gatv2_layer(x, src, dst, Wl, bl, Wr, br, att, bias, n_nodes):
            C = att.shape[1]
            xl = (x @ Wl + bl).reshape(n_nodes, H, C)
            xr = (x @ Wr + br).reshape(n_nodes, H, C)
            e = jax.nn.leaky_relu(xl[src] + xr[dst], NEG_SLOPE)
            alpha = jnp.einsum('ehc,hc->eh', e, att)
            m = jax.ops.segment_max(alpha, dst, num_segments=n_nodes)
            m = jnp.where(jnp.isfinite(m), m, 0.0)
            a = jnp.exp(alpha - m[dst])
            denom = jax.ops.segment_sum(a, dst, num_segments=n_nodes)
            a = a / (denom[dst] + 1e-16)
            out = jax.ops.segment_sum(a[:, :, None] * xl[src], dst, num_segments=n_nodes)
            return out.mean(axis=1) + bias
        key = jax.random.key(seed)
        ks = jax.random.split(key, 17)
        s = 0.05
        inp = {'x': jax.random.normal(ks[0], (N_NODES, IN_CH), jnp.float32), 'edge_index': jax.random.randint(ks[1], (2, N_EDGES), 0, N_NODES, jnp.int64), 'W1l': jax.random.normal(ks[2], (IN_CH, H * IN_CH), jnp.float32) * s, 'b1l': jnp.zeros((H * IN_CH,), jnp.float32), 'W1r': jax.random.normal(ks[3], (IN_CH, H * IN_CH), jnp.float32) * s, 'b1r': jnp.zeros((H * IN_CH,), jnp.float32), 'att1': jax.random.normal(ks[4], (H, IN_CH), jnp.float32) * s, 'bias1': jnp.zeros((IN_CH,), jnp.float32), 'W2l': jax.random.normal(ks[5], (IN_CH, H * OUT_CH), jnp.float32) * s, 'b2l': jnp.zeros((H * OUT_CH,), jnp.float32), 'W2r': jax.random.normal(ks[6], (IN_CH, H * OUT_CH), jnp.float32) * s, 'b2r': jnp.zeros((H * OUT_CH,), jnp.float32), 'att2': jax.random.normal(ks[7], (H, OUT_CH), jnp.float32) * s, 'bias2': jnp.zeros((OUT_CH,), jnp.float32), 'Wfc': jax.random.normal(ks[8], (OUT_CH, OUT_CH), jnp.float32) * s, 'bfc': jnp.zeros((OUT_CH,), jnp.float32)}
        return inp
    _L2_gnn_all = _L2_gnn_setup()
    _L2_gnn_in = {k: v for k, v in _L2_gnn_all.items() if k in ('W1l', 'b1l', 'W1r', 'b1r', 'att1', 'bias1', 'W2l', 'b2l', 'W2r', 'b2r', 'att2', 'bias2', 'Wfc', 'bfc')}
    del _L2_gnn_all

    def _L3_gnn_setup():
        import jax, jax.numpy as jnp
        import numpy as np
        N_NODES = 3125
        N_EDGES = 50000
        D = 64
        BN_EPS = 1e-05
        key = jax.random.key(seed)
        ks = jax.random.split(key, 6)
        feature = jax.random.normal(ks[0], (N_NODES, D), dtype=jnp.float32)
        src = jax.random.randint(ks[1], (N_EDGES,), 0, N_NODES, dtype=jnp.int32)
        dst = jax.random.randint(ks[2], (N_EDGES,), 0, N_NODES, dtype=jnp.int32)
        W = jax.random.normal(ks[3], (D, D), dtype=jnp.float32) / np.sqrt(D)
        b = jax.random.normal(ks[4], (D,), dtype=jnp.float32) * 0.01
        gamma = jnp.ones((D,), dtype=jnp.float32)
        beta = jnp.zeros((D,), dtype=jnp.float32)
        return {'feature': feature, 'W': W, 'b': b, 'gamma': gamma, 'beta': beta, 'src': src, 'dst': dst}
    _L3_gnn_all = _L3_gnn_setup()
    _L3_gnn_in = {k: v for k, v in _L3_gnn_all.items() if k in ('W', 'b', 'gamma', 'beta')}
    del _L3_gnn_all
    return {'x': x, 'src': src, 'dst': dst, 'edge_attr_64': edge_attr_64, 'edge_weight': edge_weight, 'edge_weight1': edge_weight1, 'L0_gnn_W_f': _L0_gnn_in['W_f'], 'L0_gnn_b_f': _L0_gnn_in['b_f'], 'L0_gnn_W_s': _L0_gnn_in['W_s'], 'L0_gnn_b_s': _L0_gnn_in['b_s'], 'L1_gnn_W1': _L1_gnn_in['W1'], 'L1_gnn_b1': _L1_gnn_in['b1'], 'L1_gnn_W2': _L1_gnn_in['W2'], 'L1_gnn_b2': _L1_gnn_in['b2'], 'L2_gnn_W1l': _L2_gnn_in['W1l'], 'L2_gnn_b1l': _L2_gnn_in['b1l'], 'L2_gnn_W1r': _L2_gnn_in['W1r'], 'L2_gnn_b1r': _L2_gnn_in['b1r'], 'L2_gnn_att1': _L2_gnn_in['att1'], 'L2_gnn_bias1': _L2_gnn_in['bias1'], 'L2_gnn_W2l': _L2_gnn_in['W2l'], 'L2_gnn_b2l': _L2_gnn_in['b2l'], 'L2_gnn_W2r': _L2_gnn_in['W2r'], 'L2_gnn_b2r': _L2_gnn_in['b2r'], 'L2_gnn_att2': _L2_gnn_in['att2'], 'L2_gnn_bias2': _L2_gnn_in['bias2'], 'L2_gnn_Wfc': _L2_gnn_in['Wfc'], 'L2_gnn_bfc': _L2_gnn_in['bfc'], 'L3_gnn_W': _L3_gnn_in['W'], 'L3_gnn_b': _L3_gnn_in['b'], 'L3_gnn_gamma': _L3_gnn_in['gamma'], 'L3_gnn_beta': _L3_gnn_in['beta']}

def reference(x, src, dst, edge_attr_64, edge_weight, edge_weight1, L0_gnn_W_f, L0_gnn_b_f, L0_gnn_W_s, L0_gnn_b_s, L1_gnn_W1, L1_gnn_b1, L1_gnn_W2, L1_gnn_b2, L2_gnn_W1l, L2_gnn_b1l, L2_gnn_W1r, L2_gnn_b1r, L2_gnn_att1, L2_gnn_bias1, L2_gnn_W2l, L2_gnn_b2l, L2_gnn_W2r, L2_gnn_b2r, L2_gnn_att2, L2_gnn_bias2, L2_gnn_Wfc, L2_gnn_bfc, L3_gnn_W, L3_gnn_b, L3_gnn_gamma, L3_gnn_beta):
    import jax
    import jax.numpy as jnp

    def _L0_gnn_ref(x, edge_attr, distance, W_f, b_f, W_s, b_s, edge_index, batch):
        import jax, jax.numpy as jnp
        import numpy as np
        N_NODES = 50000
        N_EDGES = 12500
        C = 64
        EDGE_DIM = 64
        Z_DIM = 2 * C + EDGE_DIM
        SIGMA = 3.0
        src = edge_index[0]
        dst = edge_index[1]
        z = jnp.concatenate([x[dst], x[src], edge_attr], axis=-1)
        m = jax.nn.sigmoid(z @ W_f + b_f) * jax.nn.softplus(z @ W_s + b_s)
        m = m * jnp.exp(-distance ** 2 / SIGMA ** 2 / 2.0)[:, None]
        out = jax.ops.segment_sum(m, dst, num_segments=x.shape[0])
        return out + x

    def _L1_gnn_ref(h, e, src, dst, W1, b1, W2, b2):
        import jax, jax.numpy as jnp
        import numpy as np
        N_NODES = 3125
        N_EDGES = 50000
        IN_FEATS = 64
        OUT_FEATS = 64
        EDGE_FEATS = 1
        x = jnp.concatenate([h[src], h[dst], e], axis=1)
        m = jax.nn.relu(x @ W1 + b1) @ W2 + b2
        h_new = jax.ops.segment_sum(m, dst, num_segments=h.shape[0])
        return h_new

    def _L2_gnn_ref(x, edge_index, W1l, b1l, W1r, b1r, att1, bias1, W2l, b2l, W2r, b2r, att2, bias2, Wfc, bfc):
        import jax, jax.numpy as jnp
        import numpy as np
        H = 5
        NEG_SLOPE = 0.2
        N_NODES = 50000
        N_EDGES = 12500
        IN_CH = 64
        OUT_CH = 64

        def gatv2_layer(x, src, dst, Wl, bl, Wr, br, att, bias, n_nodes):
            C = att.shape[1]
            xl = (x @ Wl + bl).reshape(n_nodes, H, C)
            xr = (x @ Wr + br).reshape(n_nodes, H, C)
            e = jax.nn.leaky_relu(xl[src] + xr[dst], NEG_SLOPE)
            alpha = jnp.einsum('ehc,hc->eh', e, att)
            m = jax.ops.segment_max(alpha, dst, num_segments=n_nodes)
            m = jnp.where(jnp.isfinite(m), m, 0.0)
            a = jnp.exp(alpha - m[dst])
            denom = jax.ops.segment_sum(a, dst, num_segments=n_nodes)
            a = a / (denom[dst] + 1e-16)
            out = jax.ops.segment_sum(a[:, :, None] * xl[src], dst, num_segments=n_nodes)
            return out.mean(axis=1) + bias
        n = x.shape[0]
        loop = jnp.arange(n, dtype=edge_index.dtype)
        src = jnp.concatenate([edge_index[0], loop])
        dst = jnp.concatenate([edge_index[1], loop])
        h = jax.nn.relu(gatv2_layer(x, src, dst, W1l, b1l, W1r, b1r, att1, bias1, n))
        h = jax.nn.relu(gatv2_layer(h, src, dst, W2l, b2l, W2r, b2r, att2, bias2, n))
        return h @ Wfc + bfc

    def _L3_gnn_ref(feature, W, b, gamma, beta, src, dst):
        import jax, jax.numpy as jnp
        import numpy as np
        N_NODES = 3125
        N_EDGES = 50000
        D = 64
        BN_EPS = 1e-05
        n = feature.shape[0]
        ones_e = jnp.ones(src.shape[0], dtype=feature.dtype)
        deg_out = jnp.maximum(jax.ops.segment_sum(ones_e, src, num_segments=n), 1.0)
        h = feature * (deg_out ** (-0.5))[:, None]
        agg = jax.ops.segment_sum(h[src], dst, num_segments=n)
        deg_in = jnp.maximum(jax.ops.segment_sum(ones_e, dst, num_segments=n), 1.0)
        agg = agg * (deg_in ** (-0.5))[:, None]
        h = agg @ W + b
        mean = jnp.mean(h, axis=0)
        var = jnp.var(h, axis=0)
        h = (h - mean) * jax.lax.rsqrt(var + BN_EPS) * gamma + beta
        h = jax.nn.elu(h)
        return feature + h
    edge_index = jnp.stack([src, dst])
    batch0 = jnp.zeros((50000,), jnp.int32)
    h = jnp.maximum(_layernorm(x, axis=-1), 0.0)
    x = x + _L0_gnn_ref(h, edge_attr_64, edge_weight, L0_gnn_W_f, L0_gnn_b_f, L0_gnn_W_s, L0_gnn_b_s, edge_index, batch0)
    h = jnp.maximum(_layernorm(x, axis=-1), 0.0)
    x = x + _L1_gnn_ref(h, edge_weight1, src, dst, L1_gnn_W1, L1_gnn_b1, L1_gnn_W2, L1_gnn_b2)
    h = jnp.maximum(_layernorm(x, axis=-1), 0.0)
    x = x + _L2_gnn_ref(h, edge_index, L2_gnn_W1l, L2_gnn_b1l, L2_gnn_W1r, L2_gnn_b1r, L2_gnn_att1, L2_gnn_bias1, L2_gnn_W2l, L2_gnn_b2l, L2_gnn_W2r, L2_gnn_b2r, L2_gnn_att2, L2_gnn_bias2, L2_gnn_Wfc, L2_gnn_bfc)
    h = jnp.maximum(_layernorm(x, axis=-1), 0.0)
    x = x + _L3_gnn_ref(h, L3_gnn_W, L3_gnn_b, L3_gnn_gamma, L3_gnn_beta, src, dst)
    return x

_drawn_inputs = setup_inputs


def setup_inputs(seed=0):
    import zlib

    import numpy as np

    out = dict(_drawn_inputs(seed))
    spreads = {'L0_gnn_b_f': (0.0, 0.755),
     'L0_gnn_b_s': (0.0, 0.457),
     'L1_gnn_b1': (0.0, 0.1),
     'L1_gnn_b2': (0.0, 0.1),
     'L2_gnn_b1l': (0.0, 0.8),
     'L2_gnn_b1r': (0.0, 0.8),
     'L2_gnn_bias1': (0.0, 0.8),
     'L2_gnn_b2l': (0.0, 0.8),
     'L2_gnn_b2r': (0.0, 0.8),
     'L2_gnn_bias2': (0.0, 0.749),
     'L2_gnn_bfc': (0.0, 0.1),
     'L3_gnn_gamma': (1.0, 0.2),
     'L3_gnn_beta': (0.0, 0.344)}
    factors = {'L2_gnn_W1l': 8.0,
     'L2_gnn_W1r': 8.0,
     'L2_gnn_att1': 8.0,
     'L2_gnn_W2l': 8.0,
     'L2_gnn_W2r': 8.0,
     'L2_gnn_att2': 8.0,
     'L2_gnn_Wfc': 5.007,
     'L3_gnn_b': 8.0}
    for name, (base, spread) in spreads.items():
        noise = np.random.default_rng([zlib.crc32(name.encode()), seed]).standard_normal(out[name].shape)
        drawn = base * np.exp(spread * noise) if base else spread * noise
        out[name] = jnp.asarray(drawn.astype(out[name].dtype))
    for name, factor in factors.items():
        out[name] = (out[name] * factor).astype(out[name].dtype)
    return out
```

```python
from contextlib import ExitStack

import concourse.bass as bass
from concourse import mybir

F32 = mybir.dt.float32
BF16 = mybir.dt.bfloat16
I32 = mybir.dt.int32
ALU = mybir.AluOpType
ACT = mybir.ActivationFunctionType
AX = mybir.AxisListType
ds = bass.ds

P = 128
N = 50000
E = 50000
C = 64
H = 5
HC = H * C
TILES = 392
FULL = N // P
REST = N - FULL * P
BLK = 4
PAIRS = TILES // (2 * BLK)
STEPS = 2 * TILES
RING = 8
CT = 98
GRP = 14
LN_EPS = 1e-5
BN_EPS = 1e-5
MW = C + H + 3
SCAN_T = 25
SCAN_G = 16
SCAN_W = SCAN_G * P
SP_ROWS = SCAN_T * H
SLOPE = 0.2
BIG = 1.0e30
CHUNKS = [(0, 128), (128, 128), (256, 64)]


class Phase(ExitStack):

    def __init__(self, nc):
        super().__init__()
        self.nc, self.sems = nc, []

    def sem(self, name):
        self.sems.append(self.nc.alloc_semaphore(name))
        return self.sems[-1]

    def __exit__(self, *exc):
        if self.sems and exc[0] is None:
            self.nc.clear_and_free_semaphores(self.sems)
            self.nc.all_engine_barrier()
        return super().__exit__(*exc)


def wide(ap, axis, n):
    ap = ap.unsqueeze(axis)
    shape = list(ap.shape)
    shape[axis] = n
    return ap.broadcast_to(shape)


def loop(eng, n, body):
    body(0, True)
    with eng.Fori(1, n) as i:
        body(i, False)


class Chain:

    def __init__(self, eng, sem):
        self.eng, self.sem, self.n = eng, sem, 0

    def __call__(self, ins):
        self.n += 1
        ins.then_inc(self.sem, 1)
        self.eng.wait_ge(self.sem, self.n)


def build(nc, io, out):
    top = ExitStack()
    with top:
        def sb(name, shape, dt=F32, ctx=top):
            return ctx.enter_context(nc.sbuf_tensor(name, shape, dt))

        def dram(name, shape, dt=F32):
            return nc.dram_tensor(name, shape, dt, kind="Internal").ap()

        h_d = dram("h_d", (TILES * P, C))
        g_d = dram("g_d", (TILES * P, C))
        m_d = dram("m_d", (TILES * P, MW))
        hsT_d = dram("hsT_d", (2 * PAIRS, C, BLK * P))
        x_d = dram("x_d", (TILES * P, C))
        dst_d = dram("dst_d", (SCAN_T * SCAN_W + 2,), I32)

        acc = sb("acc", [P, (TILES + 1) * C])
        acc3 = acc[:, :].rearrange("p (b c) -> p b c", c=C)
        accw = sb("accw", [P, TILES + 1, H])
        deg_in = sb("deg_in", [P, TILES + 1, 1])
        deg_out = sb("deg_out", [P, TILES])
        dstf = sb("dstf", [P, TILES])
        dstrel = sb("dstrel", [P, STEPS])
        src_i = sb("src_i", [P, TILES], I32)
        dst_i = sb("dst_i", [P, TILES], I32)
        gate = sb("gate", [P, TILES])
        tile_of = sb("tile_of", [1, 2, STEPS], I32)
        ident = sb("ident", [P, P])
        iota_n = sb("iota_n", [P, P])
        iota_b = sb("iota_b", [P, TILES])
        ones = sb("ones", [P, P])
        eps = sb("eps", [P, 1])

        w0 = sb("w0", [P, 2 * C])
        w0a = sb("w0a", [C + 1, 2 * C])
        w1 = sb("w1", [P, C])
        w1t = sb("w1t", [2, C])
        w1b = sb("w1b", [C + 1, C])
        wst = [sb(f"wst{g}", [P, HC]) for g in range(2)]
        wsum = [sb(f"wsum{g}", [P, HC]) for g in range(2)]
        wl = [sb(f"wl{g}", [C + 1, HC]) for g in range(2)]
        blr = [sb(f"blr{g}", [P, 2, 3]) for g in range(2)]
        bsum = [sb(f"bsum{g}", [P, 3]) for g in range(2)]
        attbd = [sb(f"attbd{g}", [P, 3, H]) for g in range(2)]
        lin = [sb(f"lin{g}", [P, 2, H]) for g in range(2)]
        lin_b = [sb(f"lin_b{g}", [P, H]) for g in range(2)]
        gbias = [sb(f"gbias{g}", [P, C]) for g in range(2)]
        wfc = sb("wfc", [C + 1, C])
        w3 = sb("w3", [C + 1, C])
        gamma = sb("gamma", [P, C])
        beta = sb("beta", [P, C])

        pe_turn = top.enter_context(nc.semaphore("pe_turn"))

        common = dict(locals())
        setup(nc, io, common)
        node_pass(nc, common, 0)
        edge_pass(nc, io, common, 0)
        reduce_pass(nc, common, 0)
        node_pass(nc, common, 1)
        edge_pass(nc, io, common, 1)
        reduce_pass(nc, common, 1)
        node_pass(nc, common, 2)
        for g in range(2):
            with Phase(nc) as ctx:
                al = ctx.enter_context(nc.sbuf_tensor(f"al{g}", [P, SCAN_T * SCAN_G, H], F32))
                als = ctx.enter_context(nc.sbuf_tensor(f"als{g}", [P, SCAN_T * SCAN_G, H], F32))
                common.update(al=al, als=als)
                attention_logits(nc, common, g)
                softmax_stats(nc, common, g)
                attention_messages(nc, common, g)
            reduce_pass(nc, common, 2 + g)
            attention_nodes(nc, common, g)
        node_pass(nc, common, 3)
        edge_pass(nc, io, common, 3)
        reduce_pass(nc, common, 4)
        finish(nc, common, out)


def setup(nc, io, S):
    acc, acc3, ident, ones, iota_n, iota_b = (S[k] for k in ("acc", "acc3", "ident", "ones", "iota_n", "iota_b"))
    dstf, dstrel, src_i, dst_i, gate = (S[k] for k in ("dstf", "dstrel", "src_i", "dst_i", "gate"))
    tile_of, eps, dst_d = S["tile_of"], S["eps"], S["dst_d"]
    with Phase(nc) as ctx:
        def sb(name, shape, dt=F32):
            return ctx.enter_context(nc.sbuf_tensor(name, shape, dt))

        def sem(name):
            return ctx.sem((name))

        rows_i = sb("rows_i", [CT, 2, 4, P], I32)
        rows_f = sb("rows_f", [CT, 3, 4, P])
        guard = sb("guard", [1, 1280], I32)
        tile_hi = sb("tile_hi", [CT, 4], I32)
        key = sb("key", [CT, 4])
        step = sb("step", [P, STEPS])
        before = sb("before", [CT, STEPS])
        a_of = sb("a_of", [P, STEPS])
        b128 = sb("b128", [P, STEPS])
        clipped = sb("clipped", [P, TILES])
        square = sb("square", [P, TILES])
        turned = [ctx.enter_context(nc.psum_tensor(f"turned{k}", [P, TILES], F32)) for k in range(3)]
        counted = [ctx.enter_context(nc.psum_tensor(f"counted{k}", [P, STEPS // 2], F32)) for k in range(2)]
        s_loaded, s_guard, s_weights, s_x = sem("s_loaded"), sem("s_guard"), sem("s_weights"), sem("s_x")
        s_blank, s_const, s_pool = sem("s_blank"), sem("s_const"), sem("s_pool")
        s_rows, s_turned, s_cmp, s_count, s_v = sem("s_rows"), sem("s_turned"), sem("s_cmp"), sem("s_count"), sem("s_v")
        s_sq, s_gate = sem("s_sq"), sem("s_gate")
        att_row = [sb(f"att_row{g}", [P, 3, HC]) for g in range(2)]
        weights = []
        w = io

        def put(dst, src):
            weights.append((dst, src))

        for t, name in enumerate(("L0_gnn_W_f", "L0_gnn_W_s")):
            cols = slice(t * C, (t + 1) * C)
            put(S["w0"][0:C, cols], w[name][C:2 * C, :])
            put(S["w0"][C:P, cols], w[name][0:C, :])
            put(S["w0a"][0:C, cols], w[name][2 * C:3 * C, :])
            put(S["w0a"][C:C + 1, cols], w[("L0_gnn_b_f", "L0_gnn_b_s")[t]].rearrange("(a c) -> a c", a=1))
        put(S["w1"][:, :], w["L1_gnn_W1"][0:2 * C, :])
        put(S["w1t"][0:1, :], w["L1_gnn_W1"][2 * C:2 * C + 1, :])
        put(S["w1t"][1:2, :], w["L1_gnn_b1"].rearrange("(a c) -> a c", a=1))
        put(S["w1b"][0:C, :], w["L1_gnn_W2"][:, :])
        put(S["w1b"][C:C + 1, :], w["L1_gnn_b2"].rearrange("(a c) -> a c", a=1))
        for g in range(2):
            n = f"{g + 1}"
            put(S["wst"][g][0:C, :], w[f"L2_gnn_W{n}l"][:, :])
            put(S["wst"][g][C:P, :], w[f"L2_gnn_W{n}r"][:, :])
            put(S["wsum"][g][C:P, :], w[f"L2_gnn_W{n}l"][:, :])
            put(S["wl"][g][0:C, :], w[f"L2_gnn_W{n}l"][:, :])
            put(S["wl"][g][C:C + 1, :], w[f"L2_gnn_b{n}l"].rearrange("(a c) -> a c", a=1))
            for s, side in enumerate("lr"):
                for q, (f0, fn) in enumerate(CHUNKS):
                    put(S["blr"][g][0:fn, s, q:q + 1],
                        w[f"L2_gnn_b{n}{side}"][f0:f0 + fn].rearrange("(c a) -> c a", a=1))
            for h in range(H):
                r = C * (h % 2)
                put(S["attbd"][g][r:r + C, h // 2, h:h + 1], w[f"L2_gnn_att{n}"][h, :].rearrange("(c a) -> c a", a=1))
            put(att_row[g][:, 0, :], w[f"L2_gnn_att{n}"].rearrange("h (a c) -> a (h c)", a=1).broadcast_to([P, HC]))
            for s, side in enumerate("lr"):
                put(att_row[g][:, 1 + s, :], w[f"L2_gnn_b{n}{side}"].rearrange("(a c) -> a c", a=1).broadcast_to([P, HC]))
            put(S["gbias"][g][:, :], w[f"L2_gnn_bias{n}"].rearrange("(a c) -> a c", a=1).broadcast_to([P, C]))
        put(S["wfc"][0:C, :], w["L2_gnn_Wfc"][:, :])
        put(S["wfc"][C:C + 1, :], w["L2_gnn_bfc"].rearrange("(a c) -> a c", a=1))
        put(S["w3"][0:C, :], w["L3_gnn_W"][:, :])
        put(S["w3"][C:C + 1, :], w["L3_gnn_b"].rearrange("(a c) -> a c", a=1))
        put(S["gamma"][:, :], w["L3_gnn_gamma"].rearrange("(a c) -> a c", a=1).broadcast_to([P, C]))
        put(S["beta"][:, :], w["L3_gnn_beta"].rearrange("(a c) -> a c", a=1).broadcast_to([P, C]))

        with nc.Block() as block:
            @block.sync
            def _(sp):
                sp.wait_ge(s_blank, 1)
                lists = [(rows_i[:, 0], io["src"]), (rows_i[:, 1], io["dst"]), (rows_f[:, 2], io["edge_weight"])]
                for dst, src in lists:
                    for c in range(4):
                        n = min(CT, FULL - c * CT)
                        sp.dma_start(dst[0:n, c, :], src[c * CT * P:(c * CT + n) * P].rearrange("(t e) -> t e", e=P)).then_inc(s_loaded, 16)
                    sp.dma_start(dst[FULL - 3 * CT:FULL - 3 * CT + 1, 3, 0:REST],
                                 src[FULL * P:E].rearrange("(t e) -> t e", t=1)).then_inc(s_loaded, 16)
                sp.wait_ge(s_blank, 2)
                for b0 in range(0, FULL, 39):
                    sp.dma_start(acc3[:, b0:b0 + 39, :], io["x"][b0 * P:(b0 + 39) * P, :].rearrange("(b p) c -> p b c", p=P)).then_inc(s_x, 16)
                sp.dma_start(acc3[0:REST, FULL, :], io["x"][FULL * P:N, :]).then_inc(s_x, 16)
                sp.wait_ge(s_blank, 3)
                sp.dma_start(dst_d[1:E + 1].rearrange("(a n) -> a n", a=16), io["dst"].rearrange("(a n) -> a n", a=16)).then_inc(s_guard, 16)
                sp.dma_start(dst_d[0:1].rearrange("(a n) -> a n", a=1), guard[0:1, 0:1]).then_inc(s_guard, 16)
                sp.dma_start(dst_d[E + 1:].rearrange("(a n) -> a n", a=1), guard[0:1, 0:SCAN_T * SCAN_W + 1 - E]).then_inc(s_guard, 16)
                sp.wait_ge(s_guard, 48)
                sp.wait_ge(s_x, 11 * 16)

            @block.scalar
            def _(act):
                act.wait_ge(s_blank, 4)
                for dst, src in weights:
                    act.dma_start(dst, src).then_inc(s_weights, 16)
                act.wait_ge(s_sq, 1)
                nc.scalar.activation(gate[:, :], square[:, :], ACT.Exp, scale=-1.0 / (2 * 3.0 ** 2)).then_inc(s_gate, 1)

            @block.gpsimd
            def _(pool):
                nc.gpsimd.iota(guard[:, :], pattern=[[1, 1280]], base=1 << 20, channel_multiplier=0).then_inc(s_pool, 1)
                nc.gpsimd.iota(iota_n[:, :], pattern=[[1, P]], base=0, channel_multiplier=0,
                               allow_small_or_imprecise_dtypes=True).then_inc(s_pool, 1)
                nc.gpsimd.iota(iota_b[:, :], pattern=[[1, TILES]], base=0, channel_multiplier=0,
                               allow_small_or_imprecise_dtypes=True).then_inc(s_pool, 1)
                nc.gpsimd.iota(step[:, :], pattern=[[1, STEPS]], base=0, channel_multiplier=0,
                               allow_small_or_imprecise_dtypes=True).then_inc(s_pool, 1)
                nc.gpsimd.memset(ident[:, :], 0.0).then_inc(s_pool, 1)
                pool.wait_ge(s_pool, 5)
                nc.gpsimd.affine_select(out=ident[:, :], in_=ident[:, :], compare_op=ALU.not_equal, fill=1.0,
                                        base=0, pattern=[[-1, P]], channel_multiplier=1).then_inc(s_const, 1)

            @block.vector
            def _(dve):
                chain = Chain(dve, s_v)
                chain(nc.vector.memset(rows_i[:, 0], 0))
                chain(nc.vector.memset(rows_i[:, 1], 1 << 20))
                nc.vector.memset(rows_f[:, 2], 0.0).then_inc(s_blank, 1)
                nc.vector.memset(acc3[:, FULL:TILES + 1, :], 0.0).then_inc(s_blank, 1)
                dve.wait_ge(s_pool, 1)
                nc.vector.memset(eps[:, :], LN_EPS).then_inc(s_blank, 1)
                for g in range(2):
                    chain(nc.vector.memset(S["attbd"][g][:, :, :], 0.0))
                    chain(nc.vector.memset(S["blr"][g][:, :, :], 0.0))
                    chain(nc.vector.memset(S["lin"][g][0:C, 1, :], 0.0))
                nc.vector.memset(ones[:, :], 1.0).then_inc(s_blank, 1)
                dve.wait_ge(s_loaded, 15 * 16)
                nc.vector.tensor_copy(rows_f[:, 0:2].rearrange("t l c e -> t (l c e)"),
                                      rows_i[:, :].rearrange("t l c e -> t (l c e)")).then_inc(s_rows, 1)
                chain(nc.vector.tensor_single_scalar(tile_hi[:, :], rows_i[:, 1, :, P - 1], 7, ALU.logical_shift_right))
                chain(nc.vector.tensor_copy(key[:, :], tile_hi[:, :]))
                chain(nc.vector.tensor_scalar(key[:, :], key[:, :], float(TILES - 1), None, ALU.min))
                dve.wait_ge(s_pool, 4)
                for c in range(4):
                    dve.wait_ge(s_cmp, c)
                    chain(nc.vector.tensor_scalar(key[:, c:c + 1], key[:, c:c + 1], float(c * CT), None, ALU.add))
                    dve.wait_ge(s_const, 1)
                    if c == 0:
                        chain(nc.vector.tensor_tensor(before[0:CT, 0:P], ident[0:CT, :], iota_n[0:CT, :], ALU.mult))
                        chain(nc.vector.tensor_reduce(clipped[0:CT, 0:1], before[0:CT, 0:P], AX.X, ALU.add))
                    chain(nc.vector.tensor_tensor(key[:, c:c + 1], key[:, c:c + 1], clipped[0:CT, 0:1], ALU.add))
                    if c > 0:
                        dve.wait_ge(s_count, c)
                    nc.vector.tensor_scalar(before[:, :], step[0:CT, :], key[:, c:c + 1], None, ALU.is_gt).then_inc(s_cmp, 1)
                dve.wait_ge(s_count, 4)
                for k in range(2):
                    half = slice(k * STEPS // 2, (k + 1) * STEPS // 2)
                    chain(nc.vector.tensor_copy(a_of[:, half], counted[k][:, :]))
                chain(nc.vector.tensor_scalar(a_of[:, :], a_of[:, :], float(TILES - 1), None, ALU.min))
                chain(nc.vector.tensor_tensor(b128[:, :], step[:, :], a_of[:, :], ALU.subtract))
                chain(nc.vector.tensor_copy(tile_of[0:1, 0, :], a_of[0:1, :]))
                chain(nc.vector.tensor_copy(tile_of[0:1, 1, :], b128[0:1, :]))
                chain(nc.vector.tensor_scalar(b128[:, :], b128[:, :], float(P), None, ALU.mult))
                dve.wait_ge(s_turned, 1)
                chain(nc.vector.tensor_copy(src_i[:, :], turned[0][:, :]))
                chain(nc.vector.tensor_copy(dstf[:, :], turned[1][:, :]))
                chain(nc.vector.tensor_scalar(clipped[:, :], dstf[:, :], float(N - 1), None, ALU.min))
                chain(nc.vector.tensor_copy(dst_i[:, :], clipped[:, :]))
                chain(nc.vector.tensor_copy(square[:, :], turned[2][:, :]))
                chain(nc.vector.tensor_tensor(square[:, :], square[:, :], square[:, :], ALU.mult))
                dve.sem_inc(s_sq, 1)
                with dve.Fori(0, STEPS) as s:
                    a = dve.value_load(tile_of[0:1, 0, ds(s, 1)], min_val=0, max_val=TILES - 1)
                    nc.vector.tensor_tensor(dstrel[:, ds(s, 1)], dstf[:, ds(a, 1)], b128[:, ds(s, 1)], ALU.subtract)
                dve.wait_ge(s_weights, 16 * len(weights))
                for g in range(2):
                    chain(nc.vector.tensor_tensor(S["wsum"][g][C:P, :], S["wsum"][g][C:P, :], S["wst"][g][C:P, :], ALU.add))
                    chain(nc.vector.tensor_tensor(S["bsum"][g][:, :], S["blr"][g][:, 0, :], S["blr"][g][:, 1, :], ALU.add))
                    chain(nc.vector.tensor_scalar(S["bsum"][g][:, :], S["bsum"][g][:, :], 1.0 - SLOPE, None, ALU.mult))
                    chain(nc.vector.tensor_scalar(att_row[g][:, 0, :], att_row[g][:, 0, :], SLOPE, None, ALU.mult))
                    chain(nc.vector.tensor_tensor(att_row[g][:, 1, :], att_row[g][:, 1, :], att_row[g][:, 2, :], ALU.add))
                    for mat, to in ((S["wst"][g][:, :], S["lin"][g][:, 0, :]), (S["wsum"][g][C:P, :], S["lin"][g][C:P, 1, :]),
                                    (att_row[g][:, 1, :], S["lin_b"][g][:, :])):
                        p0 = P - mat.shape[0]
                        chain(nc.vector.tensor_tensor(att_row[g][p0:P, 2, :], mat, att_row[g][p0:P, 0, :], ALU.mult))
                        chain(nc.vector.tensor_reduce(to, att_row[g][p0:P, 2, :].rearrange("p (h c) -> p h c", h=H), AX.X, ALU.add))

            @block.tensor
            def _(pe):
                pe.wait_ge(s_const, 1)
                pe.wait_ge(s_rows, 1)
                for k in range(3):
                    for c in range(4):
                        last = nc.tensor.transpose(turned[k][:, c * CT:(c + 1) * CT], rows_f[:, k, c, :], ident[0:CT, 0:CT])
                last.then_inc(s_turned, 1)
                pe.wait_ge(s_blank, 4)
                for c in range(4):
                    pe.wait_ge(s_cmp, c + 1)
                    for k in range(2):
                        last = nc.tensor.matmul(counted[k][:, :], ones[0:CT, :], before[:, k * STEPS // 2:(k + 1) * STEPS // 2],
                                                start=(c == 0), stop=(c == 3))
                    last.then_inc(s_count, 1)


def node_pass(nc, S, layer):
    acc3, h_d, x_d, eps, deg_out = S["acc3"], S["h_d"], S["x_d"], S["eps"], S["deg_out"]
    groups = TILES // GRP
    with Phase(nc) as ctx:
        def sem(name):
            return ctx.sem((f"{name}{layer}"))

        def sb(name, shape):
            return [ctx.enter_context(nc.sbuf_tensor(f"{name}{layer}_{k}", shape, F32)) for k in range(2)]

        mean, var, rstd = sb("mean", [P, GRP]), sb("var", [P, GRP]), sb("rstd", [P, GRP])
        xc, sq, h, xs = (sb(n, [P, GRP, C]) for n in ("xc", "sq", "h", "xs"))
        dsc = ctx.enter_context(nc.sbuf_tensor(f"dsc{layer}", [P, TILES], F32))
        n_mean, n_cent, n_sq, n_var, n_std, n_norm, n_h, n_add, n_dg = (
            [sem(f"{n}_{k}_") for k in range(2)]
            for n in ("n_mean", "n_cent", "n_sq", "n_var", "n_std", "n_norm", "n_h", "n_add", "n_dg"))
        n_out = [sem(f"n_out_{k}_") for k in range(2)]
        n_rec = sem("n_rec")
        h_rows = h_d.rearrange("(g b p) c -> g p b c", p=P, b=GRP)
        x_rows = x_d.rearrange("(g b p) c -> g p b c", p=P, b=GRP)

        def bc(v):
            return wide(v, 2, C)

        with nc.Block() as block:
            @block.vector
            def _(dve):
                if layer == 3:
                    nc.vector.tensor_scalar(dsc[:, :], deg_out[:, :], 1.0, None, ALU.max).then_inc(n_rec, 1)
                    dve.wait_ge(n_rec, 2)
                    nc.vector.reciprocal(dsc[:, :], dsc[:, :]).then_inc(n_rec, 1)
                    dve.wait_ge(n_rec, 3)

                def body(j, first):
                    for k in range(2):
                        x = acc3[:, ds((2 * j + k) * GRP, GRP), :]
                        nc.vector.tensor_reduce(mean[k][:, :], x, AX.X, ALU.add).then_inc(n_mean[k], 1)
                    for k in range(2):
                        x = acc3[:, ds((2 * j + k) * GRP, GRP), :]
                        dve.wait_ge(n_mean[k], j * 2 + 1)
                        nc.vector.tensor_scalar(mean[k][:, :], mean[k][:, :], 1.0 / C, None, ALU.mult).then_inc(n_mean[k], 1)
                        dve.wait_ge(n_mean[k], j * 2 + 2)
                        if not first:
                            dve.wait_ge(n_h[k], j)
                        nc.vector.tensor_tensor(xc[k][:, :, :], x, bc(mean[k][:, :]), ALU.subtract).then_inc(n_cent[k], 1)
                    for k in range(2):
                        dve.wait_ge(n_sq[k], j + 1)
                        nc.vector.tensor_reduce(var[k][:, :], sq[k][:, :, :], AX.X, ALU.add).then_inc(n_var[k], 1)
                    for k in range(2):
                        dve.wait_ge(n_std[k], j + 1)
                        nc.vector.reciprocal(rstd[k][:, :], rstd[k][:, :]).then_inc(n_norm[k], 1)
                        dve.wait_ge(n_norm[k], j * 2 + 1)
                        nc.vector.tensor_tensor(xc[k][:, :, :], xc[k][:, :, :], bc(rstd[k][:, :]), ALU.mult).then_inc(n_norm[k], 1)
                    for k in range(2):
                        x = acc3[:, ds((2 * j + k) * GRP, GRP), :]
                        if layer == 0:
                            dve.wait_ge(n_h[k], j + 1)
                            nc.vector.tensor_tensor(x, x, h[k][:, :, :], ALU.add).then_inc(n_add[k], 1)
                        if layer == 3:
                            dve.wait_ge(n_h[k], j + 1)
                            if not first:
                                dve.wait_ge(n_out[k], 32 * j)
                            nc.vector.tensor_tensor(xs[k][:, :, :], x, h[k][:, :, :], ALU.add).then_inc(n_add[k], 1)
                            nc.vector.tensor_tensor(sq[k][:, :, :], h[k][:, :, :], bc(dsc[:, ds((2 * j + k) * GRP, GRP)]),
                                                    ALU.mult).then_inc(n_dg[k], 1)
                loop(dve, groups // 2, body)

            @block.scalar
            def _(act):
                if layer == 3:
                    act.wait_ge(n_rec, 1)
                    nc.scalar.activation(dsc[:, :], dsc[:, :], ACT.Sqrt).then_inc(n_rec, 1)

                def body(j, first):
                    for k in range(2):
                        act.wait_ge(n_cent[k], j + 1)
                        if layer == 3 and not first:
                            act.wait_ge(n_out[k], 32 * j)
                        nc.scalar.activation(sq[k][:, :, :], xc[k][:, :, :], ACT.Square).then_inc(n_sq[k], 1)
                    for k in range(2):
                        act.wait_ge(n_var[k], j + 1)
                        if not first:
                            act.wait_ge(n_norm[k], 2 * j)
                        nc.scalar.activation(rstd[k][:, :], var[k][:, :], ACT.Sqrt, bias=eps[:, 0:1], scale=1.0 / C).then_inc(n_std[k], 1)
                    for k in range(2):
                        act.wait_ge(n_norm[k], 2 * j + 2)
                        if not first:
                            act.wait_ge(n_out[k], (32 if layer in (2, 3) else 16) * j)
                            if layer in (0, 3):
                                act.wait_ge(n_add[k], j)
                            if layer == 3:
                                act.wait_ge(n_dg[k], j)
                        nc.scalar.activation(h[k][:, :, :], xc[k][:, :, :], ACT.Relu).then_inc(n_h[k], 1)
                loop(act, groups // 2, body)

            @block.sync
            def _(sp):
                def body(j, first):
                    for k in range(2):
                        g = 2 * j + k
                        if layer == 3:
                            sp.wait_ge(n_add[k], j + 1)
                            sp.dma_start(x_rows[ds(g, 1)].rearrange("g p b c -> (g p) b c"), xs[k][:, :, :]).then_inc(n_out[k], 16)
                            sp.wait_ge(n_dg[k], j + 1)
                            sp.dma_start(h_rows[ds(g, 1)].rearrange("g p b c -> (g p) b c"), sq[k][:, :, :]).then_inc(n_out[k], 16)
                        else:
                            sp.wait_ge(n_h[k], j + 1)
                            sp.dma_start(h_rows[ds(g, 1)].rearrange("g p b c -> (g p) b c"), h[k][:, :, :]).then_inc(n_out[k], 16)
                            if layer == 2:
                                sp.dma_start(x_rows[ds(g, 1)].rearrange("g p b c -> (g p) b c"), acc3[:, ds(g * GRP, GRP), :]).then_inc(n_out[k], 16)
                loop(sp, groups // 2, body)
                for k in range(2):
                    sp.wait_ge(n_out[k], (32 if layer in (2, 3) else 16) * (groups // 2))


def gather_front(nc, S, name, ctx, table, ends, release=1):
    idx = {e: [ctx.enter_context(nc.sbuf_tensor(f"idx_{e}_{name}_{k}", [P, BLK], I32)) for k in range(2)] for e in ends}
    z = [ctx.enter_context(nc.sbuf_tensor(f"z_{name}_{k}", [P, BLK, len(ends) * C], F32)) for k in range(2)]

    def sems(n):
        return [ctx.sem((f"{n}_{name}_{k}")) for k in range(2)]

    idx_in, gathered, z_used = sems("idx_in"), sems("gathered"), sems("z_used")
    turn = ctx.sem((f"turn_{name}"))

    def load_indices(sp, j, k, first):
        if not first:
            sp.wait_ge(gathered[k], 16 * BLK * len(ends) * j)
        for e in ends:
            sp.dma_start(idx[e][k][:, :], S[f"{e}_i"][:, ds((2 * j + k) * BLK, BLK)]).then_inc(idx_in[k], 16)

    def gather(pool):
        def body(j, first):
            for k in range(2):
                pool.wait_ge(idx_in[k], 16 * len(ends) * (j + 1))
                pool.sem_inc(turn)
                if not first:
                    pool.wait_ge(z_used[k], release * j)
                    pool.sem_inc(turn)
                for t in range(BLK):
                    for n, e in enumerate(ends):
                        nc.gpsimd.indirect_dma_start(
                            out=z[k][:, t, n * C:(n + 1) * C], out_offset=None, in_=table[:, :],
                            in_offset=bass.IndirectOffsetOnAxis(ap=idx[e][k][:, t:t + 1], axis=0)).then_inc(gathered[k], 16)
        loop(pool, PAIRS, body)

    return z, gathered, z_used, load_indices, gather


def edge_pass(nc, io, S, layer):
    h_d, m_d, ident = S["h_d"], S["m_d"], S["ident"]
    ends = ("src",) if layer == 3 else ("src", "dst")
    width = {0: C + 1, 1: C, 3: C}[layer]
    m_rows = m_d.rearrange("(g b p) c -> g p b c", p=P, b=BLK)
    LASTB = (E - (2 * PAIRS - 1) * BLK * P)
    with Phase(nc) as ctx:
        name = f"e{layer}"
        z, gathered, z_used, load_indices, gather = gather_front(nc, S, name, ctx, h_d, ends, 16 if layer == 3 else 1)

        def sems(n):
            return [ctx.sem((f"{n}_{name}_{k}")) for k in range(2)]

        def sb(n, shape, dt=F32):
            return [ctx.enter_context(nc.sbuf_tensor(f"{n}_{name}_{k}", shape, dt)) for k in range(2)]

        def ps(n, shape):
            return [ctx.enter_context(nc.psum_tensor(f"{n}_{name}_{k}", shape, F32)) for k in range(2)]

        m_ready, m_out = sems("m_ready"), sems("m_out")
        zT_ready, zT_used = sems("zT_ready"), sems("zT_used")
        if layer != 3:
            zTp, zT = ps("zTp", [P, BLK * P]), sb("zT", [P, BLK * P])
            m = sb("m", [P, BLK, width])
        if layer == 0:
            att, aTp, aT = sb("att", [P, BLK, C]), ps("aTp", [C, BLK * P]), sb("aT", [C + 1, BLK * P])
            pre = ps("pre", [P, BLK, 2 * C])
            ef, ab, ln = sb("ef", [P, BLK, C]), sb("ab", [P, BLK, C]), sb("ln", [P, BLK, C])
            lo = ctx.enter_context(nc.sbuf_tensor("src_lo", [P, TILES], I32))
            hi = ctx.enter_context(nc.sbuf_tensor("src_hi", [P, TILES], I32))
            lof = ctx.enter_context(nc.sbuf_tensor("src_lof", [P, TILES], F32))
            hif = ctx.enter_context(nc.sbuf_tensor("src_hif", [P, TILES], F32))
            real = ctx.enter_context(nc.sbuf_tensor("real", [P, TILES], F32))
            hot_lo, hot_hi = sb("hot_lo", [P, BLK, P], BF16), sb("hot_hi", [P, BLK, TILES], BF16)
            count = ctx.enter_context(nc.psum_tensor("count", [P, TILES], F32))
            hot, hot_used = sems("hot"), sems("hot_used")
            att_in, att_used, aT_ready = sems("att_in"), sems("att_used"), sems("aT_ready")
            pre_ready, act_step, act_done, dve_step = sems("pre_ready"), sems("act_step"), sems("act_done"), sems("dve_step")
            s_pre = ctx.sem(("s_pre"))
            s_ones = ctx.sem(("s_ones0"))
        if layer == 1:
            aux = sb("aux", [2, BLK * P])
            uTp, uT, mp = ps("uTp", [C, BLK * P]), sb("uT", [C + 1, BLK * P]), ps("mp", [P, BLK, C])
            aux_in, uTp_ready, uT_ready, mp_ready = sems("aux_in"), sems("uTp_ready"), sems("uT_ready"), sems("mp_ready")
            s_ones = ctx.sem(("s_ones1"))

        with nc.Block() as block:
            @block.gpsimd
            def _(pool):
                gather(pool)

            @block.sync
            def _(sp):
                if layer in (0, 1):
                    sp.wait_ge(s_ones, 1)

                def load_edge_data(j, k, first, last=False):
                    blk = 2 * j + k
                    if layer == 0:
                        if not first:
                            sp.wait_ge(att_used[k], j)
                        if last:
                            full = LASTB // P
                            r0 = (2 * PAIRS - 1) * BLK * P
                            sp.dma_start(att[k][:, 0:full, :], io["edge_attr_64"][r0:r0 + full * P, :].rearrange("(b p) c -> p b c", p=P)).then_inc(att_in[k], 16)
                            sp.dma_start(att[k][0:LASTB - full * P, full, :], io["edge_attr_64"][r0 + full * P:E, :]).then_inc(att_in[k], 16)
                        else:
                            sp.dma_start(att[k][:, :, :], io["edge_attr_64"][ds(blk * BLK * P, BLK * P), :].rearrange("(b p) c -> p b c", p=P)).then_inc(att_in[k], 32)
                    if layer == 1:
                        if not first:
                            sp.wait_ge(uTp_ready[k], j)
                        ew = io["edge_weight1"].rearrange("n a -> a n")
                        if last:
                            sp.dma_start(aux[k][0:1, 0:LASTB], ew[:, (2 * PAIRS - 1) * BLK * P:E]).then_inc(aux_in[k], 16)
                        else:
                            sp.dma_start(aux[k][0:1, :], ew[:, ds(blk * BLK * P, BLK * P)]).then_inc(aux_in[k], 16)

                def store(j, k):
                    rows = m_rows[ds(2 * j + k, 1)].rearrange("g p b c -> (g p) b c")
                    if layer == 3:
                        sp.wait_ge(gathered[k], 16 * BLK * (j + 1))
                        sp.dma_start(rows[:, :, 0:C], z[k][:, :, :]).then_inc(z_used[k], 16)
                    else:
                        sp.wait_ge(m_ready[k], j + 1)
                        sp.dma_start(rows[:, :, 0:width], m[k][:, :, :]).then_inc(m_out[k], 16)

                def body(j, first, last=False):
                    for k in range(2):
                        load_indices(sp, j, k, first)
                        load_edge_data(j, k, first, last and k == 1)
                        if not first:
                            store(j - 1, k)
                body(0, True)
                with sp.Fori(1, PAIRS - 1) as j:
                    body(j, False)
                body(PAIRS - 1, False, True)
                for k in range(2):
                    store(PAIRS - 1, k)
                for k in range(2):
                    sp.wait_ge(z_used[k] if layer == 3 else m_out[k], 16 * PAIRS)

            if layer != 3:
                @block.tensor
                def _(pe):
                    def body(j, first):
                        for k in range(2):
                            pe.wait_ge(gathered[k], 16 * BLK * len(ends) * (j + 1))
                            if not first:
                                pe.wait_ge(zT_ready[k], j)
                            for t in range(BLK):
                                tr = nc.tensor.transpose(zTp[k][:, t * P:(t + 1) * P], z[k][:, t, :], ident[:, :])
                            tr.then_inc(z_used[k], 1)
                            if layer == 0:
                                pe.wait_ge(att_in[k], 32 * (j + 1))
                                if not first:
                                    pe.wait_ge(aT_ready[k], j)
                                pe.sem_inc(S["pe_turn"])
                                for t in range(BLK):
                                    tr = nc.tensor.transpose(aTp[k][:, t * P:(t + 1) * P], att[k][:, t, :], ident[:, :])
                                tr.then_inc(att_used[k], 1)
                                pe.wait_ge(hot[k], j + 1)
                                for t in range(BLK):
                                    edge = first and k == 0 and t == 0
                                    mm = nc.tensor.matmul(count[:, :], hot_lo[k][:, t, :], hot_hi[k][:, t, :],
                                                          start=edge, stop=False, skip_group_check=True)
                                mm.then_inc(hot_used[k], 1)
                            pe.wait_ge(zT_ready[k], j + 1)
                            if layer == 0:
                                pe.wait_ge(aT_ready[k], j + 1)
                                if not first:
                                    pe.wait_ge(act_done[k], j)
                                    pe.wait_ge(dve_step[k], 4 * j)
                                for t in range(BLK):
                                    e = slice(t * P, (t + 1) * P)
                                    nc.tensor.matmul(pre[k][:, t, :], zT[k][:, e], S["w0"][:, :], start=True, stop=False)
                                    mm = nc.tensor.matmul(pre[k][:, t, :], aT[k][:, e], S["w0a"][:, :], start=False, stop=True)
                                mm.then_inc(pre_ready[k], 1)
                            else:
                                pe.wait_ge(aux_in[k], 16 * (j + 1))
                                if not first:
                                    pe.wait_ge(uT_ready[k], j)
                                pe.sem_inc(S["pe_turn"])
                                nc.tensor.matmul(uTp[k][:, :], S["w1"][:, :], zT[k][:, :], start=True, stop=False)
                                nc.tensor.matmul(uTp[k][:, :], S["w1t"][:, :], aux[k][:, :], start=False, stop=True).then_inc(uTp_ready[k], 1)
                                pe.wait_ge(uT_ready[k], j + 1)
                                if not first:
                                    pe.wait_ge(m_ready[k], j)
                                for t in range(BLK):
                                    mm = nc.tensor.matmul(mp[k][:, t, :], uT[k][:, t * P:(t + 1) * P], S["w1b"][:, :], start=True, stop=True)
                                mm.then_inc(mp_ready[k], 1)
                    loop(pe, PAIRS, body)
                    if layer == 0:
                        pe.wait_ge(s_pre, 9)
                        nc.tensor.matmul(count[:, :], hot_lo[0][:, 0, :], hot_hi[0][:, 0, :], start=False, stop=True,
                                         skip_group_check=True).then_inc(s_pre, 1)

                @block.scalar
                def _(act):
                    def body(j, first):
                        for k in range(2):
                            act.wait_ge(z_used[k], j + 1)
                            if not first:
                                act.wait_ge(pre_ready[k] if layer == 0 else uTp_ready[k], j)
                            nc.scalar.copy(zT[k][:, :], zTp[k][:, :]).then_inc(zT_ready[k], 1)
                            if layer == 0:
                                act.wait_ge(pre_ready[k], j + 1)
                                if not first:
                                    act.wait_ge(dve_step[k], 4 * j)
                                    act.wait_ge(m_ready[k], j)
                                nc.scalar.activation(ef[k][:, :, :], pre[k][:, :, 0:C], ACT.Exp, scale=-1.0).then_inc(act_done[k], 1)
                                nc.scalar.activation(ab[k][:, :, :], pre[k][:, :, C:2 * C], ACT.Abs).then_inc(act_step[k], 1)
                                act.wait_ge(act_step[k], 3 * j + 1)
                                nc.scalar.activation(ab[k][:, :, :], ab[k][:, :, :], ACT.Exp, scale=-1.0).then_inc(act_step[k], 1)
                                act.wait_ge(act_step[k], 3 * j + 2)
                                nc.scalar.activation(ln[k][:, :, :], ab[k][:, :, :], ACT.Ln, bias=1.0).then_inc(act_step[k], 1)
                            else:
                                act.wait_ge(uTp_ready[k], j + 1)
                                if not first:
                                    act.wait_ge(mp_ready[k], j)
                                nc.scalar.activation(uT[k][0:C, :], uTp[k][:, :], ACT.Relu).then_inc(uT_ready[k], 1)
                    loop(act, PAIRS, body)

                @block.vector
                def _(dve):
                    if layer == 0:
                        for k in range(2):
                            nc.vector.memset(att[k][:, :, :], 0.0).then_inc(s_pre, 1)
                            nc.vector.memset(aT[k][C:C + 1, :], 1.0)
                            nc.vector.memset(m[k][:, :, C:C + 1], 1.0)
                        nc.vector.memset(real[:, :], 0.0).then_inc(s_pre, 1)
                        dve.wait_ge(s_pre, 3)
                        dve.sem_inc(s_ones, 1)
                        nc.vector.tensor_single_scalar(lo[:, :], S["src_i"][:, :], P - 1, ALU.bitwise_and).then_inc(s_pre, 1)
                        nc.vector.tensor_single_scalar(hi[:, :], S["src_i"][:, :], 7, ALU.logical_shift_right).then_inc(s_pre, 1)
                        nc.vector.tensor_scalar(real[:, :], S["dstf"][:, :], float(1 << 20), float(-P), ALU.is_equal, ALU.mult).then_inc(s_pre, 1)
                        dve.wait_ge(s_pre, 6)
                        nc.vector.tensor_copy(hif[:, :], hi[:, :]).then_inc(s_pre, 1)
                        nc.vector.tensor_tensor(lof[:, :], lo[:, :], real[:, :], ALU.add).then_inc(s_pre, 1)
                        dve.wait_ge(s_pre, 8)
                    else:
                        for k in range(2):
                            nc.vector.memset(aux[k][:, :], 1.0)
                            ms = nc.vector.memset(uT[k][C:C + 1, :], 1.0)
                        ms.then_inc(s_ones, 1)

                    def body(j, first):
                        for k in range(2):
                            blk = 2 * j + k
                            if layer == 0:
                                if not first:
                                    dve.wait_ge(hot_used[k], j)
                                nc.vector.tensor_tensor(hot_lo[k][:, :, :], wide(S["iota_n"][:, :], 1, BLK),
                                                        wide(lof[:, ds(blk * BLK, BLK)], 2, P), ALU.is_equal)
                                nc.vector.tensor_tensor(hot_hi[k][:, :, :], wide(S["iota_b"][:, :], 1, BLK),
                                                        wide(hif[:, ds(blk * BLK, BLK)], 2, TILES), ALU.is_equal).then_inc(hot[k], 1)
                                dve.wait_ge(att_used[k], j + 1)
                                if not first:
                                    dve.wait_ge(pre_ready[k], j)
                                nc.vector.tensor_copy(aT[k][0:C, :], aTp[k][:, :]).then_inc(aT_ready[k], 1)
                                dve.wait_ge(act_done[k], j + 1)
                                nc.vector.tensor_scalar(ef[k][:, :, :], ef[k][:, :, :], 1.0, None, ALU.add).then_inc(dve_step[k], 1)
                                dve.wait_ge(dve_step[k], 4 * j + 1)
                                nc.vector.reciprocal(ef[k][:, :, :], ef[k][:, :, :]).then_inc(dve_step[k], 1)
                                dve.wait_ge(act_step[k], 3 * j + 3)
                                nc.vector.scalar_tensor_tensor(out=ln[k][:, :, :], in0=pre[k][:, :, C:2 * C], scalar=0.0, in1=ln[k][:, :, :],
                                                               op0=ALU.max, op1=ALU.add).then_inc(dve_step[k], 1)
                                dve.wait_ge(dve_step[k], 4 * j + 3)
                                nc.vector.tensor_tensor(ln[k][:, :, :], ln[k][:, :, :], ef[k][:, :, :], ALU.mult).then_inc(dve_step[k], 1)
                                dve.wait_ge(dve_step[k], 4 * j + 4)
                                if not first:
                                    dve.wait_ge(m_out[k], 16 * j)
                                nc.vector.tensor_tensor(m[k][:, :, 0:C], ln[k][:, :, :], wide(S["gate"][:, ds(blk * BLK, BLK)], 2, C),
                                                        ALU.mult).then_inc(m_ready[k], 1)
                            else:
                                dve.wait_ge(mp_ready[k], j + 1)
                                if not first:
                                    dve.wait_ge(m_out[k], 16 * j)
                                nc.vector.tensor_copy(m[k][:, :, :], mp[k][:, :, :]).then_inc(m_ready[k], 1)
                    loop(dve, PAIRS, body)
                    if layer == 0:
                        for k in range(2):
                            dve.wait_ge(hot_used[k], PAIRS)
                        nc.vector.memset(hot_lo[0][:, 0, :], 0.0).then_inc(s_pre, 1)
                        dve.wait_ge(s_pre, 10)
                        nc.vector.tensor_copy(S["deg_out"][:, :], count[:, :])


def reduce_pass(nc, S, which):
    acc, acc3, accw, deg_in, m_d = S["acc"], S["acc3"], S["accw"], S["deg_in"], S["m_d"]
    width = {0: C + 1, 1: C, 2: C + H, 3: C + H, 4: C}[which]
    with Phase(nc) as ctx:
        name = f"r{which}"
        m = [ctx.enter_context(nc.sbuf_tensor(f"m_{name}_{k}", [P, width], F32)) for k in range(RING)]
        hot = [ctx.enter_context(nc.sbuf_tensor(f"hot_{name}_{k}", [P, P], F32)) for k in range(RING)]
        part = [ctx.enter_context(nc.psum_tensor(f"part_{name}_{k}", [P, width], F32)) for k in range(RING)]

        def sems(n):
            return [ctx.sem((f"{n}_{name}_{k}")) for k in range(RING)]

        m_in, hot_ready, summed, added = sems("m_in"), sems("hot_ready"), sems("summed"), sems("added")
        s_zero = ctx.sem((f"s_zero_{name}"))
        m_rows = m_d.rearrange("(a p) c -> a p c", p=P)
        turns = STEPS // RING
        with nc.Block() as block:
            @block.sync
            def _(sp):
                def body(i, first):
                    for k in range(RING):
                        a = sp.value_load(S["tile_of"][0:1, 0, ds(i * RING + k, 1)], min_val=0, max_val=TILES - 1)
                        if not first:
                            sp.wait_ge(summed[k], i)
                        sp.dma_start(m[k][:, :], m_rows[ds(a, 1), :, 0:width].rearrange("a p c -> (a p) c")).then_inc(m_in[k], 16)
                loop(sp, turns, body)

            @block.tensor
            def _(pe):
                def body(i, first):
                    for k in range(RING):
                        pe.wait_ge(hot_ready[k], i + 1)
                        pe.wait_ge(m_in[k], 16 * (i + 1))
                        if not first:
                            pe.wait_ge(added[k], i)
                        nc.tensor.matmul(part[k][:, :], hot[k][:, :], m[k][:, :], start=True, stop=True).then_inc(summed[k], 1)
                loop(pe, turns, body)

            @block.vector
            def _(dve):
                if which >= 2:
                    nc.vector.memset(acc[:, :], 0.0).then_inc(s_zero, 1)
                    if which < 4:
                        nc.vector.memset(accw[:, :, :], 0.0).then_inc(s_zero, 1)
                    dve.wait_ge(s_zero, 2 if which < 4 else 1)
                if which == 0:
                    nc.vector.memset(deg_in[:, :, :], 0.0).then_inc(s_zero, 1)
                    dve.wait_ge(s_zero, 1)

                def body(i, first):
                    for k in range(RING):
                        if not first:
                            dve.wait_ge(summed[k], i)
                        nc.vector.tensor_scalar(hot[k][:, :], S["iota_n"][:, :], S["dstrel"][:, ds(i * RING + k, 1)], None,
                                                ALU.is_equal).then_inc(hot_ready[k], 1)
                    for k in range(RING):
                        b = dve.value_load(S["tile_of"][0:1, 1, ds(i * RING + k, 1)], min_val=0, max_val=TILES)
                        dve.wait_ge(summed[k], i + 1)
                        if k > 0:
                            dve.wait_ge(added[k - 1], i + 1)
                        elif not first:
                            dve.wait_ge(added[RING - 1], i)
                        x = acc3[:, ds(b, 1), :].rearrange("p b c -> p (b c)")
                        add = nc.vector.tensor_tensor(x, x, part[k][:, 0:C], ALU.add)
                        more = {0: deg_in, 2: accw, 3: accw}.get(which)
                        if more is not None:
                            y = more[:, ds(b, 1), :].rearrange("p b c -> p (b c)")
                            add = nc.vector.tensor_tensor(y, y, part[k][:, C:width], ALU.add)
                        add.then_inc(added[k], 1)
                loop(dve, turns, body)


def attention_logits(nc, S, g):
    table = S["h_d"] if g == 0 else S["g_d"]
    al, als, ident = S["al"], S["als"], S["ident"]
    with Phase(nc) as ctx:
        name = f"l{g}"
        z, gathered, z_used, load_indices, gather = gather_front(nc, S, name, ctx, table, ("src", "dst"))

        def sems(n):
            return [ctx.sem((f"{n}_{name}_{k}")) for k in range(2)]

        def sb(n, shape):
            return [ctx.enter_context(nc.sbuf_tensor(f"{n}_{name}_{k}", shape, F32)) for k in range(2)]

        zTp = [ctx.enter_context(nc.psum_tensor(f"zTp_{name}_{k}", [P, BLK * P], F32)) for k in range(2)]
        alp = [ctx.enter_context(nc.psum_tensor(f"alp_{name}_{k}", [P, BLK, 2, H], F32)) for k in range(2)]
        tp = [ctx.enter_context(nc.psum_tensor(f"tp_{name}_{q}", [P, BLK * P], F32)) for q in range(3)]
        leak = [ctx.enter_context(nc.sbuf_tensor(f"leak_{name}_{q}", [P, BLK * P], F32)) for q in range(6)]
        zT = sb("zT", [P, BLK * P])
        zT_ready, hs_out, alp_ready, al_ready = sems("zT_ready"), sems("hs_out"), sems("alp_ready"), sems("al_ready")
        t_ready = ctx.sem((f"t_ready_{name}"))
        leak_ready = ctx.sem((f"leak_ready_{name}"))
        s_pad = ctx.sem((f"s_pad_{name}"))

        with nc.Block() as block:
            @block.gpsimd
            def _(pool):
                gather(pool)

            @block.sync
            def _(sp):
                def store(j, k):
                    sp.wait_ge(zT_ready[k], j + 1)
                    sp.dma_start(S["hsT_d"][ds(2 * j + k, 1)].rearrange("g c e -> (g c) e"), zT[k][0:C, :]).then_inc(hs_out[k], 16)

                def body(j, first):
                    for k in range(2):
                        load_indices(sp, j, k, first)
                        if not first:
                            store(j - 1, k)
                loop(sp, PAIRS, body)
                for k in range(2):
                    store(PAIRS - 1, k)
                for k in range(2):
                    sp.wait_ge(hs_out[k], 16 * PAIRS)

            @block.tensor
            def _(pe):
                def body(j, first):
                    for k in range(2):
                        pe.wait_ge(gathered[k], 32 * BLK * (j + 1))
                        if not first:
                            pe.wait_ge(zT_ready[k], j)
                        for t in range(BLK):
                            tr = nc.tensor.transpose(zTp[k][:, t * P:(t + 1) * P], z[k][:, t, :], ident[:, :])
                        tr.then_inc(z_used[k], 1)
                        pe.wait_ge(zT_ready[k], j + 1)
                        for q in range(6):
                            f0, fn = CHUNKS[q % 3]
                            if not (first and k == 0 and q < 3):
                                pe.wait_ge(leak_ready, 12 * j + 6 * k + q - 2)
                            pe.sem_inc(S["pe_turn"])
                            if q < 3:
                                mm = nc.tensor.matmul(tp[q][0:fn, :], S["wst"][g][:, f0:f0 + fn], zT[k][:, :], start=True, stop=True)
                            else:
                                mm = nc.tensor.matmul(tp[q - 3][0:fn, :], S["wsum"][g][C:P, f0:f0 + fn], zT[k][C:P, :], start=True, stop=True)
                            mm.then_inc(t_ready, 1)
                        pe.wait_ge(leak_ready, 12 * j + 6 * k + 6)
                        if not first:
                            pe.wait_ge(al_ready[k], j)
                        for t in range(BLK):
                            e = slice(t * P, (t + 1) * P)
                            for q in range(6):
                                fn = CHUNKS[q % 3][1]
                                if q == 0:
                                    nc.tensor.matmul(alp[k][:, t, 0, :], zT[k][:, e], S["lin"][g][:, 0, :], start=True, stop=False)
                                if q == 3:
                                    nc.tensor.matmul(alp[k][:, t, 1, :], zT[k][:, e], S["lin"][g][:, 1, :], start=True, stop=False)
                                mm = nc.tensor.matmul(alp[k][:, t, q // 3, :], leak[q][0:fn, e],
                                                      S["attbd"][g][0:fn, q % 3, :], start=False, stop=(q % 3 == 2))
                        mm.then_inc(alp_ready[k], 1)
                loop(pe, PAIRS, body)

            @block.scalar
            def _(act):
                def body(j, first):
                    for k in range(2):
                        act.wait_ge(z_used[k], j + 1)
                        if not first:
                            act.wait_ge(hs_out[k], 16 * j)
                            act.wait_ge(alp_ready[k], j)
                        nc.scalar.copy(zT[k][:, :], zTp[k][:, :]).then_inc(zT_ready[k], 1)
                        if not (first and k == 0):
                            act.wait_ge(alp_ready[1 - k], j + k)
                        for q in range(6):
                            fn = CHUNKS[q % 3][1]
                            act.wait_ge(t_ready, 12 * j + 6 * k + q + 1)
                            nc.scalar.activation(leak[q][0:fn, :], tp[q % 3][0:fn, :], ACT.Relu, bias=S["bsum"][g][0:fn, q % 3:q % 3 + 1],
                                                 scale=1.0 - SLOPE).then_inc(leak_ready, 1)
                loop(act, PAIRS, body)

            @block.vector
            def _(dve):
                nc.vector.memset(al[:, TILES:, :], 0.0).then_inc(s_pad, 1)
                nc.vector.memset(als[:, TILES:, :], 0.0).then_inc(s_pad, 1)

                def body(j, first):
                    for k in range(2):
                        dve.wait_ge(alp_ready[k], j + 1)
                        rows = ds((2 * j + k) * BLK, BLK)
                        nc.vector.tensor_tensor(al[:, rows, :], alp[k][:, :, 0, :], wide(S["lin_b"][g][:, :], 1, BLK), ALU.add)
                        nc.vector.tensor_tensor(als[:, rows, :], alp[k][:, :, 1, :], wide(S["lin_b"][g][:, :], 1, BLK), ALU.add).then_inc(al_ready[k], 1)
                loop(dve, PAIRS, body)


def softmax_stats(nc, S, g):
    acc, al, als, ident, ones, dst_d = S["acc"], S["al"], S["als"], S["ident"], S["ones"], S["dst_d"]
    R, W, T, G = SP_ROWS, SCAN_W, SCAN_T, SCAN_G
    with Phase(nc) as ctx:
        name = f"s{g}"
        views = [acc[0:R, k * W:(k + 1) * W] for k in range(12)]
        lg, ls, prev, nxt, fwd, bwd, pen_f, pen_b, mx, own, tot, gap = views
        dst_own, dst_prev, dst_next = own.bitcast(I32), prev.bitcast(I32), nxt.bitcast(I32)

        def sb(n, shape):
            return ctx.enter_context(nc.sbuf_tensor(f"{n}_{name}", shape, F32))

        flag = sb("flag", [R, 2])
        carry = sb("carry", [R, 2])
        row = sb("row", [1, 4, R])
        packed = sb("packed", [P, 8, 4, R])
        pt = [ctx.enter_context(nc.psum_tensor(f"pt_{name}_{k}", [P, 4, P], F32)) for k in range(4)]
        prow = ctx.enter_context(nc.psum_tensor(f"prow_{name}", [1, 4, P], F32))
        pcol = ctx.enter_context(nc.psum_tensor(f"pcol_{name}", [P, 2], F32))
        s_in, s_v, s_t, s_p, s_q = (ctx.sem((f"{n}_{name}")) for n in ("s_in", "s_v", "s_t", "s_p", "s_q"))
        s_c, s_w = (ctx.sem((f"{n}_{name}")) for n in ("s_c", "s_w"))
        s_k = ctx.sem((f"s_k_{name}"))
        s_e, s_a = (ctx.sem((f"{n}_{name}")) for n in ("s_e", "s_a"))

        def by_chunk(x, gi):
            return x[:, :, :].rearrange("p (t g) h -> p g h t", g=G)[:, gi]

        with nc.Block() as block:
            @block.sync
            def _(sp):
                for off, dst in ((1, dst_own), (0, dst_prev), (2, dst_next)):
                    for h in range(H):
                        sp.dma_start(dst[h * T:(h + 1) * T, :], dst_d[off:off + T * W].rearrange("(t e) -> t e", e=W)).then_inc(s_in, 16)

            @block.tensor
            def _(pe):
                for x in range(2):
                    for q in range(4):
                        n = 4 * x + q
                        pe.wait_ge(s_k, n + 1)
                        if n >= 4:
                            pe.wait_ge(s_c, n - 3)
                        for r in range(4):
                            tr = nc.tensor.transpose(pt[n % 4][0:R, r, :], packed[:, n, r, :], ident[:, :])
                        tr.then_inc(s_t, 1)
                for turn in range(2):
                    pe.wait_ge(s_p, 2 * turn + 1)
                    for n in range(2):
                        nc.tensor.transpose(prow[0:1, n, 0:R], carry[:, n:n + 1], ident[0:R, 0:R])
                        tr = nc.tensor.transpose(prow[0:1, 2 + n, 0:R], flag[:, n:n + 1], ident[0:R, 0:R])
                    tr.then_inc(s_q, 1)
                    pe.wait_ge(s_p, 2 * turn + 2)
                    for n in range(2):
                        mm = nc.tensor.matmul(pcol[0:R, n:n + 1], row[0:1, n, :], ones[0:1, 0:1], start=True, stop=True)
                    mm.then_inc(s_q, 1)
                pe.wait_ge(s_w, 1)
                for x in range(2):
                    for q in range(4):
                        n = 8 + 4 * x + q
                        pe.wait_ge(s_c, n - 3)
                        for r in range(4):
                            gi = 4 * q + r
                            tr = nc.tensor.transpose(pt[n % 4][:, r, 0:R], (lg, ls)[x][:, gi * P:(gi + 1) * P], ident[0:R, 0:R])
                        tr.then_inc(s_t, 1)

            @block.scalar
            def _(act):
                act.wait_ge(s_e, 1)
                nc.scalar.activation(lg, lg, ACT.Exp).then_inc(s_a, 1)
                nc.scalar.activation(ls, ls, ACT.Exp).then_inc(s_a, 1)

            @block.vector
            def _(dve):
                chain = Chain(dve, s_v)
                tt, ts, scan = nc.vector.tensor_tensor, nc.vector.tensor_scalar, nc.vector.tensor_tensor_scan
                for n in range(8):
                    for r in range(4):
                        pk = nc.vector.tensor_copy(packed[:, n, r, :].rearrange("p (h t) -> p h t", t=T), by_chunk((al, als)[n // 4], 4 * (n % 4) + r))
                    pk.then_inc(s_k, 1)
                dve.wait_ge(s_in, 15 * 16)
                chain(nc.vector.tensor_copy(tot, dst_own))
                chain(nc.vector.tensor_copy(fwd, dst_prev))
                chain(nc.vector.tensor_copy(bwd, dst_next))
                chain(tt(prev, fwd, tot, ALU.is_equal))
                chain(tt(nxt, bwd, tot, ALU.is_equal))
                chain(ts(pen_f, prev, 1.0, BIG, ALU.subtract, ALU.mult))
                chain(ts(pen_b, nxt, 1.0, BIG, ALU.subtract, ALU.mult))
                for n in range(8):
                    dve.wait_ge(s_t, n + 1)
                    dst = (lg, ls)[n // 4][:, (n % 4) * 4 * P:(n % 4 + 1) * 4 * P]
                    nc.vector.tensor_copy(dst.rearrange("p (r e) -> p r e", r=4), pt[n % 4][0:R, :, :]).then_inc(s_c, 1)
                dve.wait_ge(s_c, 8)

                def both_ways(data, gain_f, gain_b, op0, op1, start, turn):
                    rev = slice(None, None, -1)
                    chain(nc.vector.tensor_reduce(flag[:, 0:1], gain_f, AX.X, ALU.min))
                    chain(nc.vector.tensor_reduce(flag[:, 1:2], gain_b, AX.X, ALU.min))
                    chain(scan(fwd, gain_f, data, start, op0, op1))
                    chain(scan(bwd[:, rev], gain_b[:, rev], data[:, rev], start, op0, op1))
                    chain(nc.vector.tensor_copy(carry[:, 0:1], fwd[:, W - 1:W]))
                    chain(nc.vector.tensor_copy(carry[:, 1:2], bwd[:, 0:1]))
                    dve.sem_inc(s_p, 1)
                    dve.wait_ge(s_q, 2 * turn + 1)
                    chain(nc.vector.tensor_copy(row[0:1, :, :], prow[0:1, :, 0:R]))
                    ends = row[0:1, 0:4, :].rearrange("a n (h t) -> a n h t", t=T)
                    chain(nc.vector.memset(ends[:, 2, :, 0:1], start))
                    chain(nc.vector.memset(ends[:, 3, :, T - 1:T], start))
                    out_f, out_b = tot[0:1, 0:R], tot[0:1, R:2 * R]
                    chain(scan(out_f, row[0:1, 2, :], row[0:1, 0, :], start, op0, op1))
                    chain(scan(out_b[:, rev], row[0:1, 3, rev], row[0:1, 1, rev], start, op0, op1))
                    chain(nc.vector.tensor_copy(row[0:1, 0, 1:R], out_f[:, 0:R - 1]))
                    chain(nc.vector.tensor_copy(row[0:1, 1, 0:R - 1], out_b[:, 1:R]))
                    chain(nc.vector.memset(ends[:, 0, :, 0:1], start))
                    chain(nc.vector.memset(ends[:, 1, :, T - 1:T], start))
                    dve.sem_inc(s_p, 1)
                    dve.wait_ge(s_q, 2 * turn + 2)
                    chain(nc.vector.tensor_copy(carry[:, :], pcol[0:R, :]))
                    chain(scan(fwd, gain_f, data, carry[:, 0:1], op0, op1))
                    chain(scan(bwd[:, rev], gain_b[:, rev], data[:, rev], carry[:, 1:2], op0, op1))

                both_ways(lg, pen_f, pen_b, ALU.add, ALU.max, -BIG, 0)
                chain(tt(mx, fwd, bwd, ALU.max))
                chain(tt(mx, mx, ls, ALU.max))
                chain(tt(lg, lg, mx, ALU.subtract))
                chain(tt(ls, ls, mx, ALU.subtract))
                dve.sem_inc(s_e, 1)
                dve.wait_ge(s_a, 2)
                both_ways(lg, prev, nxt, ALU.mult, ALU.add, 0.0, 1)
                chain(tt(tot, bwd, lg, ALU.subtract))
                chain(tt(tot, tot, fwd, ALU.add))
                chain(tt(tot, tot, ls, ALU.add))
                chain(nc.vector.reciprocal(tot, tot))
                chain(ts(tot, tot, 1.0 / H, None, ALU.mult))
                chain(tt(lg, lg, tot, ALU.mult))
                chain(tt(ls, ls, tot, ALU.mult))
                chain(ts(own, prev, -1.0, 1.0, ALU.mult, ALU.add))
                chain(tt(ls, ls, own, ALU.mult))
                dve.sem_inc(s_w, 1)
                for n in range(8, 16):
                    dve.wait_ge(s_t, n + 1)
                    x, q = (al, als)[(n - 8) // 4], n % 4
                    for r in range(4):
                        cp = nc.vector.tensor_copy(by_chunk(x, 4 * q + r), pt[n % 4][:, r, 0:R].rearrange("p (h t) -> p h t", t=T))
                    cp.then_inc(s_c, 1)


def attention_messages(nc, S, g):
    al, als, m_d = S["al"], S["als"], S["m_d"]
    m_rows = m_d.rearrange("(g b p) c -> g p b c", p=P, b=BLK)
    with Phase(nc) as ctx:
        name = f"m{g}"

        def sems(n):
            return [ctx.sem((f"{n}_{name}_{k}")) for k in range(2)]

        def sb(n, shape):
            return [ctx.enter_context(nc.sbuf_tensor(f"{n}_{name}_{k}", shape, F32)) for k in range(2)]

        hs, m = sb("hs", [C + 1, BLK * P]), sb("m", [P, BLK, C + H])
        prod = [sb(f"prod{t}", [P, HC]) for t in range(BLK)]
        xl = [[ctx.enter_context(nc.psum_tensor(f"xl_{name}_{k}_{t}", [P, HC], F32)) for t in range(BLK)] for k in range(2)]
        hs_in, xl_ready, weighted, m_ready, m_out = sems("hs_in"), sems("xl_ready"), sems("weighted"), sems("m_ready"), sems("m_out")
        s_ones = ctx.sem((f"s_ones_{name}"))
        with nc.Block() as block:
            @block.sync
            def _(sp):
                def store(j, k):
                    sp.wait_ge(m_ready[k], j + 1)
                    sp.dma_start(m_rows[ds(2 * j + k, 1), :, :, 0:C + H].rearrange("g p b c -> (g p) b c"), m[k][:, :, :]).then_inc(m_out[k], 16)

                def body(j, first):
                    for k in range(2):
                        if not first:
                            sp.wait_ge(xl_ready[k], BLK * j)
                        sp.dma_start(hs[k][0:C, :], S["hsT_d"][ds(2 * j + k, 1)].rearrange("g c e -> (g c) e")).then_inc(hs_in[k], 16)
                        if not first:
                            store(j - 1, k)
                loop(sp, PAIRS, body)
                for k in range(2):
                    store(PAIRS - 1, k)
                for k in range(2):
                    sp.wait_ge(m_out[k], 16 * PAIRS)

            @block.tensor
            def _(pe):
                pe.wait_ge(s_ones, 1)

                def body(j, first):
                    for k in range(2):
                        pe.wait_ge(hs_in[k], 16 * (j + 1))
                        for t in range(BLK):
                            if not first:
                                pe.wait_ge(weighted[k], BLK * (j - 1) + t + 1)
                            nc.tensor.matmul(xl[k][t][:, :], hs[k][:, t * P:(t + 1) * P], S["wl"][g][:, :], start=True, stop=True).then_inc(xl_ready[k], 1)
                loop(pe, PAIRS, body)

            @block.vector
            def _(dve):
                for k in range(2):
                    ms = nc.vector.memset(hs[k][C:C + 1, :], 1.0)
                ms.then_inc(s_ones, 1)

                def body(j, first):
                    for k in range(2):
                        tiles = (2 * j + k) * BLK
                        for t in range(BLK):
                            dve.wait_ge(xl_ready[k], BLK * j + t + 1)
                            nc.vector.tensor_tensor(prod[t][k][:, :].rearrange("p (h c) -> p h c", h=H), xl[k][t][:, :].rearrange("p (h c) -> p h c", h=H),
                                                    wide(al[:, ds(tiles + t, 1), :].rearrange("p t h -> p (t h)"), 2, C),
                                                    ALU.mult).then_inc(weighted[k], 1)
                        if not first:
                            dve.wait_ge(m_out[k], 16 * j)
                        nc.vector.tensor_scalar(m[k][:, :, C:C + H], als[:, ds(tiles, BLK), :], 1.0, None, ALU.mult)
                        for t in range(BLK):
                            dve.wait_ge(weighted[k], BLK * j + t + 1)
                            red = nc.vector.tensor_reduce(m[k][:, t, 0:C], prod[t][k][:, :].rearrange("p (h c) -> p c h", h=H), AX.X, ALU.add)
                        red.then_inc(m_ready[k], 1)
                loop(dve, PAIRS, body)


def attention_nodes(nc, S, g):
    acc3, accw, deg_in, ident = S["acc3"], S["accw"], S["deg_in"], S["ident"]
    table = S["h_d"] if g == 0 else S["g_d"]
    rows_in = table.rearrange("(g b p) c -> g p b c", p=P, b=BLK)
    x_rows = S["x_d"].rearrange("(g b p) c -> g p b c", p=P, b=BLK)
    g_rows = S["g_d"].rearrange("(g b p) c -> g p b c", p=P, b=BLK)
    with Phase(nc) as ctx:
        name = f"a{g}"

        def sems(n):
            return [ctx.sem((f"{n}_{name}_{k}")) for k in range(2)]

        def sb(n, shape):
            return [ctx.enter_context(nc.sbuf_tensor(f"{n}_{name}_{k}", shape, F32)) for k in range(2)]

        hn, hT, self_sum, xo, prod = (sb("hn", [P, BLK, C]), sb("hT", [C + 1, BLK * P]), sb("self_sum", [P, BLK, C]),
                                      sb("xo", [P, BLK, C]), sb("prod", [P, BLK, HC]))
        gT = sb("gT", [C + 1, BLK * P])
        hTp = ctx.enter_context(nc.psum_tensor(f"hTp_{name}", [C, BLK * P], F32))
        xl = [ctx.enter_context(nc.psum_tensor(f"xl_{name}_{t}", [P, HC], F32)) for t in range(BLK)]
        gTp = ctx.enter_context(nc.psum_tensor(f"gTp_{name}", [C, BLK * P], F32))
        fcp = ctx.enter_context(nc.psum_tensor(f"fcp_{name}", [P, BLK, C], F32))
        hn_in, xo_in, hTp_ready, hT_ready, xl_ready, weighted, step, g_ready, g_out = (
            sems(n) for n in ("hn_in", "xo_in", "hTp_ready", "hT_ready", "xl_ready", "weighted", "step", "g_ready", "g_out"))
        gTp_ready, gT_ready, fcp_ready, x_done = sems("gTp_ready"), sems("gT_ready"), sems("fcp_ready"), sems("x_done")
        s_ones = ctx.sem((f"s_ones_{name}"))
        wself = ctx.enter_context(nc.sbuf_tensor(f"wself_{name}", [P, TILES, H], F32))
        alone = ctx.enter_context(nc.sbuf_tensor(f"alone_{name}", [P, TILES], F32))

        with nc.Block() as block:
            @block.sync
            def _(sp):
                def store(j, k):
                    sp.wait_ge(g_ready[k], j + 1)
                    sp.dma_start(g_rows[ds(2 * j + k, 1)].rearrange("g p b c -> (g p) b c"), self_sum[k][:, :, :]).then_inc(g_out[k], 16)

                def body(j, first):
                    for k in range(2):
                        if not first:
                            sp.wait_ge(hTp_ready[k], j)
                        sp.dma_start(hn[k][:, :, :], rows_in[ds(2 * j + k, 1)].rearrange("g p b c -> (g p) b c")).then_inc(hn_in[k], 16)
                        if g == 1:
                            if not first:
                                sp.wait_ge(x_done[k], j)
                            sp.dma_start(xo[k][:, :, :], x_rows[ds(2 * j + k, 1)].rearrange("g p b c -> (g p) b c")).then_inc(xo_in[k], 16)
                        if g == 0 and not first:
                            store(j - 1, k)
                loop(sp, PAIRS, body)
                if g == 0:
                    for k in range(2):
                        store(PAIRS - 1, k)
                    for k in range(2):
                        sp.wait_ge(g_out[k], 16 * PAIRS)

            @block.tensor
            def _(pe):
                pe.wait_ge(s_ones, 1)

                def body(j, first):
                    for k in range(2):
                        pe.wait_ge(hn_in[k], 16 * (j + 1))
                        if not (first and k == 0):
                            pe.wait_ge(hT_ready[1 - k], j + k)
                        pe.sem_inc(S["pe_turn"])
                        for t in range(BLK):
                            tr = nc.tensor.transpose(hTp[:, t * P:(t + 1) * P], hn[k][:, t, :], ident[:, :])
                        tr.then_inc(hTp_ready[k], 1)
                        pe.wait_ge(hT_ready[k], j + 1)
                        if not (first and k == 0):
                            pe.wait_ge(weighted[1 - k], BLK * (j + k))
                        for t in range(BLK):
                            mm = nc.tensor.matmul(xl[t][:, :], hT[k][:, t * P:(t + 1) * P], S["wl"][g][:, :], start=True, stop=True)
                            mm.then_inc(xl_ready[k], 1)
                        if g == 1:
                            pe.wait_ge(g_ready[k], j + 1)
                            if not (first and k == 0):
                                pe.wait_ge(gT_ready[1 - k], j + k)
                            pe.sem_inc(S["pe_turn"])
                            for t in range(BLK):
                                tr = nc.tensor.transpose(gTp[:, t * P:(t + 1) * P], self_sum[k][:, t, :], ident[:, :])
                            tr.then_inc(gTp_ready[k], 1)
                            pe.wait_ge(gT_ready[k], j + 1)
                            if not (first and k == 0):
                                pe.wait_ge(x_done[1 - k], j + k)
                            for t in range(BLK):
                                mm = nc.tensor.matmul(fcp[:, t, :], gT[k][:, t * P:(t + 1) * P], S["wfc"][:, :], start=True, stop=True)
                            mm.then_inc(fcp_ready[k], 1)
                loop(pe, PAIRS, body)

            @block.scalar
            def _(act):
                def body(j, first):
                    for k in range(2):
                        act.wait_ge(hTp_ready[k], j + 1)
                        if not first:
                            act.wait_ge(xl_ready[k], BLK * j)
                        nc.scalar.copy(hT[k][0:C, :], hTp[:, :]).then_inc(hT_ready[k], 1)
                        if g == 1:
                            act.wait_ge(gTp_ready[k], j + 1)
                            if not first:
                                act.wait_ge(fcp_ready[k], j)
                            nc.scalar.copy(gT[k][0:C, :], gTp[:, :]).then_inc(gT_ready[k], 1)
                loop(act, PAIRS, body)

            @block.vector
            def _(dve):
                for k in range(2):
                    nc.vector.memset(hT[k][C:C + 1, :], 1.0)
                    ms = nc.vector.memset(gT[k][C:C + 1, :], 1.0)
                ms.then_inc(s_ones, 1)
                nc.vector.tensor_scalar(alone[:, :], deg_in[:, 0:TILES, 0], 0.0, 1.0 / H, ALU.is_equal, ALU.mult).then_inc(s_ones, 1)
                dve.wait_ge(s_ones, 2)
                nc.vector.tensor_tensor(wself[:, :, :], accw[:, 0:TILES, :], wide(alone[:, :], 2, H), ALU.add).then_inc(s_ones, 1)
                dve.wait_ge(s_ones, 3)

                def body(j, first):
                    for k in range(2):
                        tiles = (2 * j + k) * BLK
                        here = acc3[:, ds(tiles, BLK), :]
                        for t in range(BLK):
                            dve.wait_ge(xl_ready[k], BLK * j + t + 1)
                            nc.vector.tensor_tensor(prod[k][:, t, :].rearrange("p (h c) -> p h c", h=H), xl[t][:, :].rearrange("p (h c) -> p h c", h=H),
                                                    wide(wself[:, ds(tiles + t, 1), :].rearrange("p t h -> p (t h)"), 2, C),
                                                    ALU.mult).then_inc(weighted[k], 1)
                        dve.wait_ge(weighted[k], BLK * (j + 1))
                        if not first:
                            if g == 0:
                                dve.wait_ge(g_out[k], 16 * j)
                            else:
                                dve.wait_ge(gTp_ready[k], j)
                        for t in range(BLK):
                            red = nc.vector.tensor_reduce(self_sum[k][:, t, :], prod[k][:, t, :].rearrange("p (h c) -> p c h", h=H), AX.X, ALU.add)
                        red.then_inc(step[k], 1)
                        dve.wait_ge(step[k], 3 * j + 1)
                        nc.vector.tensor_tensor(self_sum[k][:, :, :], self_sum[k][:, :, :], here, ALU.add).then_inc(step[k], 1)
                        dve.wait_ge(step[k], 3 * j + 2)
                        nc.vector.tensor_tensor(self_sum[k][:, :, :], self_sum[k][:, :, :], wide(S["gbias"][g][:, :], 1, BLK),
                                                ALU.add).then_inc(step[k], 1)
                        dve.wait_ge(step[k], 3 * j + 3)
                        nc.vector.tensor_scalar(self_sum[k][:, :, :], self_sum[k][:, :, :], 0.0, None, ALU.max).then_inc(g_ready[k], 1)
                        if g == 1:
                            dve.wait_ge(fcp_ready[k], j + 1)
                            dve.wait_ge(xo_in[k], 16 * (j + 1))
                            nc.vector.tensor_tensor(here, fcp[:, :, :], xo[k][:, :, :], ALU.add).then_inc(x_done[k], 1)
                loop(dve, PAIRS, body)


def finish(nc, S, out):
    acc3, deg_in, ident, ones, x_d = S["acc3"], S["deg_in"], S["ident"], S["ones"], S["x_d"]
    x_rows = x_d.rearrange("(g b p) c -> g p b c", p=P, b=BLK)
    TRUE = FULL - FULL % BLK
    with Phase(nc) as ctx:
        name = "f"

        def sems(n):
            return [ctx.sem((f"{n}_{name}_{k}")) for k in range(2)]

        def sem(n):
            return ctx.sem((f"{n}_{name}"))

        def sb(n, shape):
            return [ctx.enter_context(nc.sbuf_tensor(f"{n}_{name}_{k}", shape, F32)) for k in range(2)]

        def one(n, shape):
            return ctx.enter_context(nc.sbuf_tensor(f"{n}_{name}", shape, F32))

        din = one("din", [P, TILES])
        aT = sb("aT", [C + 1, BLK * P])
        aTp = [ctx.enter_context(nc.psum_tensor(f"aTp_{k}", [C, BLK * P], F32)) for k in range(2)]
        hp = [ctx.enter_context(nc.psum_tensor(f"hp_{k}", [P, BLK, C], F32)) for k in range(2)]
        tot = ctx.enter_context(nc.psum_tensor("tot_f", [P, 2, C], F32))
        aTp_ready, aT_ready, hp_ready, hp_done, scaled = sems("aTp_ready"), sems("aT_ready"), sems("hp_ready"), sems("hp_done"), sems("scaled")
        s_ones, s_d, s_v, s_sum, s_tot, s_a = sem("s_ones"), sem("s_d"), sem("s_v"), sem("s_sum"), sem("s_tot"), sem("s_a")
        GB = 2 * BLK
        sums, mean, scale, shift = one("sums", [P, C]), one("mean", [P, C]), one("scale", [P, C]), one("shift", [P, C])
        psum28 = one("psum28", [P, PAIRS, C])
        fs, y, neg, sq = (sb(n, [P, BLK, C]) for n in ("fs", "y", "neg", "sq"))
        with nc.Block() as block:
            @block.vector
            def _(dve):
                for k in range(2):
                    nc.vector.memset(aT[k][C:C + 1, :], 1.0)
                nc.vector.tensor_scalar(din[:, :], deg_in[:, 0:TILES, 0], 1.0, None, ALU.max).then_inc(s_d, 1)
                dve.wait_ge(s_d, 2)
                nc.vector.reciprocal(din[:, :], din[:, :]).then_inc(s_d, 1)
                dve.wait_ge(s_d, 3)

                def body(j, first):
                    for k in range(2):
                        here = acc3[:, ds((2 * j + k) * BLK, BLK), :]
                        if not first:
                            dve.wait_ge(aTp_ready[k], j)
                        nc.vector.tensor_tensor(fs[k][:, :, :], here, wide(din[:, ds((2 * j + k) * BLK, BLK)], 2, C), ALU.mult).then_inc(scaled[k], 1)
                    for k in range(2):
                        here = acc3[:, ds((2 * j + k) * BLK, BLK), :]
                        dve.wait_ge(hp_ready[k], j + 1)
                        nc.vector.tensor_scalar(here, hp[k][:, :, :], 1.0, None, ALU.mult).then_inc(hp_done[k], 1)
                loop(dve, PAIRS, body)

            @block.scalar
            def _(act):
                act.wait_ge(s_d, 1)
                nc.scalar.activation(din[:, :], din[:, :], ACT.Sqrt).then_inc(s_d, 1)

                def body(j, first):
                    for k in range(2):
                        act.wait_ge(aTp_ready[k], j + 1)
                        if not first:
                            act.wait_ge(hp_ready[k], j)
                        nc.scalar.copy(aT[k][0:C, :], aTp[k][:, :]).then_inc(aT_ready[k], 1)
                loop(act, PAIRS, body)

            @block.tensor
            def _(pe):
                pe.wait_ge(s_d, 3)

                def body(j, first):
                    for k in range(2):
                        pe.wait_ge(scaled[k], j + 1)
                        if not first:
                            pe.wait_ge(aT_ready[k], j)
                        pe.sem_inc(S["pe_turn"])
                        for t in range(BLK):
                            tr = nc.tensor.transpose(aTp[k][:, t * P:(t + 1) * P], fs[k][:, t, :], ident[:, :])
                        tr.then_inc(aTp_ready[k], 1)
                        pe.wait_ge(aT_ready[k], j + 1)
                        if not first:
                            pe.wait_ge(hp_done[k], j)
                        for t in range(BLK):
                            mm = nc.tensor.matmul(hp[k][:, t, :], aT[k][:, t * P:(t + 1) * P], S["w3"][:, :], start=True, stop=True)
                        mm.then_inc(hp_ready[k], 1)
                loop(pe, PAIRS, body)

        out_full = out[0:FULL * P, :].rearrange("(b p) c -> p b c", p=P)
        LB = 2 * PAIRS - 1
        with nc.Block() as block:
            y_in, y_done, e1, e2, e3, out_sem, o_in = (sems(n) for n in ("y_in", "y_done", "e1", "e2", "e3", "out_sem", "o_in"))
            s_sq = sem("s_sq")

            @block.vector
            def _(dve):
                chain = Chain(dve, s_v)

                chain(nc.vector.tensor_reduce(sums[:, :], acc3[:, 0:FULL, :].rearrange("p b c -> p c b"), AX.X, ALU.add))
                chain(nc.vector.tensor_tensor(sums[0:REST, :], sums[0:REST, :], acc3[0:REST, FULL, :], ALU.add))
                dve.sem_inc(s_sum, 1)
                dve.wait_ge(s_tot, 1)
                chain(nc.vector.tensor_scalar(mean[:, :], tot[:, 0, :], 1.0 / N, None, ALU.mult))
                chain(nc.vector.tensor_tensor(acc3[:, 0:TILES, :], acc3[:, 0:TILES, :], wide(mean[:, :], 1, TILES), ALU.subtract))

                def body(j, first):
                    for k in range(2):
                        here = acc3[:, ds((2 * j + k) * BLK, BLK), :]
                        if not first:
                            dve.wait_ge(y_done[k], j)
                        nc.vector.tensor_tensor(sq[k][:, :, :], here, here, ALU.mult).then_inc(y_in[k], 1)
                        dve.wait_ge(y_in[k], j + 1)
                        nc.vector.tensor_reduce(psum28[:, ds(j, 1), :].rearrange("p j c -> p (j c)") if k == 0 else y[0][:, 0, :],
                                                sq[k][:, :, :].rearrange("p b c -> p c b"), AX.X, ALU.add).then_inc(y_done[k], 1)
                        if k == 1:
                            dve.wait_ge(y_done[1], j + 1)
                            v = psum28[:, ds(j, 1), :].rearrange("p j c -> p (j c)")
                            nc.vector.tensor_tensor(v, v, y[0][:, 0, :], ALU.add).then_inc(s_sq, 1)
                            dve.wait_ge(s_sq, j + 1)
                chain(nc.vector.memset(acc3[:, FULL + 1:TILES, :], 0.0))
                chain(nc.vector.tensor_copy(y[1][0:REST, 0, :], acc3[0:REST, FULL, :]))
                chain(nc.vector.memset(acc3[:, FULL, :], 0.0))
                chain(nc.vector.tensor_copy(acc3[0:REST, FULL, :], y[1][0:REST, 0, :]))
                loop(dve, PAIRS, body)
                chain(nc.vector.tensor_reduce(sums[:, :], psum28[:, :, :].rearrange("p j c -> p c j"), AX.X, ALU.add))
                dve.sem_inc(s_sum, 1)
                dve.wait_ge(s_a, 1)
                chain(nc.vector.reciprocal(scale[:, :], shift[:, :]))
                chain(nc.vector.tensor_tensor(scale[:, :], scale[:, :], S["gamma"][:, :], ALU.mult))

                def tail(j, first):
                    for k in range(2):
                        here = acc3[:, ds((2 * j + k) * BLK, BLK), :]
                        nc.vector.tensor_tensor(here, here, wide(scale[:, :], 1, BLK), ALU.mult).then_inc(e1[k], 1)
                    for k in range(2):
                        here = acc3[:, ds((2 * j + k) * BLK, BLK), :]
                        dve.wait_ge(e1[k], 3 * j + 1)
                        if not first:
                            dve.wait_ge(e3[k], 2 * j)
                        nc.vector.tensor_tensor(y[k][:, :, :], here, wide(S["beta"][:, :], 1, BLK), ALU.add).then_inc(e1[k], 1)
                    for k in range(2):
                        dve.wait_ge(e1[k], 3 * j + 2)
                        if not first:
                            dve.wait_ge(e2[k], j)
                        nc.vector.tensor_scalar(neg[k][:, :, :], y[k][:, :, :], 0.0, None, ALU.min).then_inc(e1[k], 1)
                    for k in range(2):
                        dve.wait_ge(o_in[k], 16 * (j + 1))
                        nc.vector.scalar_tensor_tensor(out=y[k][:, :, :], in0=y[k][:, :, :], scalar=0.0, in1=fs[k][:, :, :],
                                                       op0=ALU.max, op1=ALU.add).then_inc(e3[k], 1)
                    for k in range(2):
                        here = acc3[:, ds((2 * j + k) * BLK, BLK), :]
                        dve.wait_ge(e2[k], j + 1)
                        dve.wait_ge(e3[k], 2 * j + 1)
                        nc.vector.scalar_tensor_tensor(out=here, in0=sq[k][:, :, :], scalar=-1.0, in1=y[k][:, :, :],
                                                       op0=ALU.add, op1=ALU.add).then_inc(e3[k], 1)
                loop(dve, PAIRS, tail)

            @block.scalar
            def _(act):
                act.wait_ge(s_tot, 2)
                nc.scalar.activation(shift[:, :], tot[:, 1, :], ACT.Sqrt, bias=S["eps"][:, 0:1], scale=1.0 / N).then_inc(s_a, 1)

                def body(j, first):
                    for k in range(2):
                        act.wait_ge(e1[k], 3 * j + 3)
                        if not first:
                            act.wait_ge(e3[k], 2 * j)
                        nc.scalar.activation(sq[k][:, :, :], neg[k][:, :, :], ACT.Exp).then_inc(e2[k], 1)
                loop(act, PAIRS, body)

            @block.tensor
            def _(pe):
                for n in range(2):
                    pe.wait_ge(s_sum, n + 1)
                    nc.tensor.matmul(tot[:, n, :], ones[:, :], sums[:, :], start=True, stop=True).then_inc(s_tot, 1)

            @block.sync
            def _(sp):
                def body(j, first):
                    for k in range(2):
                        blk = 2 * j + k
                        if not first:
                            sp.wait_ge(e3[k], 2 * j)
                        sp.dma_start(fs[k][:, :, :], x_rows[ds(blk, 1)].rearrange("g p b c -> (g p) b c")).then_inc(o_in[k], 16)
                        if not first:
                            sp.dma_start(out[ds((blk - 2) * BLK * P, BLK * P), :].rearrange("(b p) c -> p b c", p=P),
                                         acc3[:, ds((blk - 2) * BLK, BLK), :]).then_inc(out_sem[k], 16)
                loop(sp, PAIRS, body)
                sp.wait_ge(e3[0], 2 * PAIRS)
                sp.dma_start(out[(LB - 1) * BLK * P:LB * BLK * P, :].rearrange("(b p) c -> p b c", p=P), acc3[:, (LB - 1) * BLK:LB * BLK, :]).then_inc(out_sem[0], 16)
                sp.wait_ge(e3[1], 2 * PAIRS)
                sp.dma_start(out[LB * BLK * P:FULL * P, :].rearrange("(b p) c -> p b c", p=P), acc3[:, LB * BLK:FULL, :]).then_inc(out_sem[1], 16)
                sp.dma_start(out[FULL * P:N, :], acc3[0:REST, FULL, :]).then_inc(out_sem[1], 16)
                sp.wait_ge(out_sem[0], 16 * PAIRS)
                sp.wait_ge(out_sem[1], 16 * (PAIRS + 1))


_INS = ['x', 'src', 'dst', 'edge_attr_64', 'edge_weight', 'edge_weight1',
        'L0_gnn_W_f', 'L0_gnn_b_f', 'L0_gnn_W_s', 'L0_gnn_b_s', 'L1_gnn_W1', 'L1_gnn_b1', 'L1_gnn_W2', 'L1_gnn_b2',
        'L2_gnn_W1l', 'L2_gnn_b1l', 'L2_gnn_W1r', 'L2_gnn_b1r', 'L2_gnn_att1', 'L2_gnn_bias1',
        'L2_gnn_W2l', 'L2_gnn_b2l', 'L2_gnn_W2r', 'L2_gnn_b2r', 'L2_gnn_att2', 'L2_gnn_bias2',
        'L2_gnn_Wfc', 'L2_gnn_bfc', 'L3_gnn_W', 'L3_gnn_b', 'L3_gnn_gamma', 'L3_gnn_beta']


def kernel(**inputs):
    import numpy as _np
    import concourse.bacc as _bacc
    from concourse import mybir as _mybir
    from concourse.bass_utils import run_bass_kernel_spmd as _run

    nc = _bacc.Bacc("TRN2", target_bir_lowering=False, num_devices=1)
    arrays, io = {}, {}
    for name in _INS:
        a = _np.ascontiguousarray(inputs[name])
        arrays[f"in_{name}_dram"] = a
        io[name] = nc.dram_tensor(f"in_{name}_dram", a.shape, _mybir.dt.from_np(a.dtype), kind="ExternalInput").ap()
    out = nc.dram_tensor("out_0_dram", (N, C), _mybir.dt.float32, kind="ExternalOutput").ap()
    build(nc, io, out)
    r = _run(nc, [arrays], core_ids=[0])
    return r.results[0]["out_0_dram"]
```

```python
from contextlib import ExitStack

import concourse.bass as bass
from concourse import mybir

F32 = mybir.dt.float32
BF16 = mybir.dt.bfloat16
I32 = mybir.dt.int32
ALU = mybir.AluOpType
ACT = mybir.ActivationFunctionType
AX = mybir.AxisListType
ds = bass.ds

P = 128
N = 50000
E = 50000
C = 64
H = 5
HC = H * C
TILES = 392
FULL = N // P
REST = N - FULL * P
BLK = 4
PAIRS = TILES // (2 * BLK)
WIN = 2
EXTRA = 200
RING = 4
CT = 98
GRP = 14
LN_EPS = 1e-5
BN_EPS = 1e-5
MW = C + H + 3
SCAN_T = 25
SCAN_G = 16
SCAN_W = SCAN_G * P
SP_ROWS = SCAN_T * H
SLOPE = 0.2
BIG = 1.0e30
CHUNKS = [(0, 128), (128, 128), (256, 64)]


class Phase(ExitStack):

    def __init__(self, nc):
        super().__init__()
        self.nc, self.sems = nc, []

    def sem(self, name):
        self.sems.append(self.nc.alloc_semaphore(name))
        return self.sems[-1]

    def __exit__(self, *exc):
        if self.sems and exc[0] is None:
            self.nc.clear_and_free_semaphores(self.sems)
            self.nc.all_engine_barrier()
        return super().__exit__(*exc)


def wide(ap, axis, n):
    ap = ap.unsqueeze(axis)
    shape = list(ap.shape)
    shape[axis] = n
    return ap.broadcast_to(shape)


def loop(eng, n, body):
    body(0, True)
    with eng.Fori(1, n) as i:
        body(i, False)


def need(eng, sem, count):
    if not (isinstance(count, int) and count <= 0):
        eng.wait_ge(sem, count)


class Chain:

    def __init__(self, eng, sem):
        self.eng, self.sem, self.n = eng, sem, 0

    def __call__(self, ins):
        self.n += 1
        ins.then_inc(self.sem, 1)
        self.eng.wait_ge(self.sem, self.n)


def build(nc, io, out):
    top = ExitStack()
    with top:
        def sb(name, shape, dt=F32, ctx=top):
            return ctx.enter_context(nc.sbuf_tensor(name, shape, dt))

        def dram(name, shape, dt=F32):
            return nc.dram_tensor(name, shape, dt, kind="Internal").ap()

        h_d = dram("h_d", (TILES * P, C))
        g_d = dram("g_d", (TILES * P, C))
        m_d = dram("m_d", (TILES * P, MW))
        hsT_d = dram("hsT_d", (2 * PAIRS, C, BLK * P))
        x_d = dram("x_d", (TILES * P, C))
        dst_d = dram("dst_d", (SCAN_T * SCAN_W + 2,), I32)

        acc = sb("acc", [P, (TILES + 1) * C])
        acc3 = acc[:, :].rearrange("p (b c) -> p b c", c=C)
        accw = sb("accw", [P, TILES + 1, H])
        deg_in = sb("deg_in", [P, TILES + 1, 1])
        deg_out = sb("deg_out", [P, TILES])
        dstf = sb("dstf", [P, TILES])
        rel = sb("rel", [P, TILES])
        src_i = sb("src_i", [P, TILES], I32)
        dst_i = sb("dst_i", [P, TILES], I32)
        gate = sb("gate", [P, TILES])
        lo_i = sb("lo_i", [1, TILES], I32)
        extra_i = sb("extra_i", [1, 2, EXTRA], I32)
        extra_n = sb("extra_n", [1, 4], I32)
        extra_lo = sb("extra_lo", [P, EXTRA])
        ident = sb("ident", [P, P])
        iota_n = sb("iota_n", [P, WIN * P])
        iota_b = sb("iota_b", [P, TILES])
        ones = sb("ones", [P, P])
        eps = sb("eps", [P, 1])

        w0 = sb("w0", [P, 2 * C])
        w0a = sb("w0a", [C + 1, 2 * C])
        w1 = sb("w1", [P, C])
        w1t = sb("w1t", [2, C])
        w1b = sb("w1b", [C + 1, C])
        wst = [sb(f"wst{g}", [P, HC]) for g in range(2)]
        wsum = [sb(f"wsum{g}", [P, HC]) for g in range(2)]
        wl = [sb(f"wl{g}", [C + 1, HC]) for g in range(2)]
        blr = [sb(f"blr{g}", [P, 2, 3]) for g in range(2)]
        bsum = [sb(f"bsum{g}", [P, 3]) for g in range(2)]
        attbd = [sb(f"attbd{g}", [P, 3, H]) for g in range(2)]
        lin = [sb(f"lin{g}", [P, 2, H]) for g in range(2)]
        lin_b = [sb(f"lin_b{g}", [P, H]) for g in range(2)]
        gbias = [sb(f"gbias{g}", [P, C]) for g in range(2)]
        wfc = sb("wfc", [C + 1, C])
        w3 = sb("w3", [C + 1, C])
        gamma = sb("gamma", [P, C])
        beta = sb("beta", [P, C])

        pe_turn = top.enter_context(nc.semaphore("pe_turn"))

        common = dict(locals())
        setup(nc, io, common)
        node_pass(nc, common, 0)
        edge_pass(nc, io, common, 0)
        extra_pass(nc, common, 0)
        node_pass(nc, common, 1)
        edge_pass(nc, io, common, 1)
        extra_pass(nc, common, 1)
        node_pass(nc, common, 2)
        for g in range(2):
            with Phase(nc) as ctx:
                al = ctx.enter_context(nc.sbuf_tensor(f"al{g}", [P, SCAN_T * SCAN_G, H], F32))
                als = ctx.enter_context(nc.sbuf_tensor(f"als{g}", [P, SCAN_T * SCAN_G, H], F32))
                common.update(al=al, als=als)
                attention_logits(nc, common, g)
                softmax_stats(nc, common, g)
                attention_messages(nc, common, g)
            extra_pass(nc, common, 2 + g)
            attention_nodes(nc, common, g)
        node_pass(nc, common, 3)
        edge_pass(nc, io, common, 3)
        extra_pass(nc, common, 4)
        finish(nc, common, out)


def setup(nc, io, S):
    acc, acc3, ident, ones, iota_n, iota_b = (S[k] for k in ("acc", "acc3", "ident", "ones", "iota_n", "iota_b"))
    dstf, rel, src_i, dst_i, gate = (S[k] for k in ("dstf", "rel", "src_i", "dst_i", "gate"))
    lo_i, extra_i, extra_n, extra_lo, eps, dst_d = (S[k] for k in ("lo_i", "extra_i", "extra_n", "extra_lo", "eps", "dst_d"))
    with Phase(nc) as ctx:
        def sb(name, shape, dt=F32):
            return ctx.enter_context(nc.sbuf_tensor(name, shape, dt))

        def sem(name):
            return ctx.sem((name))

        rows_i = sb("rows_i", [CT, 2, 4, P], I32)
        rows_f = sb("rows_f", [CT, 3, 4, P])
        guard = sb("guard", [1, 1280], I32)
        hi_i = sb("hi_i", [1, TILES], I32)
        lo, hi, more, upto, base = (sb(n, [1, TILES]) for n in ("lo", "hi", "more", "upto", "base"))
        diff_i = sb("diff_i", [1, TILES], I32)
        total_i = sb("total_i", [1, 1], I32)
        col = sb("col", [CT, 2, 4])
        wide_diff = sb("wide_diff", [CT, 4, P])
        step = sb("step", [P, EXTRA])
        passed = sb("passed", [CT, 4, EXTRA])
        a_of = sb("a_of", [P, EXTRA])
        clipped = sb("clipped", [P, TILES])
        square = sb("square", [P, TILES])
        turned = [ctx.enter_context(nc.psum_tensor(f"turned{k}", [P, TILES], F32)) for k in range(3)]
        ends = ctx.enter_context(nc.psum_tensor("ends", [1, TILES], F32))
        lo_all = ctx.enter_context(nc.psum_tensor("lo_all", [P, TILES], F32))
        turned_col = ctx.enter_context(nc.psum_tensor("turned_col", [P, 2, 4], F32))
        counted = ctx.enter_context(nc.psum_tensor("counted", [P, 2, EXTRA], F32))
        s_loaded, s_guard, s_weights, s_x = sem("s_loaded"), sem("s_guard"), sem("s_weights"), sem("s_x")
        s_blank, s_const, s_pool = sem("s_blank"), sem("s_const"), sem("s_pool")
        s_rows, s_turned, s_ends, s_need, s_v = sem("s_rows"), sem("s_turned"), sem("s_ends"), sem("s_need"), sem("s_v")
        s_sq, s_gate = sem("s_sq"), sem("s_gate")
        att_row = [sb(f"att_row{g}", [P, 3, HC]) for g in range(2)]
        weights = []
        w = io

        def put(dst, src):
            weights.append((dst, src))

        for t, name in enumerate(("L0_gnn_W_f", "L0_gnn_W_s")):
            cols = slice(t * C, (t + 1) * C)
            put(S["w0"][0:C, cols], w[name][C:2 * C, :])
            put(S["w0"][C:P, cols], w[name][0:C, :])
            put(S["w0a"][0:C, cols], w[name][2 * C:3 * C, :])
            put(S["w0a"][C:C + 1, cols], w[("L0_gnn_b_f", "L0_gnn_b_s")[t]].rearrange("(a c) -> a c", a=1))
        put(S["w1"][:, :], w["L1_gnn_W1"][0:2 * C, :])
        put(S["w1t"][0:1, :], w["L1_gnn_W1"][2 * C:2 * C + 1, :])
        put(S["w1t"][1:2, :], w["L1_gnn_b1"].rearrange("(a c) -> a c", a=1))
        put(S["w1b"][0:C, :], w["L1_gnn_W2"][:, :])
        put(S["w1b"][C:C + 1, :], w["L1_gnn_b2"].rearrange("(a c) -> a c", a=1))
        for g in range(2):
            n = f"{g + 1}"
            put(S["wst"][g][0:C, :], w[f"L2_gnn_W{n}l"][:, :])
            put(S["wst"][g][C:P, :], w[f"L2_gnn_W{n}r"][:, :])
            put(S["wsum"][g][C:P, :], w[f"L2_gnn_W{n}l"][:, :])
            put(S["wl"][g][0:C, :], w[f"L2_gnn_W{n}l"][:, :])
            put(S["wl"][g][C:C + 1, :], w[f"L2_gnn_b{n}l"].rearrange("(a c) -> a c", a=1))
            for s, side in enumerate("lr"):
                for q, (f0, fn) in enumerate(CHUNKS):
                    put(S["blr"][g][0:fn, s, q:q + 1],
                        w[f"L2_gnn_b{n}{side}"][f0:f0 + fn].rearrange("(c a) -> c a", a=1))
            for h in range(H):
                r = C * (h % 2)
                put(S["attbd"][g][r:r + C, h // 2, h:h + 1], w[f"L2_gnn_att{n}"][h, :].rearrange("(c a) -> c a", a=1))
            put(att_row[g][:, 0, :], w[f"L2_gnn_att{n}"].rearrange("h (a c) -> a (h c)", a=1).broadcast_to([P, HC]))
            for s, side in enumerate("lr"):
                put(att_row[g][:, 1 + s, :], w[f"L2_gnn_b{n}{side}"].rearrange("(a c) -> a c", a=1).broadcast_to([P, HC]))
            put(S["gbias"][g][:, :], w[f"L2_gnn_bias{n}"].rearrange("(a c) -> a c", a=1).broadcast_to([P, C]))
        put(S["wfc"][0:C, :], w["L2_gnn_Wfc"][:, :])
        put(S["wfc"][C:C + 1, :], w["L2_gnn_bfc"].rearrange("(a c) -> a c", a=1))
        put(S["w3"][0:C, :], w["L3_gnn_W"][:, :])
        put(S["w3"][C:C + 1, :], w["L3_gnn_b"].rearrange("(a c) -> a c", a=1))
        put(S["gamma"][:, :], w["L3_gnn_gamma"].rearrange("(a c) -> a c", a=1).broadcast_to([P, C]))
        put(S["beta"][:, :], w["L3_gnn_beta"].rearrange("(a c) -> a c", a=1).broadcast_to([P, C]))

        with nc.Block() as block:
            @block.sync
            def _(sp):
                sp.wait_ge(s_blank, 1)
                lists = [(rows_i[:, 0], io["src"]), (rows_i[:, 1], io["dst"]), (rows_f[:, 2], io["edge_weight"])]
                for dst, src in lists:
                    for c in range(4):
                        n = min(CT, FULL - c * CT)
                        sp.dma_start(dst[0:n, c, :], src[c * CT * P:(c * CT + n) * P].rearrange("(t e) -> t e", e=P)).then_inc(s_loaded, 16)
                    sp.dma_start(dst[FULL - 3 * CT:FULL - 3 * CT + 1, 3, 0:REST],
                                 src[FULL * P:E].rearrange("(t e) -> t e", t=1)).then_inc(s_loaded, 16)
                sp.wait_ge(s_blank, 2)
                for b0 in range(0, FULL, 39):
                    sp.dma_start(acc3[:, b0:b0 + 39, :], io["x"][b0 * P:(b0 + 39) * P, :].rearrange("(b p) c -> p b c", p=P)).then_inc(s_x, 16)
                sp.dma_start(acc3[0:REST, FULL, :], io["x"][FULL * P:N, :]).then_inc(s_x, 16)
                sp.wait_ge(s_blank, 3)
                sp.dma_start(dst_d[1:E + 1].rearrange("(a n) -> a n", a=16), io["dst"].rearrange("(a n) -> a n", a=16)).then_inc(s_guard, 16)
                sp.dma_start(dst_d[0:1].rearrange("(a n) -> a n", a=1), guard[0:1, 0:1]).then_inc(s_guard, 16)
                sp.dma_start(dst_d[E + 1:].rearrange("(a n) -> a n", a=1), guard[0:1, 0:SCAN_T * SCAN_W + 1 - E]).then_inc(s_guard, 16)
                sp.wait_ge(s_guard, 48)
                sp.wait_ge(s_x, 11 * 16)

            @block.scalar
            def _(act):
                act.wait_ge(s_blank, 4)
                for dst, src in weights:
                    act.dma_start(dst, src).then_inc(s_weights, 16)
                act.wait_ge(s_sq, 1)
                nc.scalar.activation(gate[:, :], square[:, :], ACT.Exp, scale=-1.0 / (2 * 3.0 ** 2)).then_inc(s_gate, 1)

            @block.gpsimd
            def _(pool):
                nc.gpsimd.iota(guard[:, :], pattern=[[1, 1280]], base=1 << 20, channel_multiplier=0).then_inc(s_pool, 1)
                nc.gpsimd.iota(iota_n[:, :], pattern=[[1, WIN * P]], base=0, channel_multiplier=0,
                               allow_small_or_imprecise_dtypes=True).then_inc(s_pool, 1)
                nc.gpsimd.iota(iota_b[:, :], pattern=[[1, TILES]], base=0, channel_multiplier=0,
                               allow_small_or_imprecise_dtypes=True).then_inc(s_pool, 1)
                nc.gpsimd.iota(step[:, :], pattern=[[1, EXTRA]], base=0, channel_multiplier=0,
                               allow_small_or_imprecise_dtypes=True).then_inc(s_pool, 1)
                nc.gpsimd.memset(ident[:, :], 0.0).then_inc(s_pool, 1)
                pool.wait_ge(s_pool, 5)
                nc.gpsimd.affine_select(out=ident[:, :], in_=ident[:, :], compare_op=ALU.not_equal, fill=1.0,
                                        base=0, pattern=[[-1, P]], channel_multiplier=1).then_inc(s_const, 1)

            @block.vector
            def _(dve):
                chain = Chain(dve, s_v)
                chain(nc.vector.memset(rows_i[:, 0], 0))
                chain(nc.vector.memset(rows_i[:, 1], 1 << 20))
                nc.vector.memset(rows_f[:, 2], 0.0).then_inc(s_blank, 1)
                nc.vector.memset(acc3[:, FULL:TILES + 1, :], 0.0).then_inc(s_blank, 1)
                dve.wait_ge(s_pool, 1)
                nc.vector.memset(eps[:, :], LN_EPS).then_inc(s_blank, 1)
                for g in range(2):
                    chain(nc.vector.memset(S["attbd"][g][:, :, :], 0.0))
                    chain(nc.vector.memset(S["blr"][g][:, :, :], 0.0))
                    chain(nc.vector.memset(S["lin"][g][0:C, 1, :], 0.0))
                nc.vector.memset(ones[:, :], 1.0).then_inc(s_blank, 1)
                dve.wait_ge(s_loaded, 15 * 16)
                nc.vector.tensor_copy(rows_f[:, 0:2].rearrange("t l c e -> t (l c e)"),
                                      rows_i[:, :].rearrange("t l c e -> t (l c e)")).then_inc(s_rows, 1)
                dve.wait_ge(s_turned, 1)
                chain(nc.vector.tensor_copy(src_i[:, :], turned[0][:, :]))
                chain(nc.vector.tensor_copy(dstf[:, :], turned[1][:, :]))
                chain(nc.vector.tensor_scalar(clipped[:, :], dstf[:, :], float(N - 1), None, ALU.min))
                chain(nc.vector.tensor_copy(dst_i[:, :], clipped[:, :]))
                chain(nc.vector.tensor_copy(square[:, :], turned[2][:, :]))
                chain(nc.vector.tensor_tensor(square[:, :], square[:, :], square[:, :], ALU.mult))
                dve.sem_inc(s_sq, 1)
                dve.sem_inc(s_need, 1)
                chain(nc.vector.tensor_copy(lo_i[:, :], clipped[0:1, :]))
                chain(nc.vector.tensor_single_scalar(lo_i[:, :], lo_i[:, :], 7, ALU.logical_shift_right))
                dve.wait_ge(s_ends, 1)
                chain(nc.vector.tensor_copy(hi_i[:, :], ends[:, :]))
                chain(nc.vector.tensor_single_scalar(hi_i[:, :], hi_i[:, :], 7, ALU.logical_shift_right))
                chain(nc.vector.tensor_copy(lo[:, :], lo_i[:, :]))
                chain(nc.vector.tensor_copy(hi[:, :], hi_i[:, :]))
                dve.sem_inc(s_need, 1)
                chain(nc.vector.tensor_tensor(hi[:, :], hi[:, :], lo[:, :], ALU.subtract))
                chain(nc.vector.tensor_copy(diff_i[:, :], hi[:, :]))
                chain(nc.vector.tensor_single_scalar(diff_i[:, :], diff_i[:, :], WIN.bit_length() - 1, ALU.logical_shift_right))
                chain(nc.vector.tensor_copy(more[:, :], diff_i[:, :]))
                chain(nc.vector.memset(hi[:, :], 1.0))
                chain(nc.vector.tensor_tensor_scan(upto[:, :], hi[:, :], more[:, :], 0.0, ALU.mult, ALU.add))
                chain(nc.vector.tensor_tensor(base[:, :], upto[:, :], more[:, :], ALU.subtract))
                chain(nc.vector.scalar_tensor_tensor(out=base[:, :], in0=base[:, :], scalar=-float(WIN), in1=lo[:, :],
                                                     op0=ALU.mult, op1=ALU.add))
                chain(nc.vector.memset(hi[:, :], 0.0))
                chain(nc.vector.tensor_tensor(hi[:, 0:TILES - 1], base[:, 1:TILES], base[:, 0:TILES - 1], ALU.subtract))
                chain(nc.vector.tensor_copy(total_i[:, :], upto[:, TILES - 1:TILES]))
                chain(nc.vector.tensor_scalar(more[:, 0:1], upto[:, TILES - 1:TILES], float(RING - 1), float(RING), ALU.add, ALU.max))
                chain(nc.vector.tensor_copy(total_i[:, :], more[:, 0:1]))
                chain(nc.vector.tensor_single_scalar(extra_n[:, 0:1], total_i[:, :], RING.bit_length() - 1, ALU.logical_shift_right))
                dve.sem_inc(s_need, 1)
                dve.wait_ge(s_ends, 2)
                chain(nc.vector.tensor_copy(col[:, :, :], turned_col[0:CT, :, :]))
                for c in range(4):
                    chain(nc.vector.tensor_scalar(passed[:, c, :], step[0:CT, :], col[:, 0, c:c + 1], None, ALU.is_ge))
                    chain(nc.vector.tensor_copy(wide_diff[:, c, :], col[:, 1, c:c + 1].broadcast_to([CT, P])))
                dve.sem_inc(s_need, 1)
                dve.wait_ge(s_ends, 3)
                chain(nc.vector.tensor_scalar(a_of[:, :], counted[:, 0, :], float(TILES - 1), None, ALU.min))
                chain(nc.vector.tensor_copy(extra_i[:, 0, :], a_of[0:1, :]))
                chain(nc.vector.tensor_scalar(step[:, :], step[:, :], 1.0, float(WIN), ALU.add, ALU.mult))
                chain(nc.vector.tensor_tensor(step[:, :], step[:, :], counted[:, 1, :], ALU.add))
                chain(nc.vector.tensor_copy(clipped[:, 0:1], lo_all[:, 0:1]))
                chain(nc.vector.tensor_scalar(step[:, :], step[:, :], clipped[:, 0:1], float(TILES - 1), ALU.add, ALU.min))
                chain(nc.vector.tensor_copy(extra_i[:, 1, :], step[0:1, :]))
                chain(nc.vector.tensor_scalar(extra_lo[:, :], step[:, :], float(P), None, ALU.mult))
                chain(nc.vector.scalar_tensor_tensor(out=rel[:, :], in0=lo_all[:, :], scalar=-float(P), in1=dstf[:, :],
                                                     op0=ALU.mult, op1=ALU.add))
                dve.wait_ge(s_weights, 16 * len(weights))
                for g in range(2):
                    chain(nc.vector.tensor_tensor(S["wsum"][g][C:P, :], S["wsum"][g][C:P, :], S["wst"][g][C:P, :], ALU.add))
                    chain(nc.vector.tensor_tensor(S["bsum"][g][:, :], S["blr"][g][:, 0, :], S["blr"][g][:, 1, :], ALU.add))
                    chain(nc.vector.tensor_scalar(S["bsum"][g][:, :], S["bsum"][g][:, :], 1.0 - SLOPE, None, ALU.mult))
                    chain(nc.vector.tensor_scalar(att_row[g][:, 0, :], att_row[g][:, 0, :], SLOPE, None, ALU.mult))
                    chain(nc.vector.tensor_tensor(att_row[g][:, 1, :], att_row[g][:, 1, :], att_row[g][:, 2, :], ALU.add))
                    for mat, to in ((S["wst"][g][:, :], S["lin"][g][:, 0, :]), (S["wsum"][g][C:P, :], S["lin"][g][C:P, 1, :]),
                                    (att_row[g][:, 1, :], S["lin_b"][g][:, :])):
                        p0 = P - mat.shape[0]
                        chain(nc.vector.tensor_tensor(att_row[g][p0:P, 2, :], mat, att_row[g][p0:P, 0, :], ALU.mult))
                        chain(nc.vector.tensor_reduce(to, att_row[g][p0:P, 2, :].rearrange("p (h c) -> p h c", h=H), AX.X, ALU.add))

            @block.tensor
            def _(pe):
                pe.wait_ge(s_const, 1)
                pe.wait_ge(s_rows, 1)
                for k in range(3):
                    for c in range(4):
                        last = nc.tensor.transpose(turned[k][:, c * CT:(c + 1) * CT], rows_f[:, k, c, :], ident[0:CT, 0:CT])
                last.then_inc(s_turned, 1)
                pe.wait_ge(s_blank, 4)
                pe.wait_ge(s_need, 1)
                nc.tensor.matmul(ends[:, :], ident[:, P - 1:P], clipped[:, :], start=True, stop=True).then_inc(s_ends, 1)
                pe.wait_ge(s_need, 2)
                nc.tensor.matmul(lo_all[:, :], ones[0:1, :], lo[:, :], start=True, stop=True)
                pe.wait_ge(s_need, 3)
                for c in range(4):
                    for n, row in enumerate((upto, hi)):
                        mm = nc.tensor.matmul(turned_col[0:CT, n, c:c + 1], row[0:1, c * CT:(c + 1) * CT], ones[0:1, 0:1], start=True, stop=True)
                mm.then_inc(s_ends, 1)
                pe.wait_ge(s_need, 4)
                for n, left in enumerate((None, wide_diff)):
                    for c in range(4):
                        mm = nc.tensor.matmul(counted[:, n, :], ones[0:CT, :] if left is None else left[:, c, :], passed[:, c, :],
                                              start=(c == 0), stop=(c == 3))
                mm.then_inc(s_ends, 1)


def node_pass(nc, S, layer):
    acc3, h_d, x_d, eps, deg_out = S["acc3"], S["h_d"], S["x_d"], S["eps"], S["deg_out"]
    groups = TILES // GRP
    with Phase(nc) as ctx:
        def sem(name):
            return ctx.sem((f"{name}{layer}"))

        def sb(name, shape):
            return [ctx.enter_context(nc.sbuf_tensor(f"{name}{layer}_{k}", shape, F32)) for k in range(2)]

        mean, var, rstd = sb("mean", [P, GRP]), sb("var", [P, GRP]), sb("rstd", [P, GRP])
        xc, sq, h, xs = (sb(n, [P, GRP, C]) for n in ("xc", "sq", "h", "xs"))
        dsc = ctx.enter_context(nc.sbuf_tensor(f"dsc{layer}", [P, TILES], F32))
        n_mean, n_cent, n_sq, n_var, n_std, n_norm, n_h, n_add, n_dg = (
            [sem(f"{n}_{k}_") for k in range(2)]
            for n in ("n_mean", "n_cent", "n_sq", "n_var", "n_std", "n_norm", "n_h", "n_add", "n_dg"))
        n_out = [sem(f"n_out_{k}_") for k in range(2)]
        n_rec = sem("n_rec")
        h_rows = h_d.rearrange("(g b p) c -> g p b c", p=P, b=GRP)
        x_rows = x_d.rearrange("(g b p) c -> g p b c", p=P, b=GRP)

        def bc(v):
            return wide(v, 2, C)

        with nc.Block() as block:
            @block.vector
            def _(dve):
                if layer == 3:
                    nc.vector.tensor_scalar(dsc[:, :], deg_out[:, :], 1.0, None, ALU.max).then_inc(n_rec, 1)
                    dve.wait_ge(n_rec, 2)
                    nc.vector.reciprocal(dsc[:, :], dsc[:, :]).then_inc(n_rec, 1)
                    dve.wait_ge(n_rec, 3)

                def body(j, first):
                    for k in range(2):
                        x = acc3[:, ds((2 * j + k) * GRP, GRP), :]
                        nc.vector.tensor_reduce(mean[k][:, :], x, AX.X, ALU.add).then_inc(n_mean[k], 1)
                    for k in range(2):
                        x = acc3[:, ds((2 * j + k) * GRP, GRP), :]
                        dve.wait_ge(n_mean[k], j * 2 + 1)
                        nc.vector.tensor_scalar(mean[k][:, :], mean[k][:, :], 1.0 / C, None, ALU.mult).then_inc(n_mean[k], 1)
                        dve.wait_ge(n_mean[k], j * 2 + 2)
                        if not first:
                            dve.wait_ge(n_h[k], j)
                        nc.vector.tensor_tensor(xc[k][:, :, :], x, bc(mean[k][:, :]), ALU.subtract).then_inc(n_cent[k], 1)
                    for k in range(2):
                        dve.wait_ge(n_sq[k], j + 1)
                        nc.vector.tensor_reduce(var[k][:, :], sq[k][:, :, :], AX.X, ALU.add).then_inc(n_var[k], 1)
                    for k in range(2):
                        dve.wait_ge(n_std[k], j + 1)
                        nc.vector.reciprocal(rstd[k][:, :], rstd[k][:, :]).then_inc(n_norm[k], 1)
                        dve.wait_ge(n_norm[k], j * 2 + 1)
                        nc.vector.tensor_tensor(xc[k][:, :, :], xc[k][:, :, :], bc(rstd[k][:, :]), ALU.mult).then_inc(n_norm[k], 1)
                    for k in range(2):
                        x = acc3[:, ds((2 * j + k) * GRP, GRP), :]
                        if layer == 0:
                            dve.wait_ge(n_h[k], j + 1)
                            nc.vector.tensor_tensor(x, x, h[k][:, :, :], ALU.add).then_inc(n_add[k], 1)
                        if layer == 3:
                            dve.wait_ge(n_h[k], j + 1)
                            if not first:
                                dve.wait_ge(n_out[k], 32 * j)
                            nc.vector.tensor_tensor(xs[k][:, :, :], x, h[k][:, :, :], ALU.add).then_inc(n_add[k], 1)
                            nc.vector.tensor_tensor(sq[k][:, :, :], h[k][:, :, :], bc(dsc[:, ds((2 * j + k) * GRP, GRP)]),
                                                    ALU.mult).then_inc(n_dg[k], 1)
                loop(dve, groups // 2, body)

            @block.scalar
            def _(act):
                if layer == 3:
                    act.wait_ge(n_rec, 1)
                    nc.scalar.activation(dsc[:, :], dsc[:, :], ACT.Sqrt).then_inc(n_rec, 1)

                def body(j, first):
                    for k in range(2):
                        act.wait_ge(n_cent[k], j + 1)
                        if layer == 3 and not first:
                            act.wait_ge(n_out[k], 32 * j)
                        nc.scalar.activation(sq[k][:, :, :], xc[k][:, :, :], ACT.Square).then_inc(n_sq[k], 1)
                    for k in range(2):
                        act.wait_ge(n_var[k], j + 1)
                        if not first:
                            act.wait_ge(n_norm[k], 2 * j)
                        nc.scalar.activation(rstd[k][:, :], var[k][:, :], ACT.Sqrt, bias=eps[:, 0:1], scale=1.0 / C).then_inc(n_std[k], 1)
                    for k in range(2):
                        act.wait_ge(n_norm[k], 2 * j + 2)
                        if not first:
                            act.wait_ge(n_out[k], (32 if layer in (2, 3) else 16) * j)
                            if layer in (0, 3):
                                act.wait_ge(n_add[k], j)
                            if layer == 3:
                                act.wait_ge(n_dg[k], j)
                        nc.scalar.activation(h[k][:, :, :], xc[k][:, :, :], ACT.Relu).then_inc(n_h[k], 1)
                loop(act, groups // 2, body)

            @block.sync
            def _(sp):
                def body(j, first):
                    for k in range(2):
                        g = 2 * j + k
                        if layer == 3:
                            sp.wait_ge(n_add[k], j + 1)
                            sp.dma_start(x_rows[ds(g, 1)].rearrange("g p b c -> (g p) b c"), xs[k][:, :, :]).then_inc(n_out[k], 16)
                            sp.wait_ge(n_dg[k], j + 1)
                            sp.dma_start(h_rows[ds(g, 1)].rearrange("g p b c -> (g p) b c"), sq[k][:, :, :]).then_inc(n_out[k], 16)
                        else:
                            sp.wait_ge(n_h[k], j + 1)
                            sp.dma_start(h_rows[ds(g, 1)].rearrange("g p b c -> (g p) b c"), h[k][:, :, :]).then_inc(n_out[k], 16)
                            if layer == 2:
                                sp.dma_start(x_rows[ds(g, 1)].rearrange("g p b c -> (g p) b c"), acc3[:, ds(g * GRP, GRP), :]).then_inc(n_out[k], 16)
                loop(sp, groups // 2, body)
                for k in range(2):
                    sp.wait_ge(n_out[k], (32 if layer in (2, 3) else 16) * (groups // 2))


def gather_front(nc, S, name, ctx, table, ends, release=1):
    idx = {e: [ctx.enter_context(nc.sbuf_tensor(f"idx_{e}_{name}_{k}", [P, BLK], I32)) for k in range(2)] for e in ends}
    z = [ctx.enter_context(nc.sbuf_tensor(f"z_{name}_{k}", [P, BLK, len(ends) * C], F32)) for k in range(2)]

    def sems(n):
        return [ctx.sem((f"{n}_{name}_{k}")) for k in range(2)]

    idx_in, gathered, z_used = sems("idx_in"), sems("gathered"), sems("z_used")
    turn = ctx.sem((f"turn_{name}"))

    def load_indices(sp, j, k, first):
        if not first:
            sp.wait_ge(gathered[k], 16 * BLK * len(ends) * j)
        for e in ends:
            sp.dma_start(idx[e][k][:, :], S[f"{e}_i"][:, ds((2 * j + k) * BLK, BLK)]).then_inc(idx_in[k], 16)

    def gather(pool, also=None):
        def body(j, first):
            for k in range(2):
                pool.wait_ge(idx_in[k], 16 * len(ends) * (j + 1))
                pool.sem_inc(turn)
                if not first:
                    pool.wait_ge(z_used[k], release * j)
                    pool.sem_inc(turn)
                    if also is not None:
                        pool.wait_ge(also, 2 * j + k - 1)
                        pool.sem_inc(turn)
                for t in range(BLK):
                    for n, e in enumerate(ends):
                        nc.gpsimd.indirect_dma_start(
                            out=z[k][:, t, n * C:(n + 1) * C], out_offset=None, in_=table[:, :],
                            in_offset=bass.IndirectOffsetOnAxis(ap=idx[e][k][:, t:t + 1], axis=0)).then_inc(gathered[k], 16)
        loop(pool, PAIRS, body)

    return z, gathered, z_used, load_indices, gather


def edge_pass(nc, io, S, layer):
    h_d, m_d, ident = S["h_d"], S["m_d"], S["ident"]
    ends = ("src",) if layer == 3 else ("src", "dst")
    width = {0: C + 1, 1: C, 3: C}[layer]
    m_rows = m_d.rearrange("(g b p) c -> g p b c", p=P, b=BLK)
    LASTB = (E - (2 * PAIRS - 1) * BLK * P)
    with Phase(nc) as ctx:
        name = f"e{layer}"
        z, gathered, z_used, load_indices, gather = gather_front(nc, S, name, ctx, h_d, ends, 16 if layer == 3 else 1)

        def sems(n):
            return [ctx.sem((f"{n}_{name}_{k}")) for k in range(2)]

        def sb(n, shape, dt=F32):
            return [ctx.enter_context(nc.sbuf_tensor(f"{n}_{name}_{k}", shape, dt)) for k in range(2)]

        def ps(n, shape):
            return [ctx.enter_context(nc.psum_tensor(f"{n}_{name}_{k}", shape, F32)) for k in range(2)]

        m_ready, m_out = sems("m_ready"), sems("m_out")
        s_clear = ctx.sem(f"s_clear_{name}")
        zT_ready, zT_used = sems("zT_ready"), sems("zT_used")
        if layer != 3:
            zTp, zT = ps("zTp", [P, BLK * P]), sb("zT", [P, BLK * P])
            m = sb("m", [P, BLK, width])
        sums = NodeSums(nc, S, ctx, name, width, S["deg_in"] if layer == 0 else None)
        if layer == 0:
            att, aT = sb("att", [P, BLK, C]), sb("aT", [C + 1, BLK * P])
            aTp = ctx.enter_context(nc.psum_tensor("aTp", [C, BLK * P], F32))
            pre = ps("pre", [P, BLK, 2 * C])
            ef, ab, ln = sb("ef", [P, BLK, C]), sb("ab", [P, BLK, C]), sb("ln", [P, BLK, C])
            lo = ctx.enter_context(nc.sbuf_tensor("src_lo", [P, TILES], I32))
            hi = ctx.enter_context(nc.sbuf_tensor("src_hi", [P, TILES], I32))
            lof = ctx.enter_context(nc.sbuf_tensor("src_lof", [P, TILES], F32))
            hif = ctx.enter_context(nc.sbuf_tensor("src_hif", [P, TILES], F32))
            real = ctx.enter_context(nc.sbuf_tensor("real", [P, TILES], F32))
            hot_lo, hot_hi = sb("hot_lo", [P, BLK, P], BF16), sb("hot_hi", [P, BLK, TILES], BF16)
            count = ctx.enter_context(nc.psum_tensor("count", [P, TILES], F32))
            hot, hot_used = sems("hot"), sems("hot_used")
            att_in, att_used, aT_ready = sems("att_in"), sems("att_used"), sems("aT_ready")
            pre_ready, act_step, act_done, dve_step = sems("pre_ready"), sems("act_step"), sems("act_done"), sems("dve_step")
            s_pre = ctx.sem(("s_pre"))
            s_ones = ctx.sem(("s_ones0"))
        if layer == 1:
            aux = sb("aux", [2, BLK * P])
            uTp, uT, mp = ps("uTp", [C, BLK * P]), sb("uT", [C + 1, BLK * P]), ps("mp", [P, BLK, C])
            aux_in, uTp_ready, uT_ready, mp_ready = sems("aux_in"), sems("uTp_ready"), sems("uT_ready"), sems("mp_ready")
            s_ones = ctx.sem(("s_ones1"))

        with nc.Block() as block:
            @block.gpsimd
            def _(pool):
                gather(pool, sums.summed if layer == 3 else None)

            @block.sync
            def _(sp):
                if layer in (0, 1):
                    sp.wait_ge(s_ones, 1)

                def load_edge_data(j, k, first, last=False):
                    blk = 2 * j + k
                    if layer == 0:
                        if not first:
                            sp.wait_ge(att_used[k], j)
                        if last:
                            full = LASTB // P
                            r0 = (2 * PAIRS - 1) * BLK * P
                            sp.dma_start(att[k][:, 0:full, :], io["edge_attr_64"][r0:r0 + full * P, :].rearrange("(b p) c -> p b c", p=P)).then_inc(att_in[k], 16)
                            sp.dma_start(att[k][0:LASTB - full * P, full, :], io["edge_attr_64"][r0 + full * P:E, :]).then_inc(att_in[k], 16)
                        else:
                            sp.dma_start(att[k][:, :, :], io["edge_attr_64"][ds(blk * BLK * P, BLK * P), :].rearrange("(b p) c -> p b c", p=P)).then_inc(att_in[k], 32)
                    if layer == 1:
                        if not first:
                            sp.wait_ge(uTp_ready[k], j)
                        ew = io["edge_weight1"].rearrange("n a -> a n")
                        if last:
                            sp.dma_start(aux[k][0:1, 0:LASTB], ew[:, (2 * PAIRS - 1) * BLK * P:E]).then_inc(aux_in[k], 16)
                        else:
                            sp.dma_start(aux[k][0:1, :], ew[:, ds(blk * BLK * P, BLK * P)]).then_inc(aux_in[k], 16)

                def store(j, k):
                    rows = m_rows[ds(2 * j + k, 1)].rearrange("g p b c -> (g p) b c")
                    if layer == 3:
                        sp.wait_ge(gathered[k], 16 * BLK * (j + 1))
                        sp.dma_start(rows[:, :, 0:C], z[k][:, :, :]).then_inc(z_used[k], 16)
                    else:
                        sp.wait_ge(m_ready[k], j + 1)
                        sp.dma_start(rows[:, :, 0:width], m[k][:, :, :]).then_inc(m_out[k], 16)

                def body(j, first, last=False):
                    for k in range(2):
                        load_indices(sp, j, k, first)
                        load_edge_data(j, k, first, last and k == 1)
                        if not first:
                            store(j - 1, k)
                body(0, True)
                with sp.Fori(1, PAIRS - 1) as j:
                    body(j, False)
                body(PAIRS - 1, False, True)
                for k in range(2):
                    store(PAIRS - 1, k)
                for k in range(2):
                    sp.wait_ge(z_used[k] if layer == 3 else m_out[k], 16 * PAIRS)

            if layer == 3:
                @block.tensor
                def _(pe):
                    def body(j, first):
                        for k in range(2):
                            pe.wait_ge(gathered[k], 16 * BLK * (j + 1))
                            sums.multiply(pe, 2 * j + k, k, z[k])
                    loop(pe, PAIRS, body)

                @block.vector
                def _(dve):
                    nc.vector.memset(S["acc"][:, :], 0.0).then_inc(s_clear, 1)
                    dve.wait_ge(s_clear, 1)

                    def body(j, first):
                        for k in range(2):
                            sums.hot(dve, 2 * j + k, k)
                            if not (first and k == 0):
                                sums.add(dve, 2 * j + k - 1)
                    loop(dve, PAIRS, body)
                    sums.add(dve, 2 * PAIRS - 1)
            else:
                @block.tensor
                def _(pe):
                    def body(j, first):
                        for k in range(2):
                            pe.wait_ge(gathered[k], 16 * BLK * len(ends) * (j + 1))
                            if not first:
                                pe.wait_ge(zT_ready[k], j)
                            for t in range(BLK):
                                tr = nc.tensor.transpose(zTp[k][:, t * P:(t + 1) * P], z[k][:, t, :], ident[:, :])
                            tr.then_inc(z_used[k], 1)
                            if layer == 0:
                                pe.wait_ge(att_in[k], 32 * (j + 1))
                                need(pe, aT_ready[1 - k], j + k)
                                pe.sem_inc(S["pe_turn"])
                                for t in range(BLK):
                                    tr = nc.tensor.transpose(aTp[:, t * P:(t + 1) * P], att[k][:, t, :], ident[:, :])
                                tr.then_inc(att_used[k], 1)
                                pe.wait_ge(hot[k], j + 1)
                                for t in range(BLK):
                                    edge = first and k == 0 and t == 0
                                    mm = nc.tensor.matmul(count[:, :], hot_lo[k][:, t, :], hot_hi[k][:, t, :],
                                                          start=edge, stop=False, skip_group_check=True)
                                mm.then_inc(hot_used[k], 1)
                            if not (first and k == 0):
                                pe.wait_ge(m_ready[1 - k], j + k)
                                sums.multiply(pe, 2 * j + k - 1, 1 - k, m[1 - k])
                            pe.wait_ge(zT_ready[k], j + 1)
                            if layer == 0:
                                pe.wait_ge(aT_ready[k], j + 1)
                                if not first:
                                    pe.wait_ge(act_done[k], j)
                                    pe.wait_ge(dve_step[k], 4 * j)
                                for t in range(BLK):
                                    e = slice(t * P, (t + 1) * P)
                                    nc.tensor.matmul(pre[k][:, t, :], zT[k][:, e], S["w0"][:, :], start=True, stop=False)
                                    mm = nc.tensor.matmul(pre[k][:, t, :], aT[k][:, e], S["w0a"][:, :], start=False, stop=True)
                                mm.then_inc(pre_ready[k], 1)
                            else:
                                pe.wait_ge(aux_in[k], 16 * (j + 1))
                                if not first:
                                    pe.wait_ge(uT_ready[k], j)
                                pe.sem_inc(S["pe_turn"])
                                nc.tensor.matmul(uTp[k][:, :], S["w1"][:, :], zT[k][:, :], start=True, stop=False)
                                nc.tensor.matmul(uTp[k][:, :], S["w1t"][:, :], aux[k][:, :], start=False, stop=True).then_inc(uTp_ready[k], 1)
                                pe.wait_ge(uT_ready[k], j + 1)
                                if not first:
                                    pe.wait_ge(m_ready[k], j)
                                for t in range(BLK):
                                    mm = nc.tensor.matmul(mp[k][:, t, :], uT[k][:, t * P:(t + 1) * P], S["w1b"][:, :], start=True, stop=True)
                                mm.then_inc(mp_ready[k], 1)
                    loop(pe, PAIRS, body)
                    pe.wait_ge(m_ready[1], PAIRS)
                    sums.multiply(pe, 2 * PAIRS - 1, 1, m[1])
                    if layer == 0:
                        pe.wait_ge(s_pre, 9)
                        nc.tensor.matmul(count[:, :], hot_lo[0][:, 0, :], hot_hi[0][:, 0, :], start=False, stop=True,
                                         skip_group_check=True).then_inc(s_pre, 1)

                @block.scalar
                def _(act):
                    def body(j, first):
                        for k in range(2):
                            act.wait_ge(z_used[k], j + 1)
                            if not first:
                                act.wait_ge(pre_ready[k] if layer == 0 else uTp_ready[k], j)
                            nc.scalar.copy(zT[k][:, :], zTp[k][:, :]).then_inc(zT_ready[k], 1)
                            if layer == 0:
                                act.wait_ge(pre_ready[k], j + 1)
                                if not first:
                                    act.wait_ge(dve_step[k], 4 * j)
                                    act.wait_ge(m_ready[k], j)
                                nc.scalar.activation(ef[k][:, :, :], pre[k][:, :, 0:C], ACT.Exp, scale=-1.0).then_inc(act_done[k], 1)
                                nc.scalar.activation(ab[k][:, :, :], pre[k][:, :, C:2 * C], ACT.Abs).then_inc(act_step[k], 1)
                                act.wait_ge(act_step[k], 3 * j + 1)
                                nc.scalar.activation(ab[k][:, :, :], ab[k][:, :, :], ACT.Exp, scale=-1.0).then_inc(act_step[k], 1)
                                act.wait_ge(act_step[k], 3 * j + 2)
                                nc.scalar.activation(ln[k][:, :, :], ab[k][:, :, :], ACT.Ln, bias=1.0).then_inc(act_step[k], 1)
                            else:
                                act.wait_ge(uTp_ready[k], j + 1)
                                if not first:
                                    act.wait_ge(mp_ready[k], j)
                                nc.scalar.activation(uT[k][0:C, :], uTp[k][:, :], ACT.Relu).then_inc(uT_ready[k], 1)
                    loop(act, PAIRS, body)

                @block.vector
                def _(dve):
                    if layer == 0:
                        nc.vector.memset(S["deg_in"][:, :, :], 0.0)
                        for k in range(2):
                            nc.vector.memset(att[k][:, :, :], 0.0).then_inc(s_pre, 1)
                            nc.vector.memset(aT[k][C:C + 1, :], 1.0)
                            nc.vector.memset(m[k][:, :, C:C + 1], 1.0)
                        nc.vector.memset(real[:, :], 0.0).then_inc(s_pre, 1)
                        dve.wait_ge(s_pre, 3)
                        dve.sem_inc(s_ones, 1)
                        nc.vector.tensor_single_scalar(lo[:, :], S["src_i"][:, :], P - 1, ALU.bitwise_and).then_inc(s_pre, 1)
                        nc.vector.tensor_single_scalar(hi[:, :], S["src_i"][:, :], 7, ALU.logical_shift_right).then_inc(s_pre, 1)
                        nc.vector.tensor_scalar(real[:, :], S["dstf"][:, :], float(1 << 20), float(-P), ALU.is_equal, ALU.mult).then_inc(s_pre, 1)
                        dve.wait_ge(s_pre, 6)
                        nc.vector.tensor_copy(hif[:, :], hi[:, :]).then_inc(s_pre, 1)
                        nc.vector.tensor_tensor(lof[:, :], lo[:, :], real[:, :], ALU.add).then_inc(s_pre, 1)
                        dve.wait_ge(s_pre, 8)
                    else:
                        for k in range(2):
                            nc.vector.memset(aux[k][:, :], 1.0)
                            ms = nc.vector.memset(uT[k][C:C + 1, :], 1.0)
                        ms.then_inc(s_ones, 1)

                    def body(j, first):
                        for k in range(2):
                            blk = 2 * j + k
                            sums.hot(dve, blk, k)
                            if layer == 0:
                                if not first:
                                    dve.wait_ge(hot_used[k], j)
                                nc.vector.tensor_tensor(hot_lo[k][:, :, :], wide(S["iota_n"][:, 0:P], 1, BLK),
                                                        wide(lof[:, ds(blk * BLK, BLK)], 2, P), ALU.is_equal)
                                nc.vector.tensor_tensor(hot_hi[k][:, :, :], wide(S["iota_b"][:, :], 1, BLK),
                                                        wide(hif[:, ds(blk * BLK, BLK)], 2, TILES), ALU.is_equal).then_inc(hot[k], 1)
                                dve.wait_ge(att_used[k], j + 1)
                                if not first:
                                    dve.wait_ge(pre_ready[k], j)
                                nc.vector.tensor_copy(aT[k][0:C, :], aTp[:, :]).then_inc(aT_ready[k], 1)
                                dve.wait_ge(act_done[k], j + 1)
                                nc.vector.tensor_scalar(ef[k][:, :, :], ef[k][:, :, :], 1.0, None, ALU.add).then_inc(dve_step[k], 1)
                                dve.wait_ge(dve_step[k], 4 * j + 1)
                                nc.vector.reciprocal(ef[k][:, :, :], ef[k][:, :, :]).then_inc(dve_step[k], 1)
                                dve.wait_ge(act_step[k], 3 * j + 3)
                                nc.vector.scalar_tensor_tensor(out=ln[k][:, :, :], in0=pre[k][:, :, C:2 * C], scalar=0.0, in1=ln[k][:, :, :],
                                                               op0=ALU.max, op1=ALU.add).then_inc(dve_step[k], 1)
                                dve.wait_ge(dve_step[k], 4 * j + 3)
                                nc.vector.tensor_tensor(ln[k][:, :, :], ln[k][:, :, :], ef[k][:, :, :], ALU.mult).then_inc(dve_step[k], 1)
                                dve.wait_ge(dve_step[k], 4 * j + 4)
                                if not first:
                                    dve.wait_ge(m_out[k], 16 * j)
                                need(dve, sums.summed, blk - 1)
                                nc.vector.tensor_tensor(m[k][:, :, 0:C], ln[k][:, :, :], wide(S["gate"][:, ds(blk * BLK, BLK)], 2, C),
                                                        ALU.mult).then_inc(m_ready[k], 1)
                            else:
                                dve.wait_ge(mp_ready[k], j + 1)
                                if not first:
                                    dve.wait_ge(m_out[k], 16 * j)
                                need(dve, sums.summed, blk - 1)
                                nc.vector.tensor_copy(m[k][:, :, :], mp[k][:, :, :]).then_inc(m_ready[k], 1)
                            if not (first and k == 0):
                                sums.add(dve, blk - 1)
                    loop(dve, PAIRS, body)
                    sums.add(dve, 2 * PAIRS - 1)
                    if layer == 0:
                        for k in range(2):
                            dve.wait_ge(hot_used[k], PAIRS)
                        nc.vector.memset(hot_lo[0][:, 0, :], 0.0).then_inc(s_pre, 1)
                        dve.wait_ge(s_pre, 10)
                        nc.vector.tensor_copy(S["deg_out"][:, :], count[:, :])


class NodeSums:

    def __init__(self, nc, S, ctx, name, width, more):
        self.nc, self.S, self.width, self.more = nc, S, width, more
        self.hots = [ctx.enter_context(nc.sbuf_tensor(f"hot_{name}_{k}", [P, BLK, WIN * P], F32)) for k in range(2)]
        self.parts = [ctx.enter_context(nc.psum_tensor(f"part_{name}_{k}", [P, 2, WIN, width], F32)) for k in range(2)]
        self.hot_ready, self.summed, self.added = (ctx.sem(f"{n}_{name}") for n in ("hot_ready", "summed", "added"))

    def hot(self, dve, n, k):
        need(dve, self.summed, n - 1)
        self.nc.vector.tensor_tensor(self.hots[k][:, :, :], wide(self.S["iota_n"][:, :], 1, BLK),
                                     wide(self.S["rel"][:, ds(n * BLK, BLK)], 2, WIN * P), ALU.is_equal).then_inc(self.hot_ready, 1)

    def multiply(self, pe, n, k, m):
        need(pe, self.hot_ready, n + 1)
        need(pe, self.added, n * BLK)
        pe.sem_inc(self.S["pe_turn"])
        for t in range(BLK):
            for w in range(WIN):
                mm = self.nc.tensor.matmul(self.parts[t // 2][:, t % 2, w, :], self.hots[k][:, t, w * P:(w + 1) * P], m[:, t, :],
                                           start=True, stop=True)
        mm.then_inc(self.summed, 1)

    def add(self, dve, n):
        los = self.nc.values_load_multi_w_load_instructions(self.S["lo_i"][0:1, ds(n * BLK, BLK)], engines=(dve.engine,),
                                                            min_val=0, max_val=TILES - 1)[1]
        dve.wait_ge(self.summed, n + 1)
        for t in range(BLK):
            need(dve, self.added, n * BLK + t)
            part = self.parts[t // 2]
            x = self.S["acc3"][:, ds(los[t], WIN), :]
            ins = self.nc.vector.tensor_tensor(x, x, part[:, t % 2, :, 0:C], ALU.add)
            if self.more is not None:
                y = self.more[:, ds(los[t], WIN), :]
                ins = self.nc.vector.tensor_tensor(y, y, part[:, t % 2, :, C:self.width], ALU.add)
            ins.then_inc(self.added, 1)


def extra_pass(nc, S, which):
    acc3, m_d = S["acc3"], S["m_d"]
    more = {0: S["deg_in"], 2: S["accw"], 3: S["accw"]}.get(which)
    width = {0: C + 1, 1: C, 2: C + H, 3: C + H, 4: C}[which]
    with Phase(nc) as ctx:
        name = f"r{which}"
        m = [ctx.enter_context(nc.sbuf_tensor(f"m_{name}_{k}", [P, width], F32)) for k in range(RING)]
        at = [ctx.enter_context(nc.sbuf_tensor(f"at_{name}_{k}", [P, 1], F32)) for k in range(RING)]
        hot = [ctx.enter_context(nc.sbuf_tensor(f"hot_{name}_{k}", [P, WIN * P], F32)) for k in range(RING)]
        part = [ctx.enter_context(nc.psum_tensor(f"part_{name}_{k}", [P, WIN, width], F32)) for k in range(RING)]
        m_in, at_ready, hot_ready, summed, added = (
            [ctx.sem(f"{n}_{name}_{k}") for k in range(RING)] for n in ("m_in", "at_ready", "hot_ready", "summed", "added"))
        m_rows = m_d.rearrange("(a p) c -> a p c", p=P)

        def all_turns(eng, body):
            n = eng.value_load(S["extra_n"][0:1, 0:1], min_val=1, max_val=EXTRA // RING)
            with eng.Fori(1, n + 1) as i:
                body(i)

        def load(eng, row, i):
            return nc.values_load_multi_w_load_instructions(S["extra_i"][0:1, row, ds(i * RING - RING, RING)], engines=(eng.engine,),
                                                            min_val=0, max_val=TILES - 1)[1]

        with nc.Block() as block:
            @block.sync
            def _(sp):
                for k in range(RING):
                    sp.sem_inc(summed[k], 1)

                def body(i):
                    a = load(sp, 0, i)
                    for k in range(RING):
                        sp.wait_ge(summed[k], i)
                        sp.dma_start(m[k][:, :], m_rows[ds(a[k], 1), :, 0:width].rearrange("a p c -> (a p) c")).then_inc(m_in[k], 16)
                all_turns(sp, body)

            @block.tensor
            def _(pe):
                def body(i):
                    for k in range(RING):
                        pe.wait_ge(hot_ready[k], i)
                        pe.wait_ge(m_in[k], 16 * i)
                        pe.wait_ge(added[k], i)
                        for w in range(WIN):
                            mm = nc.tensor.matmul(part[k][:, w, :], hot[k][:, w * P:(w + 1) * P], m[k][:, :], start=True, stop=True)
                        mm.then_inc(summed[k], 1)
                all_turns(pe, body)

            @block.vector
            def _(dve):
                for k in range(RING):
                    dve.sem_inc(added[k], 1)

                def body(i):
                    a, b = load(dve, 0, i), load(dve, 1, i)
                    for k in range(RING):
                        nc.vector.tensor_tensor(at[k][:, :], S["dstf"][:, ds(a[k], 1)], S["extra_lo"][:, ds(i * RING - RING + k, 1)],
                                                ALU.subtract).then_inc(at_ready[k], 1)
                    for k in range(RING):
                        dve.wait_ge(at_ready[k], i)
                        nc.vector.tensor_scalar(hot[k][:, :], S["iota_n"][:, :], at[k][:, 0:1], None, ALU.is_equal).then_inc(hot_ready[k], 1)
                    for k in range(RING):
                        dve.wait_ge(summed[k], i + 1)
                        if k > 0:
                            dve.wait_ge(added[k - 1], i + 1)
                        x = acc3[:, ds(b[k], WIN), :]
                        ins = nc.vector.tensor_tensor(x, x, part[k][:, :, 0:C], ALU.add)
                        if more is not None:
                            y = more[:, ds(b[k], WIN), :]
                            ins = nc.vector.tensor_tensor(y, y, part[k][:, :, C:width], ALU.add)
                        ins.then_inc(added[k], 1)
                    dve.wait_ge(added[RING - 1], i + 1)
                all_turns(dve, body)


def attention_logits(nc, S, g):
    table = S["h_d"] if g == 0 else S["g_d"]
    al, als, ident = S["al"], S["als"], S["ident"]
    with Phase(nc) as ctx:
        name = f"l{g}"
        z, gathered, z_used, load_indices, gather = gather_front(nc, S, name, ctx, table, ("src", "dst"))

        def sems(n):
            return [ctx.sem((f"{n}_{name}_{k}")) for k in range(2)]

        def sb(n, shape):
            return [ctx.enter_context(nc.sbuf_tensor(f"{n}_{name}_{k}", shape, F32)) for k in range(2)]

        zTp = [ctx.enter_context(nc.psum_tensor(f"zTp_{name}_{k}", [P, BLK * P], F32)) for k in range(2)]
        alp = [ctx.enter_context(nc.psum_tensor(f"alp_{name}_{k}", [P, BLK, 2, H], F32)) for k in range(2)]
        tp = [ctx.enter_context(nc.psum_tensor(f"tp_{name}_{q}", [P, BLK * P], F32)) for q in range(3)]
        leak = [ctx.enter_context(nc.sbuf_tensor(f"leak_{name}_{q}", [P, BLK * P], F32)) for q in range(6)]
        zT = sb("zT", [P, BLK * P])
        zT_ready, hs_out, alp_ready, al_ready = sems("zT_ready"), sems("hs_out"), sems("alp_ready"), sems("al_ready")
        t_ready = ctx.sem((f"t_ready_{name}"))
        leak_ready = ctx.sem((f"leak_ready_{name}"))
        s_pad = ctx.sem((f"s_pad_{name}"))

        with nc.Block() as block:
            @block.gpsimd
            def _(pool):
                gather(pool)

            @block.sync
            def _(sp):
                def store(j, k):
                    sp.wait_ge(zT_ready[k], j + 1)
                    sp.dma_start(S["hsT_d"][ds(2 * j + k, 1)].rearrange("g c e -> (g c) e"), zT[k][0:C, :]).then_inc(hs_out[k], 16)

                def body(j, first):
                    for k in range(2):
                        load_indices(sp, j, k, first)
                        if not first:
                            store(j - 1, k)
                loop(sp, PAIRS, body)
                for k in range(2):
                    store(PAIRS - 1, k)
                for k in range(2):
                    sp.wait_ge(hs_out[k], 16 * PAIRS)

            @block.tensor
            def _(pe):
                def body(j, first):
                    for k in range(2):
                        pe.wait_ge(gathered[k], 32 * BLK * (j + 1))
                        if not first:
                            pe.wait_ge(zT_ready[k], j)
                        for t in range(BLK):
                            tr = nc.tensor.transpose(zTp[k][:, t * P:(t + 1) * P], z[k][:, t, :], ident[:, :])
                        tr.then_inc(z_used[k], 1)
                        pe.wait_ge(zT_ready[k], j + 1)
                        for q in range(6):
                            f0, fn = CHUNKS[q % 3]
                            if not (first and k == 0 and q < 3):
                                pe.wait_ge(leak_ready, 12 * j + 6 * k + q - 2)
                            pe.sem_inc(S["pe_turn"])
                            if q < 3:
                                mm = nc.tensor.matmul(tp[q][0:fn, :], S["wst"][g][:, f0:f0 + fn], zT[k][:, :], start=True, stop=True)
                            else:
                                mm = nc.tensor.matmul(tp[q - 3][0:fn, :], S["wsum"][g][C:P, f0:f0 + fn], zT[k][C:P, :], start=True, stop=True)
                            mm.then_inc(t_ready, 1)
                        pe.wait_ge(leak_ready, 12 * j + 6 * k + 6)
                        if not first:
                            pe.wait_ge(al_ready[k], j)
                        for t in range(BLK):
                            e = slice(t * P, (t + 1) * P)
                            for q in range(6):
                                fn = CHUNKS[q % 3][1]
                                if q == 0:
                                    nc.tensor.matmul(alp[k][:, t, 0, :], zT[k][:, e], S["lin"][g][:, 0, :], start=True, stop=False)
                                if q == 3:
                                    nc.tensor.matmul(alp[k][:, t, 1, :], zT[k][:, e], S["lin"][g][:, 1, :], start=True, stop=False)
                                mm = nc.tensor.matmul(alp[k][:, t, q // 3, :], leak[q][0:fn, e],
                                                      S["attbd"][g][0:fn, q % 3, :], start=False, stop=(q % 3 == 2))
                        mm.then_inc(alp_ready[k], 1)
                loop(pe, PAIRS, body)

            @block.scalar
            def _(act):
                def body(j, first):
                    for k in range(2):
                        act.wait_ge(z_used[k], j + 1)
                        if not first:
                            act.wait_ge(hs_out[k], 16 * j)
                            act.wait_ge(alp_ready[k], j)
                        nc.scalar.copy(zT[k][:, :], zTp[k][:, :]).then_inc(zT_ready[k], 1)
                        if not (first and k == 0):
                            act.wait_ge(alp_ready[1 - k], j + k)
                        for q in range(6):
                            fn = CHUNKS[q % 3][1]
                            act.wait_ge(t_ready, 12 * j + 6 * k + q + 1)
                            nc.scalar.activation(leak[q][0:fn, :], tp[q % 3][0:fn, :], ACT.Relu, bias=S["bsum"][g][0:fn, q % 3:q % 3 + 1],
                                                 scale=1.0 - SLOPE).then_inc(leak_ready, 1)
                loop(act, PAIRS, body)

            @block.vector
            def _(dve):
                nc.vector.memset(al[:, TILES:, :], 0.0).then_inc(s_pad, 1)
                nc.vector.memset(als[:, TILES:, :], 0.0).then_inc(s_pad, 1)

                def body(j, first):
                    for k in range(2):
                        dve.wait_ge(alp_ready[k], j + 1)
                        rows = ds((2 * j + k) * BLK, BLK)
                        nc.vector.tensor_tensor(al[:, rows, :], alp[k][:, :, 0, :], wide(S["lin_b"][g][:, :], 1, BLK), ALU.add)
                        nc.vector.tensor_tensor(als[:, rows, :], alp[k][:, :, 1, :], wide(S["lin_b"][g][:, :], 1, BLK), ALU.add).then_inc(al_ready[k], 1)
                loop(dve, PAIRS, body)


def softmax_stats(nc, S, g):
    acc, al, als, ident, ones, dst_d = S["acc"], S["al"], S["als"], S["ident"], S["ones"], S["dst_d"]
    R, W, T, G = SP_ROWS, SCAN_W, SCAN_T, SCAN_G
    with Phase(nc) as ctx:
        name = f"s{g}"
        views = [acc[0:R, k * W:(k + 1) * W] for k in range(12)]
        lg, ls, prev, nxt, fwd, bwd, pen_f, pen_b, mx, own, tot, gap = views
        dst_own, dst_prev, dst_next = own.bitcast(I32), prev.bitcast(I32), nxt.bitcast(I32)

        def sb(n, shape):
            return ctx.enter_context(nc.sbuf_tensor(f"{n}_{name}", shape, F32))

        flag = sb("flag", [R, 2])
        carry = sb("carry", [R, 2])
        row = sb("row", [1, 4, R])
        packed = sb("packed", [P, 8, 4, R])
        pt = [ctx.enter_context(nc.psum_tensor(f"pt_{name}_{k}", [P, 4, P], F32)) for k in range(4)]
        prow = ctx.enter_context(nc.psum_tensor(f"prow_{name}", [1, 4, P], F32))
        pcol = ctx.enter_context(nc.psum_tensor(f"pcol_{name}", [P, 2], F32))
        s_in, s_v, s_t, s_p, s_q = (ctx.sem((f"{n}_{name}")) for n in ("s_in", "s_v", "s_t", "s_p", "s_q"))
        s_c, s_w = (ctx.sem((f"{n}_{name}")) for n in ("s_c", "s_w"))
        s_k = ctx.sem((f"s_k_{name}"))
        s_e, s_a = (ctx.sem((f"{n}_{name}")) for n in ("s_e", "s_a"))

        def by_chunk(x, gi):
            return x[:, :, :].rearrange("p (t g) h -> p g h t", g=G)[:, gi]

        with nc.Block() as block:
            @block.sync
            def _(sp):
                for off, dst in ((1, dst_own), (0, dst_prev), (2, dst_next)):
                    for h in range(H):
                        sp.dma_start(dst[h * T:(h + 1) * T, :], dst_d[off:off + T * W].rearrange("(t e) -> t e", e=W)).then_inc(s_in, 16)

            @block.tensor
            def _(pe):
                for x in range(2):
                    for q in range(4):
                        n = 4 * x + q
                        pe.wait_ge(s_k, n + 1)
                        if n >= 4:
                            pe.wait_ge(s_c, n - 3)
                        for r in range(4):
                            tr = nc.tensor.transpose(pt[n % 4][0:R, r, :], packed[:, n, r, :], ident[:, :])
                        tr.then_inc(s_t, 1)
                for turn in range(2):
                    pe.wait_ge(s_p, 2 * turn + 1)
                    for n in range(2):
                        nc.tensor.transpose(prow[0:1, n, 0:R], carry[:, n:n + 1], ident[0:R, 0:R])
                        tr = nc.tensor.transpose(prow[0:1, 2 + n, 0:R], flag[:, n:n + 1], ident[0:R, 0:R])
                    tr.then_inc(s_q, 1)
                    pe.wait_ge(s_p, 2 * turn + 2)
                    for n in range(2):
                        mm = nc.tensor.matmul(pcol[0:R, n:n + 1], row[0:1, n, :], ones[0:1, 0:1], start=True, stop=True)
                    mm.then_inc(s_q, 1)
                pe.wait_ge(s_w, 1)
                for x in range(2):
                    for q in range(4):
                        n = 8 + 4 * x + q
                        pe.wait_ge(s_c, n - 3)
                        for r in range(4):
                            gi = 4 * q + r
                            tr = nc.tensor.transpose(pt[n % 4][:, r, 0:R], (lg, ls)[x][:, gi * P:(gi + 1) * P], ident[0:R, 0:R])
                        tr.then_inc(s_t, 1)

            @block.scalar
            def _(act):
                act.wait_ge(s_e, 1)
                nc.scalar.activation(lg, lg, ACT.Exp).then_inc(s_a, 1)
                nc.scalar.activation(ls, ls, ACT.Exp).then_inc(s_a, 1)

            @block.vector
            def _(dve):
                chain = Chain(dve, s_v)
                tt, ts, scan = nc.vector.tensor_tensor, nc.vector.tensor_scalar, nc.vector.tensor_tensor_scan
                for n in range(8):
                    for r in range(4):
                        pk = nc.vector.tensor_copy(packed[:, n, r, :].rearrange("p (h t) -> p h t", t=T), by_chunk((al, als)[n // 4], 4 * (n % 4) + r))
                    pk.then_inc(s_k, 1)
                dve.wait_ge(s_in, 15 * 16)
                chain(nc.vector.tensor_copy(tot, dst_own))
                chain(nc.vector.tensor_copy(fwd, dst_prev))
                chain(nc.vector.tensor_copy(bwd, dst_next))
                chain(tt(prev, fwd, tot, ALU.is_equal))
                chain(tt(nxt, bwd, tot, ALU.is_equal))
                chain(ts(pen_f, prev, 1.0, BIG, ALU.subtract, ALU.mult))
                chain(ts(pen_b, nxt, 1.0, BIG, ALU.subtract, ALU.mult))
                for n in range(8):
                    dve.wait_ge(s_t, n + 1)
                    dst = (lg, ls)[n // 4][:, (n % 4) * 4 * P:(n % 4 + 1) * 4 * P]
                    nc.vector.tensor_copy(dst.rearrange("p (r e) -> p r e", r=4), pt[n % 4][0:R, :, :]).then_inc(s_c, 1)
                dve.wait_ge(s_c, 8)

                def both_ways(data, gain_f, gain_b, op0, op1, start, turn):
                    rev = slice(None, None, -1)
                    chain(nc.vector.tensor_reduce(flag[:, 0:1], gain_f, AX.X, ALU.min))
                    chain(nc.vector.tensor_reduce(flag[:, 1:2], gain_b, AX.X, ALU.min))
                    chain(scan(fwd, gain_f, data, start, op0, op1))
                    chain(scan(bwd[:, rev], gain_b[:, rev], data[:, rev], start, op0, op1))
                    chain(nc.vector.tensor_copy(carry[:, 0:1], fwd[:, W - 1:W]))
                    chain(nc.vector.tensor_copy(carry[:, 1:2], bwd[:, 0:1]))
                    dve.sem_inc(s_p, 1)
                    dve.wait_ge(s_q, 2 * turn + 1)
                    chain(nc.vector.tensor_copy(row[0:1, :, :], prow[0:1, :, 0:R]))
                    ends = row[0:1, 0:4, :].rearrange("a n (h t) -> a n h t", t=T)
                    chain(nc.vector.memset(ends[:, 2, :, 0:1], start))
                    chain(nc.vector.memset(ends[:, 3, :, T - 1:T], start))
                    out_f, out_b = tot[0:1, 0:R], tot[0:1, R:2 * R]
                    chain(scan(out_f, row[0:1, 2, :], row[0:1, 0, :], start, op0, op1))
                    chain(scan(out_b[:, rev], row[0:1, 3, rev], row[0:1, 1, rev], start, op0, op1))
                    chain(nc.vector.tensor_copy(row[0:1, 0, 1:R], out_f[:, 0:R - 1]))
                    chain(nc.vector.tensor_copy(row[0:1, 1, 0:R - 1], out_b[:, 1:R]))
                    chain(nc.vector.memset(ends[:, 0, :, 0:1], start))
                    chain(nc.vector.memset(ends[:, 1, :, T - 1:T], start))
                    dve.sem_inc(s_p, 1)
                    dve.wait_ge(s_q, 2 * turn + 2)
                    chain(nc.vector.tensor_copy(carry[:, :], pcol[0:R, :]))
                    chain(scan(fwd, gain_f, data, carry[:, 0:1], op0, op1))
                    chain(scan(bwd[:, rev], gain_b[:, rev], data[:, rev], carry[:, 1:2], op0, op1))

                both_ways(lg, pen_f, pen_b, ALU.add, ALU.max, -BIG, 0)
                chain(tt(mx, fwd, bwd, ALU.max))
                chain(tt(mx, mx, ls, ALU.max))
                chain(tt(lg, lg, mx, ALU.subtract))
                chain(tt(ls, ls, mx, ALU.subtract))
                dve.sem_inc(s_e, 1)
                dve.wait_ge(s_a, 2)
                both_ways(lg, prev, nxt, ALU.mult, ALU.add, 0.0, 1)
                chain(tt(tot, bwd, lg, ALU.subtract))
                chain(tt(tot, tot, fwd, ALU.add))
                chain(tt(tot, tot, ls, ALU.add))
                chain(nc.vector.reciprocal(tot, tot))
                chain(ts(tot, tot, 1.0 / H, None, ALU.mult))
                chain(tt(lg, lg, tot, ALU.mult))
                chain(tt(ls, ls, tot, ALU.mult))
                chain(ts(own, prev, -1.0, 1.0, ALU.mult, ALU.add))
                chain(tt(ls, ls, own, ALU.mult))
                dve.sem_inc(s_w, 1)
                for n in range(8, 16):
                    dve.wait_ge(s_t, n + 1)
                    x, q = (al, als)[(n - 8) // 4], n % 4
                    for r in range(4):
                        cp = nc.vector.tensor_copy(by_chunk(x, 4 * q + r), pt[n % 4][:, r, 0:R].rearrange("p (h t) -> p h t", t=T))
                    cp.then_inc(s_c, 1)


def attention_messages(nc, S, g):
    al, als, m_d = S["al"], S["als"], S["m_d"]
    m_rows = m_d.rearrange("(g b p) c -> g p b c", p=P, b=BLK)
    with Phase(nc) as ctx:
        name = f"m{g}"

        def sems(n):
            return [ctx.sem((f"{n}_{name}_{k}")) for k in range(2)]

        def sb(n, shape):
            return [ctx.enter_context(nc.sbuf_tensor(f"{n}_{name}_{k}", shape, F32)) for k in range(2)]

        hs, m = sb("hs", [C + 1, BLK * P]), sb("m", [P, BLK, C + H])
        prod = [sb(f"prod{t}", [P, HC]) for t in range(BLK)]
        xl = [ctx.enter_context(nc.psum_tensor(f"xl_{name}_{t}", [P, HC], F32)) for t in range(BLK)]
        sums = NodeSums(nc, S, ctx, name, C + H, S["accw"])
        s_clear = ctx.sem(f"s_clear_{name}")
        hs_in, xl_ready, weighted, m_ready, m_out = sems("hs_in"), sems("xl_ready"), sems("weighted"), sems("m_ready"), sems("m_out")
        s_ones = ctx.sem((f"s_ones_{name}"))
        with nc.Block() as block:
            @block.sync
            def _(sp):
                def store(j, k):
                    sp.wait_ge(m_ready[k], j + 1)
                    sp.dma_start(m_rows[ds(2 * j + k, 1), :, :, 0:C + H].rearrange("g p b c -> (g p) b c"), m[k][:, :, :]).then_inc(m_out[k], 16)

                def body(j, first):
                    for k in range(2):
                        if not first:
                            sp.wait_ge(xl_ready[k], BLK * j)
                        sp.dma_start(hs[k][0:C, :], S["hsT_d"][ds(2 * j + k, 1)].rearrange("g c e -> (g c) e")).then_inc(hs_in[k], 16)
                        if not first:
                            store(j - 1, k)
                loop(sp, PAIRS, body)
                for k in range(2):
                    store(PAIRS - 1, k)
                for k in range(2):
                    sp.wait_ge(m_out[k], 16 * PAIRS)

            @block.tensor
            def _(pe):
                pe.wait_ge(s_ones, 1)

                def body(j, first):
                    for k in range(2):
                        pe.wait_ge(hs_in[k], 16 * (j + 1))
                        for t in range(BLK):
                            need(pe, weighted[1 - k], BLK * (j + k - 1) + t + 1 if not (first and k == 0) else 0)
                            nc.tensor.matmul(xl[t][:, :], hs[k][:, t * P:(t + 1) * P], S["wl"][g][:, :], start=True, stop=True).then_inc(xl_ready[k], 1)
                        if not (first and k == 0):
                            pe.wait_ge(m_ready[1 - k], j + k)
                            sums.multiply(pe, 2 * j + k - 1, 1 - k, m[1 - k])
                loop(pe, PAIRS, body)
                pe.wait_ge(m_ready[1], PAIRS)
                sums.multiply(pe, 2 * PAIRS - 1, 1, m[1])

            @block.vector
            def _(dve):
                for k in range(2):
                    ms = nc.vector.memset(hs[k][C:C + 1, :], 1.0)
                ms.then_inc(s_ones, 1)

                def body(j, first):
                    for k in range(2):
                        tiles = (2 * j + k) * BLK
                        sums.hot(dve, 2 * j + k, k)
                        for t in range(BLK):
                            dve.wait_ge(xl_ready[k], BLK * j + t + 1)
                            nc.vector.tensor_tensor(prod[t][k][:, :].rearrange("p (h c) -> p h c", h=H), xl[t][:, :].rearrange("p (h c) -> p h c", h=H),
                                                    wide(al[:, ds(tiles + t, 1), :].rearrange("p t h -> p (t h)"), 2, C),
                                                    ALU.mult).then_inc(weighted[k], 1)
                        if not first:
                            dve.wait_ge(m_out[k], 16 * j)
                        need(dve, sums.summed, 2 * j + k - 1)
                        nc.vector.tensor_scalar(m[k][:, :, C:C + H], als[:, ds(tiles, BLK), :], 1.0, None, ALU.mult)
                        for t in range(BLK):
                            dve.wait_ge(weighted[k], BLK * j + t + 1)
                            red = nc.vector.tensor_reduce(m[k][:, t, 0:C], prod[t][k][:, :].rearrange("p (h c) -> p c h", h=H), AX.X, ALU.add)
                        red.then_inc(m_ready[k], 1)
                        if first and k == 0:
                            dve.wait_ge(s_clear, 2)
                        else:
                            sums.add(dve, 2 * j + k - 1)
                loop(dve, PAIRS, body)
                sums.add(dve, 2 * PAIRS - 1)

            @block.gpsimd
            def _(pool):
                nc.gpsimd.memset(S["acc"][:, :], 0.0).then_inc(s_clear, 1)
                nc.gpsimd.memset(S["accw"][:, :, :], 0.0).then_inc(s_clear, 1)


def attention_nodes(nc, S, g):
    acc3, accw, deg_in, ident = S["acc3"], S["accw"], S["deg_in"], S["ident"]
    table = S["h_d"] if g == 0 else S["g_d"]
    rows_in = table.rearrange("(g b p) c -> g p b c", p=P, b=BLK)
    x_rows = S["x_d"].rearrange("(g b p) c -> g p b c", p=P, b=BLK)
    g_rows = S["g_d"].rearrange("(g b p) c -> g p b c", p=P, b=BLK)
    with Phase(nc) as ctx:
        name = f"a{g}"

        def sems(n):
            return [ctx.sem((f"{n}_{name}_{k}")) for k in range(2)]

        def sb(n, shape):
            return [ctx.enter_context(nc.sbuf_tensor(f"{n}_{name}_{k}", shape, F32)) for k in range(2)]

        hn, hT, self_sum, xo, prod = (sb("hn", [P, BLK, C]), sb("hT", [C + 1, BLK * P]), sb("self_sum", [P, BLK, C]),
                                      sb("xo", [P, BLK, C]), sb("prod", [P, BLK, HC]))
        gT = sb("gT", [C + 1, BLK * P])
        hTp = ctx.enter_context(nc.psum_tensor(f"hTp_{name}", [C, BLK * P], F32))
        xl = [ctx.enter_context(nc.psum_tensor(f"xl_{name}_{t}", [P, HC], F32)) for t in range(BLK)]
        gTp = ctx.enter_context(nc.psum_tensor(f"gTp_{name}", [C, BLK * P], F32))
        fcp = ctx.enter_context(nc.psum_tensor(f"fcp_{name}", [P, BLK, C], F32))
        hn_in, xo_in, hTp_ready, hT_ready, xl_ready, weighted, step, g_ready, g_out = (
            sems(n) for n in ("hn_in", "xo_in", "hTp_ready", "hT_ready", "xl_ready", "weighted", "step", "g_ready", "g_out"))
        gTp_ready, gT_ready, fcp_ready, x_done = sems("gTp_ready"), sems("gT_ready"), sems("fcp_ready"), sems("x_done")
        s_ones = ctx.sem((f"s_ones_{name}"))
        wself = ctx.enter_context(nc.sbuf_tensor(f"wself_{name}", [P, TILES, H], F32))
        alone = ctx.enter_context(nc.sbuf_tensor(f"alone_{name}", [P, TILES], F32))

        with nc.Block() as block:
            @block.sync
            def _(sp):
                def store(j, k):
                    sp.wait_ge(g_ready[k], j + 1)
                    sp.dma_start(g_rows[ds(2 * j + k, 1)].rearrange("g p b c -> (g p) b c"), self_sum[k][:, :, :]).then_inc(g_out[k], 16)

                def body(j, first):
                    for k in range(2):
                        if not first:
                            sp.wait_ge(hTp_ready[k], j)
                        sp.dma_start(hn[k][:, :, :], rows_in[ds(2 * j + k, 1)].rearrange("g p b c -> (g p) b c")).then_inc(hn_in[k], 16)
                        if g == 1:
                            if not first:
                                sp.wait_ge(x_done[k], j)
                            sp.dma_start(xo[k][:, :, :], x_rows[ds(2 * j + k, 1)].rearrange("g p b c -> (g p) b c")).then_inc(xo_in[k], 16)
                        if g == 0 and not first:
                            store(j - 1, k)
                loop(sp, PAIRS, body)
                if g == 0:
                    for k in range(2):
                        store(PAIRS - 1, k)
                    for k in range(2):
                        sp.wait_ge(g_out[k], 16 * PAIRS)

            @block.tensor
            def _(pe):
                pe.wait_ge(s_ones, 1)

                def body(j, first):
                    for k in range(2):
                        pe.wait_ge(hn_in[k], 16 * (j + 1))
                        if not (first and k == 0):
                            pe.wait_ge(hT_ready[1 - k], j + k)
                        pe.sem_inc(S["pe_turn"])
                        for t in range(BLK):
                            tr = nc.tensor.transpose(hTp[:, t * P:(t + 1) * P], hn[k][:, t, :], ident[:, :])
                        tr.then_inc(hTp_ready[k], 1)
                        pe.wait_ge(hT_ready[k], j + 1)
                        if not (first and k == 0):
                            pe.wait_ge(weighted[1 - k], BLK * (j + k))
                        for t in range(BLK):
                            mm = nc.tensor.matmul(xl[t][:, :], hT[k][:, t * P:(t + 1) * P], S["wl"][g][:, :], start=True, stop=True)
                            mm.then_inc(xl_ready[k], 1)
                        if g == 1:
                            pe.wait_ge(g_ready[k], j + 1)
                            if not (first and k == 0):
                                pe.wait_ge(gT_ready[1 - k], j + k)
                            pe.sem_inc(S["pe_turn"])
                            for t in range(BLK):
                                tr = nc.tensor.transpose(gTp[:, t * P:(t + 1) * P], self_sum[k][:, t, :], ident[:, :])
                            tr.then_inc(gTp_ready[k], 1)
                            pe.wait_ge(gT_ready[k], j + 1)
                            if not (first and k == 0):
                                pe.wait_ge(x_done[1 - k], j + k)
                            for t in range(BLK):
                                mm = nc.tensor.matmul(fcp[:, t, :], gT[k][:, t * P:(t + 1) * P], S["wfc"][:, :], start=True, stop=True)
                            mm.then_inc(fcp_ready[k], 1)
                loop(pe, PAIRS, body)

            @block.scalar
            def _(act):
                def body(j, first):
                    for k in range(2):
                        act.wait_ge(hTp_ready[k], j + 1)
                        if not first:
                            act.wait_ge(xl_ready[k], BLK * j)
                        nc.scalar.copy(hT[k][0:C, :], hTp[:, :]).then_inc(hT_ready[k], 1)
                        if g == 1:
                            act.wait_ge(gTp_ready[k], j + 1)
                            if not first:
                                act.wait_ge(fcp_ready[k], j)
                            nc.scalar.copy(gT[k][0:C, :], gTp[:, :]).then_inc(gT_ready[k], 1)
                loop(act, PAIRS, body)

            @block.vector
            def _(dve):
                for k in range(2):
                    nc.vector.memset(hT[k][C:C + 1, :], 1.0)
                    ms = nc.vector.memset(gT[k][C:C + 1, :], 1.0)
                ms.then_inc(s_ones, 1)
                nc.vector.tensor_scalar(alone[:, :], deg_in[:, 0:TILES, 0], 0.0, 1.0 / H, ALU.is_equal, ALU.mult).then_inc(s_ones, 1)
                dve.wait_ge(s_ones, 2)
                nc.vector.tensor_tensor(wself[:, :, :], accw[:, 0:TILES, :], wide(alone[:, :], 2, H), ALU.add).then_inc(s_ones, 1)
                dve.wait_ge(s_ones, 3)

                def body(j, first):
                    for k in range(2):
                        tiles = (2 * j + k) * BLK
                        here = acc3[:, ds(tiles, BLK), :]
                        for t in range(BLK):
                            dve.wait_ge(xl_ready[k], BLK * j + t + 1)
                            nc.vector.tensor_tensor(prod[k][:, t, :].rearrange("p (h c) -> p h c", h=H), xl[t][:, :].rearrange("p (h c) -> p h c", h=H),
                                                    wide(wself[:, ds(tiles + t, 1), :].rearrange("p t h -> p (t h)"), 2, C),
                                                    ALU.mult).then_inc(weighted[k], 1)
                        dve.wait_ge(weighted[k], BLK * (j + 1))
                        if not first:
                            if g == 0:
                                dve.wait_ge(g_out[k], 16 * j)
                            else:
                                dve.wait_ge(gTp_ready[k], j)
                        for t in range(BLK):
                            red = nc.vector.tensor_reduce(self_sum[k][:, t, :], prod[k][:, t, :].rearrange("p (h c) -> p c h", h=H), AX.X, ALU.add)
                        red.then_inc(step[k], 1)
                        dve.wait_ge(step[k], 3 * j + 1)
                        nc.vector.tensor_tensor(self_sum[k][:, :, :], self_sum[k][:, :, :], here, ALU.add).then_inc(step[k], 1)
                        dve.wait_ge(step[k], 3 * j + 2)
                        nc.vector.tensor_tensor(self_sum[k][:, :, :], self_sum[k][:, :, :], wide(S["gbias"][g][:, :], 1, BLK),
                                                ALU.add).then_inc(step[k], 1)
                        dve.wait_ge(step[k], 3 * j + 3)
                        nc.vector.tensor_scalar(self_sum[k][:, :, :], self_sum[k][:, :, :], 0.0, None, ALU.max).then_inc(g_ready[k], 1)
                        if g == 1:
                            dve.wait_ge(fcp_ready[k], j + 1)
                            dve.wait_ge(xo_in[k], 16 * (j + 1))
                            nc.vector.tensor_tensor(here, fcp[:, :, :], xo[k][:, :, :], ALU.add).then_inc(x_done[k], 1)
                loop(dve, PAIRS, body)


def finish(nc, S, out):
    acc3, deg_in, ident, ones, x_d = S["acc3"], S["deg_in"], S["ident"], S["ones"], S["x_d"]
    x_rows = x_d.rearrange("(g b p) c -> g p b c", p=P, b=BLK)
    TRUE = FULL - FULL % BLK
    with Phase(nc) as ctx:
        name = "f"

        def sems(n):
            return [ctx.sem((f"{n}_{name}_{k}")) for k in range(2)]

        def sem(n):
            return ctx.sem((f"{n}_{name}"))

        def sb(n, shape):
            return [ctx.enter_context(nc.sbuf_tensor(f"{n}_{name}_{k}", shape, F32)) for k in range(2)]

        def one(n, shape):
            return ctx.enter_context(nc.sbuf_tensor(f"{n}_{name}", shape, F32))

        din = one("din", [P, TILES])
        aT = sb("aT", [C + 1, BLK * P])
        aTp = [ctx.enter_context(nc.psum_tensor(f"aTp_{k}", [C, BLK * P], F32)) for k in range(2)]
        hp = [ctx.enter_context(nc.psum_tensor(f"hp_{k}", [P, BLK, C], F32)) for k in range(2)]
        tot = ctx.enter_context(nc.psum_tensor("tot_f", [P, 2, C], F32))
        aTp_ready, aT_ready, hp_ready, hp_done, scaled = sems("aTp_ready"), sems("aT_ready"), sems("hp_ready"), sems("hp_done"), sems("scaled")
        s_ones, s_d, s_v, s_sum, s_tot, s_a = sem("s_ones"), sem("s_d"), sem("s_v"), sem("s_sum"), sem("s_tot"), sem("s_a")
        GB = 2 * BLK
        sums, mean, scale, shift = one("sums", [P, C]), one("mean", [P, C]), one("scale", [P, C]), one("shift", [P, C])
        psum28 = one("psum28", [P, PAIRS, C])
        fs, y, neg, sq = (sb(n, [P, BLK, C]) for n in ("fs", "y", "neg", "sq"))
        with nc.Block() as block:
            @block.vector
            def _(dve):
                for k in range(2):
                    nc.vector.memset(aT[k][C:C + 1, :], 1.0)
                nc.vector.tensor_scalar(din[:, :], deg_in[:, 0:TILES, 0], 1.0, None, ALU.max).then_inc(s_d, 1)
                dve.wait_ge(s_d, 2)
                nc.vector.reciprocal(din[:, :], din[:, :]).then_inc(s_d, 1)
                dve.wait_ge(s_d, 3)

                def body(j, first):
                    for k in range(2):
                        here = acc3[:, ds((2 * j + k) * BLK, BLK), :]
                        if not first:
                            dve.wait_ge(aTp_ready[k], j)
                        nc.vector.tensor_tensor(fs[k][:, :, :], here, wide(din[:, ds((2 * j + k) * BLK, BLK)], 2, C), ALU.mult).then_inc(scaled[k], 1)
                    for k in range(2):
                        here = acc3[:, ds((2 * j + k) * BLK, BLK), :]
                        dve.wait_ge(hp_ready[k], j + 1)
                        nc.vector.tensor_scalar(here, hp[k][:, :, :], 1.0, None, ALU.mult).then_inc(hp_done[k], 1)
                loop(dve, PAIRS, body)

            @block.scalar
            def _(act):
                act.wait_ge(s_d, 1)
                nc.scalar.activation(din[:, :], din[:, :], ACT.Sqrt).then_inc(s_d, 1)

                def body(j, first):
                    for k in range(2):
                        act.wait_ge(aTp_ready[k], j + 1)
                        if not first:
                            act.wait_ge(hp_ready[k], j)
                        nc.scalar.copy(aT[k][0:C, :], aTp[k][:, :]).then_inc(aT_ready[k], 1)
                loop(act, PAIRS, body)

            @block.tensor
            def _(pe):
                pe.wait_ge(s_d, 3)

                def body(j, first):
                    for k in range(2):
                        pe.wait_ge(scaled[k], j + 1)
                        if not first:
                            pe.wait_ge(aT_ready[k], j)
                        pe.sem_inc(S["pe_turn"])
                        for t in range(BLK):
                            tr = nc.tensor.transpose(aTp[k][:, t * P:(t + 1) * P], fs[k][:, t, :], ident[:, :])
                        tr.then_inc(aTp_ready[k], 1)
                        pe.wait_ge(aT_ready[k], j + 1)
                        if not first:
                            pe.wait_ge(hp_done[k], j)
                        for t in range(BLK):
                            mm = nc.tensor.matmul(hp[k][:, t, :], aT[k][:, t * P:(t + 1) * P], S["w3"][:, :], start=True, stop=True)
                        mm.then_inc(hp_ready[k], 1)
                loop(pe, PAIRS, body)

        out_full = out[0:FULL * P, :].rearrange("(b p) c -> p b c", p=P)
        LB = 2 * PAIRS - 1
        with nc.Block() as block:
            y_in, y_done, e1, e2, e3, out_sem, o_in = (sems(n) for n in ("y_in", "y_done", "e1", "e2", "e3", "out_sem", "o_in"))
            s_sq = sem("s_sq")

            @block.vector
            def _(dve):
                chain = Chain(dve, s_v)

                chain(nc.vector.tensor_reduce(sums[:, :], acc3[:, 0:FULL, :].rearrange("p b c -> p c b"), AX.X, ALU.add))
                chain(nc.vector.tensor_tensor(sums[0:REST, :], sums[0:REST, :], acc3[0:REST, FULL, :], ALU.add))
                dve.sem_inc(s_sum, 1)
                dve.wait_ge(s_tot, 1)
                chain(nc.vector.tensor_scalar(mean[:, :], tot[:, 0, :], 1.0 / N, None, ALU.mult))
                chain(nc.vector.tensor_tensor(acc3[:, 0:TILES, :], acc3[:, 0:TILES, :], wide(mean[:, :], 1, TILES), ALU.subtract))

                def body(j, first):
                    for k in range(2):
                        here = acc3[:, ds((2 * j + k) * BLK, BLK), :]
                        if not first:
                            dve.wait_ge(y_done[k], j)
                        nc.vector.tensor_tensor(sq[k][:, :, :], here, here, ALU.mult).then_inc(y_in[k], 1)
                        dve.wait_ge(y_in[k], j + 1)
                        nc.vector.tensor_reduce(psum28[:, ds(j, 1), :].rearrange("p j c -> p (j c)") if k == 0 else y[0][:, 0, :],
                                                sq[k][:, :, :].rearrange("p b c -> p c b"), AX.X, ALU.add).then_inc(y_done[k], 1)
                        if k == 1:
                            dve.wait_ge(y_done[1], j + 1)
                            v = psum28[:, ds(j, 1), :].rearrange("p j c -> p (j c)")
                            nc.vector.tensor_tensor(v, v, y[0][:, 0, :], ALU.add).then_inc(s_sq, 1)
                            dve.wait_ge(s_sq, j + 1)
                chain(nc.vector.memset(acc3[:, FULL + 1:TILES, :], 0.0))
                chain(nc.vector.tensor_copy(y[1][0:REST, 0, :], acc3[0:REST, FULL, :]))
                chain(nc.vector.memset(acc3[:, FULL, :], 0.0))
                chain(nc.vector.tensor_copy(acc3[0:REST, FULL, :], y[1][0:REST, 0, :]))
                loop(dve, PAIRS, body)
                chain(nc.vector.tensor_reduce(sums[:, :], psum28[:, :, :].rearrange("p j c -> p c j"), AX.X, ALU.add))
                dve.sem_inc(s_sum, 1)
                dve.wait_ge(s_a, 1)
                chain(nc.vector.reciprocal(scale[:, :], shift[:, :]))
                chain(nc.vector.tensor_tensor(scale[:, :], scale[:, :], S["gamma"][:, :], ALU.mult))

                def tail(j, first):
                    for k in range(2):
                        here = acc3[:, ds((2 * j + k) * BLK, BLK), :]
                        nc.vector.tensor_tensor(here, here, wide(scale[:, :], 1, BLK), ALU.mult).then_inc(e1[k], 1)
                    for k in range(2):
                        here = acc3[:, ds((2 * j + k) * BLK, BLK), :]
                        dve.wait_ge(e1[k], 3 * j + 1)
                        if not first:
                            dve.wait_ge(e3[k], 2 * j)
                        nc.vector.tensor_tensor(y[k][:, :, :], here, wide(S["beta"][:, :], 1, BLK), ALU.add).then_inc(e1[k], 1)
                    for k in range(2):
                        dve.wait_ge(e1[k], 3 * j + 2)
                        if not first:
                            dve.wait_ge(e2[k], j)
                        nc.vector.tensor_scalar(neg[k][:, :, :], y[k][:, :, :], 0.0, None, ALU.min).then_inc(e1[k], 1)
                    for k in range(2):
                        dve.wait_ge(o_in[k], 16 * (j + 1))
                        nc.vector.scalar_tensor_tensor(out=y[k][:, :, :], in0=y[k][:, :, :], scalar=0.0, in1=fs[k][:, :, :],
                                                       op0=ALU.max, op1=ALU.add).then_inc(e3[k], 1)
                    for k in range(2):
                        here = acc3[:, ds((2 * j + k) * BLK, BLK), :]
                        dve.wait_ge(e2[k], j + 1)
                        dve.wait_ge(e3[k], 2 * j + 1)
                        nc.vector.scalar_tensor_tensor(out=here, in0=sq[k][:, :, :], scalar=-1.0, in1=y[k][:, :, :],
                                                       op0=ALU.add, op1=ALU.add).then_inc(e3[k], 1)
                loop(dve, PAIRS, tail)

            @block.scalar
            def _(act):
                act.wait_ge(s_tot, 2)
                nc.scalar.activation(shift[:, :], tot[:, 1, :], ACT.Sqrt, bias=S["eps"][:, 0:1], scale=1.0 / N).then_inc(s_a, 1)

                def body(j, first):
                    for k in range(2):
                        act.wait_ge(e1[k], 3 * j + 3)
                        if not first:
                            act.wait_ge(e3[k], 2 * j)
                        nc.scalar.activation(sq[k][:, :, :], neg[k][:, :, :], ACT.Exp).then_inc(e2[k], 1)
                loop(act, PAIRS, body)

            @block.tensor
            def _(pe):
                for n in range(2):
                    pe.wait_ge(s_sum, n + 1)
                    nc.tensor.matmul(tot[:, n, :], ones[:, :], sums[:, :], start=True, stop=True).then_inc(s_tot, 1)

            @block.sync
            def _(sp):
                def body(j, first):
                    for k in range(2):
                        blk = 2 * j + k
                        if not first:
                            sp.wait_ge(e3[k], 2 * j)
                        sp.dma_start(fs[k][:, :, :], x_rows[ds(blk, 1)].rearrange("g p b c -> (g p) b c")).then_inc(o_in[k], 16)
                        if not first:
                            sp.dma_start(out[ds((blk - 2) * BLK * P, BLK * P), :].rearrange("(b p) c -> p b c", p=P),
                                         acc3[:, ds((blk - 2) * BLK, BLK), :]).then_inc(out_sem[k], 16)
                loop(sp, PAIRS, body)
                sp.wait_ge(e3[0], 2 * PAIRS)
                sp.dma_start(out[(LB - 1) * BLK * P:LB * BLK * P, :].rearrange("(b p) c -> p b c", p=P), acc3[:, (LB - 1) * BLK:LB * BLK, :]).then_inc(out_sem[0], 16)
                sp.wait_ge(e3[1], 2 * PAIRS)
                sp.dma_start(out[LB * BLK * P:FULL * P, :].rearrange("(b p) c -> p b c", p=P), acc3[:, LB * BLK:FULL, :]).then_inc(out_sem[1], 16)
                sp.dma_start(out[FULL * P:N, :], acc3[0:REST, FULL, :]).then_inc(out_sem[1], 16)
                sp.wait_ge(out_sem[0], 16 * PAIRS)
                sp.wait_ge(out_sem[1], 16 * (PAIRS + 1))


_INS = ['x', 'src', 'dst', 'edge_attr_64', 'edge_weight', 'edge_weight1',
        'L0_gnn_W_f', 'L0_gnn_b_f', 'L0_gnn_W_s', 'L0_gnn_b_s', 'L1_gnn_W1', 'L1_gnn_b1', 'L1_gnn_W2', 'L1_gnn_b2',
        'L2_gnn_W1l', 'L2_gnn_b1l', 'L2_gnn_W1r', 'L2_gnn_b1r', 'L2_gnn_att1', 'L2_gnn_bias1',
        'L2_gnn_W2l', 'L2_gnn_b2l', 'L2_gnn_W2r', 'L2_gnn_b2r', 'L2_gnn_att2', 'L2_gnn_bias2',
        'L2_gnn_Wfc', 'L2_gnn_bfc', 'L3_gnn_W', 'L3_gnn_b', 'L3_gnn_gamma', 'L3_gnn_beta']


def kernel(**inputs):
    import numpy as _np
    import concourse.bacc as _bacc
    from concourse import mybir as _mybir
    from concourse.bass_utils import run_bass_kernel_spmd as _run

    nc = _bacc.Bacc("TRN2", target_bir_lowering=False, num_devices=1)
    arrays, io = {}, {}
    for name in _INS:
        a = _np.ascontiguousarray(inputs[name])
        arrays[f"in_{name}_dram"] = a
        io[name] = nc.dram_tensor(f"in_{name}_dram", a.shape, _mybir.dt.from_np(a.dtype), kind="ExternalInput").ap()
    out = nc.dram_tensor("out_0_dram", (N, C), _mybir.dt.float32, kind="ExternalOutput").ap()
    build(nc, io, out)
    r = _run(nc, [arrays], core_ids=[0])
    return r.results[0]["out_0_dram"]
```
